# Optimizing a Trainium2 kernel written in Bass

```python
import numpy as np
import jax
import jax.numpy as jnp

def _softmax(x, axis=-1):
    return jax.nn.softmax(x, axis=axis)

def _gelu(x):
    return jax.nn.gelu(x, approximate=True)

def _silu(x):
    return jax.nn.silu(x)

def _sigmoid(x):
    return jax.nn.sigmoid(x)

def _layernorm(x, axis=-1, eps=1e-05):
    m = jnp.mean(x, axis=axis, keepdims=True)
    v = jnp.var(x, axis=axis, keepdims=True)
    return (x - m) / jnp.sqrt(v + eps)

def _scatter_add(tgt, idx, src, axis=0):
    return tgt.at[idx].add(src)

def _segment_sum(src, seg, n):
    return jax.ops.segment_sum(src, seg, n)
kernel_name = 'mk_gnn_preln_d2_gnn_r64_84ae25'

def setup_inputs(seed: int=0):
    np.random.seed(seed)
    _w = jnp.asarray

    def _rec_inputs():
        import jax
        import jax.numpy as jnp
        _gk = jax.random.key(seed)
        x = -0.000202 + 1 * jax.random.normal(jax.random.fold_in(_gk, 1), (50000, 128), jnp.float32)
        src = jax.random.randint(jax.random.fold_in(_gk, 2), (12500,), 0, 50000, jnp.int32)
        dst = jax.random.randint(jax.random.fold_in(_gk, 3), (12500,), 0, 50000, jnp.int32)
        _o = jnp.argsort(dst, stable=True)
        src = src[_o]
        dst = dst[_o]
        edge_type_16 = jax.random.randint(jax.random.fold_in(_gk, 12), (12500,), 0, 16, jnp.int32)
        edge_type_5 = jax.random.randint(jax.random.fold_in(_gk, 13), (12500,), 0, 5, jnp.int32)
        return (x, src, dst, edge_type_16, edge_type_5)
    x, src, dst, edge_type_16, edge_type_5 = _rec_inputs()

    def _L0_gnn_setup():
        import jax, jax.numpy as jnp
        import numpy as np
        N = 50000
        E = 10000
        IN = 128
        OUT = 128
        H = 4
        DH = OUT // H
        R = 5
        key = jax.random.key(seed)
        k0, k1, k2, k3 = jax.random.split(key, 4)
        x = jax.random.normal(k0, (N, IN), dtype=jnp.float32)
        Ws = jax.random.normal(k1, (R, IN, H * DH), dtype=jnp.float32) * (1.0 / np.sqrt(IN))
        bs = jnp.zeros((R, H * DH), dtype=jnp.float32)
        edge_index = jax.random.randint(k2, (2, E), 0, N)
        edge_types = jax.random.randint(k3, (E,), 0, R)
        return {'x': x, 'Ws': Ws, 'bs': bs, 'edge_index': edge_index, 'edge_types': edge_types}
    _L0_gnn_all = _L0_gnn_setup()
    _L0_gnn_in = {k: v for k, v in _L0_gnn_all.items() if k in ('Ws', 'bs')}
    del _L0_gnn_all

    def _L1_gnn_setup():
        import jax, jax.numpy as jnp
        import numpy as np
        N = 50000
        R = 16
        B = 8
        D = 128
        E = 12500
        EPS = 1e-05
        SLOPE = 0.1

        def _layernorm(x, g, b):
            mu = jnp.mean(x, axis=-1, keepdims=True)
            var = jnp.mean(jnp.square(x - mu), axis=-1, keepdims=True)
            return (x - mu) * jax.lax.rsqrt(var + EPS) * g + b

        def _rgcn_layer(x, src, dst, et, weight, comp, root, bias):
            W = jnp.einsum('rb,bio->rio', comp, weight)
            xW = jnp.einsum('ni,rio->nro', x, W)
            m = xW[src, et]
            seg = et * N + dst
            cnt = jax.ops.segment_sum(jnp.ones((src.shape[0],), x.dtype), seg, num_segments=R * N)
            norm = 1.0 / jnp.maximum(cnt, 1.0)
            m = m * norm[seg][:, None]
            agg = jax.ops.segment_sum(m, dst, num_segments=N)
            return agg + x @ root + bias
        key = jax.random.key(seed)
        ks = jax.random.split(key, 12)
        gain = np.sqrt(2.0 / (1.0 + SLOPE ** 2))

        def xavier(k, shape):
            fan_in, fan_out = (shape[-2], shape[-1])
            bound = gain * np.sqrt(6.0 / (fan_in + fan_out))
            return jax.random.uniform(k, shape, jnp.float32, -bound, bound)
        entity = jax.random.normal(ks[0], (N, D), jnp.float32)
        edge_index = jax.random.randint(ks[1], (2, E), 0, N, jnp.int64)
        edge_types = jax.random.randint(ks[2], (E,), 0, R, jnp.int64)
        return {'entity': entity, 'train_pos_edge_index': edge_index, 'train_pos_edge_types': edge_types, 'weight1': xavier(ks[3], (B, D, D)), 'comp1': jax.random.normal(ks[4], (R, B), jnp.float32) / np.sqrt(B), 'root1': xavier(ks[5], (D, D)), 'bias1': jnp.zeros((D,), jnp.float32), 'ln1_g': jnp.ones((D,), jnp.float32), 'ln1_b': jnp.zeros((D,), jnp.float32), 'weight2': xavier(ks[6], (B, D, D)), 'comp2': jax.random.normal(ks[7], (R, B), jnp.float32) / np.sqrt(B), 'root2': xavier(ks[8], (D, D)), 'bias2': jnp.zeros((D,), jnp.float32), 'ln2_g': jnp.ones((D,), jnp.float32), 'ln2_b': jnp.zeros((D,), jnp.float32)}
    _L1_gnn_all = _L1_gnn_setup()
    _L1_gnn_in = {k: v for k, v in _L1_gnn_all.items() if k in ('weight1', 'comp1', 'root1', 'bias1', 'ln1_g', 'ln1_b', 'weight2', 'comp2', 'root2', 'bias2', 'ln2_g', 'ln2_b')}
    del _L1_gnn_all
    return {'x': x, 'src': src, 'dst': dst, 'edge_type_16': edge_type_16, 'edge_type_5': edge_type_5, 'L0_gnn_Ws': _L0_gnn_in['Ws'], 'L0_gnn_bs': _L0_gnn_in['bs'], 'L1_gnn_weight1': _L1_gnn_in['weight1'], 'L1_gnn_comp1': _L1_gnn_in['comp1'], 'L1_gnn_root1': _L1_gnn_in['root1'], 'L1_gnn_bias1': _L1_gnn_in['bias1'], 'L1_gnn_ln1_g': _L1_gnn_in['ln1_g'], 'L1_gnn_ln1_b': _L1_gnn_in['ln1_b'], 'L1_gnn_weight2': _L1_gnn_in['weight2'], 'L1_gnn_comp2': _L1_gnn_in['comp2'], 'L1_gnn_root2': _L1_gnn_in['root2'], 'L1_gnn_bias2': _L1_gnn_in['bias2'], 'L1_gnn_ln2_g': _L1_gnn_in['ln2_g'], 'L1_gnn_ln2_b': _L1_gnn_in['ln2_b']}

def reference(x, src, dst, edge_type_16, edge_type_5, L0_gnn_Ws, L0_gnn_bs, L1_gnn_weight1, L1_gnn_comp1, L1_gnn_root1, L1_gnn_bias1, L1_gnn_ln1_g, L1_gnn_ln1_b, L1_gnn_weight2, L1_gnn_comp2, L1_gnn_root2, L1_gnn_bias2, L1_gnn_ln2_g, L1_gnn_ln2_b):
    import jax
    import jax.numpy as jnp

    def _L0_gnn_ref(x, Ws, bs, edge_index, edge_types):
        import jax, jax.numpy as jnp
        import numpy as np
        N = 50000
        E = 10000
        IN = 128
        OUT = 128
        H = 4
        DH = OUT // H
        R = 5
        'Per-relation linear -> gather(src) -> scatter-add(dst) -> mean, then concat.\n\n            Faithful to GraphAttentionLayer.forward with concat=True (att params are\n            unused in the original forward; dropout is identity at inference).\n            '
        src, dst = (edge_index[0], edge_index[1])
        outs = []
        for r in range(R):
            mask = edge_types == r
            mf = mask.astype(x.dtype)
            x_r = (x @ Ws[r] + bs[r]).reshape(N, H, DH)
            msgs = x_r[src] * mf[:, None, None]
            agg = jax.ops.segment_sum(msgs, dst, num_segments=N)
            deg = jnp.clip(jax.ops.segment_sum(mf, dst, num_segments=N), 1.0)
            outs.append(agg / deg[:, None, None])
        out = jnp.concatenate(outs, axis=-1)
        out = out.reshape(N, -1)[:, :OUT]
        return out

    def _L1_gnn_ref(entity, train_pos_edge_index, train_pos_edge_types, weight1, comp1, root1, bias1, ln1_g, ln1_b, weight2, comp2, root2, bias2, ln2_g, ln2_b):
        import jax, jax.numpy as jnp
        import numpy as np
        N = 50000
        R = 16
        B = 8
        D = 128
        E = 12500
        EPS = 1e-05
        SLOPE = 0.1

        def _layernorm(x, g, b):
            mu = jnp.mean(x, axis=-1, keepdims=True)
            var = jnp.mean(jnp.square(x - mu), axis=-1, keepdims=True)
            return (x - mu) * jax.lax.rsqrt(var + EPS) * g + b

        def _rgcn_layer(x, src, dst, et, weight, comp, root, bias):
            W = jnp.einsum('rb,bio->rio', comp, weight)
            xW = jnp.einsum('ni,rio->nro', x, W)
            m = xW[src, et]
            seg = et * N + dst
            cnt = jax.ops.segment_sum(jnp.ones((src.shape[0],), x.dtype), seg, num_segments=R * N)
            norm = 1.0 / jnp.maximum(cnt, 1.0)
            m = m * norm[seg][:, None]
            agg = jax.ops.segment_sum(m, dst, num_segments=N)
            return agg + x @ root + bias
        src, dst = (train_pos_edge_index[0], train_pos_edge_index[1])
        et = train_pos_edge_types
        x = _rgcn_layer(entity, src, dst, et, weight1, comp1, root1, bias1)
        x = _layernorm(x, ln1_g, ln1_b)
        x = jnp.where(x >= 0, x, SLOPE * x)
        x = _rgcn_layer(x, src, dst, et, weight2, comp2, root2, bias2)
        x = _layernorm(x, ln2_g, ln2_b)
        x = jnp.where(x >= 0, x, SLOPE * x)
        return x
    edge_index = jnp.stack([src, dst])
    h = jnp.maximum(_layernorm(x, axis=-1), 0.0)
    x = x + _L0_gnn_ref(h, L0_gnn_Ws, L0_gnn_bs, edge_index, edge_type_5)
    h = jnp.maximum(_layernorm(x, axis=-1), 0.0)
    x = x + _L1_gnn_ref(h, edge_index, edge_type_16, L1_gnn_weight1, L1_gnn_comp1, L1_gnn_root1, L1_gnn_bias1, L1_gnn_ln1_g, L1_gnn_ln1_b, L1_gnn_weight2, L1_gnn_comp2, L1_gnn_root2, L1_gnn_bias2, L1_gnn_ln2_g, L1_gnn_ln2_b)
    return x

_drawn_inputs = setup_inputs


def setup_inputs(seed=0):
    import zlib

    import numpy as np

    out = dict(_drawn_inputs(seed))
    spreads = {'L0_gnn_bs': (0.0, 0.432),
     'L1_gnn_bias1': (0.0, 0.1),
     'L1_gnn_ln1_g': (1.0, 0.2),
     'L1_gnn_ln1_b': (0.0, 0.1),
     'L1_gnn_bias2': (0.0, 0.1),
     'L1_gnn_ln2_g': (1.0, 0.2),
     'L1_gnn_ln2_b': (0.0, 0.1)}
    factors = {}
    for name, (base, spread) in spreads.items():
        noise = np.random.default_rng([zlib.crc32(name.encode()), seed]).standard_normal(out[name].shape)
        drawn = base * np.exp(spread * noise) if base else spread * noise
        out[name] = jnp.asarray(drawn.astype(out[name].dtype))
    for name, factor in factors.items():
        out[name] = (out[name] * factor).astype(out[name].dtype)
    return out
```

```python
from contextlib import ExitStack

import concourse.bass as bass
from concourse import mybir

ALU = mybir.AluOpType
ACT = mybir.ActivationFunctionType
AX = mybir.AxisListType
F32 = mybir.dt.float32
BF16 = mybir.dt.bfloat16
I32 = mybir.dt.int32

N = 50000
E = 12500
D = 128
R1 = 16
B1 = 8
HEAD = 32
P = 125
TG = 4
NT = E // P
NG = NT // TG
GE = TG * P
DA = 3
LOB = 256
HIC = 98
CT = 10
CE = CT * P
NCH = NT // CT
EPS = 1e-5
SLOPE = 0.1
SRC_, DST_, OUT_ = 0, 1, 2


def gnn_kernel(nc, x, src, dst_ext, dst_both, et_both, et5, w0, b0, v1, comp1, root1, bias1, g1, be1,
               v2, comp2, root2, bias2, g2, be2, out):
    ctx = ExitStack()
    with ctx:
        def sb(name, shape, dt=F32):
            return ctx.enter_context(nc.sbuf_tensor(name, shape, dt))

        def sem(name):
            return ctx.enter_context(nc.semaphore(name))

        def dram(name, shape, dt=F32):
            return nc.dram_tensor(name, shape, dt).ap()

        tab1 = dram("tab1", [2 * E, D])
        tab2 = dram("tab2", [2 * E, D])
        x1_dram = dram("x1_dram", [E, D])
        own1_dram = dram("own1_dram", [D, E])
        own2_dram = dram("own2_dram", [D, E])

        ident = sb("ident", [128, 128])
        identb = sb("identb", [128, 128], BF16)
        anti = sb("anti", [128, 128])
        sel = sb("sel", [48, R1, 128], BF16)
        ones = sb("ones", [128, 128])
        onesb = sb("onesb", [128, 128], BF16)
        zerob = sb("zerob", [128, LOB], BF16)
        iota_lo = sb("iota_lo", [P, LOB])
        relno = sb("relno", [64, 1])
        rowno = sb("rowno", [P, 1])
        tileno = sb("tileno", [P, NT])
        slotno = sb("slotno", [P, NT])
        blockno = sb("blockno", [128, 1])
        epst = sb("epst", [128, 1])

        wt = sb("wt", [128, 2, 9, 128])
        wsum = sb("wsum", [128, 18])
        w0t = sb("w0t", [128, 4 * HEAD])
        b0t = sb("b0t", [128, 1])
        ln = sb("ln", [128, 4])
        brow = sb("brow", [96, 2, 128])
        bsum = sb("bsum", [96, 2])
        bpart = sb("bpart", [96, 2, 128], BF16)
        bias = sb("bias", [96, 2, TG, 128], BF16)
        compt = sb("compt", [32, 2 * B1])

        raw = sb("raw", [NT, 3, P], I32)
        rawf = sb("rawf", [NT, 3, P])
        part = sb("part", [NT, 4, P], I32)
        turn = sb("turn", [NT, 7, P])
        lastf = sb("lastf", [NT, P])
        gidx = sb("gidx", [P, NG, 2 * TG], I32)
        sidx = sb("sidx", [P, NG, TG], I32)
        tidx = sb("tidx", [P, NG, TG], I32)
        meta = sb("meta", [P, NG, 6 * TG])
        metat = sb("metat", [P, 6 * TG])
        found = sb("found", [P, NT])
        foundi = sb("foundi", [P, NT], I32)
        hit = sb("hit", [P, NT])
        slotf = sb("slotf", [P, NT])
        res = sb("res", [P, TG])
        hot_hi = sb("hot_hi", [P, TG, 2 * HIC], BF16)
        hot_lo = sb("hot_lo", [P, 2, TG, LOB], BF16)
        hot_hit = sb("hot_hit", [HIC, TG * 2, 128], BF16)
        node_tab = sb("node_tab", [HIC, 2, 2, LOB], BF16)
        junk_d = sb("junk_d", [P, DA * TG, D], BF16)
        junk_e = sb("junk_e", [P, TG, D], BF16)

        dstc = sb("dstc", [64, CE + 1], I32)
        etc = sb("etc", [64, CE], I32)
        hotc = sb("hotc", [64, CE])
        carryc = sb("carryc", [64, 1])
        cnt_f = sb("cnt_f", [P, NT])
        cnt_b = sb("cnt_b", [P, NT])
        coef = sb("coef", [P, NT, R1])
        coef3 = sb("coef3", [P, NT, 48], BF16)
        coef3g = sb("coef3g", [P, TG, 48], BF16)
        coeft = sb("coeft", [48, E], BF16)
        cont = sb("cont", [128, E], BF16)

        xd = sb("xd", [P, 2, DA * TG, D])
        nd = sb("nd", [P, DA * TG, D])
        fd = sb("fd", [128, DA, GE])
        zd = sb("zd", [128, DA, GE])
        st_d = sb("st_d", [P, DA * TG, 6])
        mv_d = sb("mv_d", [P, 3, DA * TG])
        sd_d = sb("sd_d", [P, DA * TG])
        rs_d = sb("rs_d", [P, DA * TG])
        ss_d = sb("ss_d", [P, DA * TG])

        gat = sb("gat", [P, 2, 2 * TG, D])
        nowidx = sb("nowidx", [P, 2, 2 * TG], I32)
        nowout = sb("nowout", [P, TG], I32)
        dstb = sb("dstb", [128, 2, GE + 1], I32)
        et5b = sb("et5b", [128, 2, GE], I32)
        ne = sb("ne", [P, TG, D])
        fe = sb("fe", [128, GE])
        ye = sb("ye", [P, TG, D])
        mask = sb("mask", [128, GE])
        deg = sb("deg", [128, GE])
        msg = sb("msg", [128, GE])
        agg = sb("agg", [128, GE])
        mean = sb("mean", [128, GE])
        carry = sb("carry", [128, 2])
        x1e = sb("x1e", [P, TG, D])
        ne2 = sb("ne2", [P, TG, D])
        own = sb("own", [128, 2, GE])
        fo = sb("fo", [128, GE])
        scaled = sb("scaled", [128, 2, GE])
        st_e = sb("st_e", [P, TG, 6])
        mv_e = sb("mv_e", [P, 3, TG])
        sd_e = sb("sd_e", [P, TG])
        rs_e = sb("rs_e", [P, TG])
        ss_e = sb("ss_e", [P, TG])

        dT = ctx.enter_context(nc.psum_tensor("dT", [128, DA, 512], F32))
        dY = ctx.enter_context(nc.psum_tensor("dY", [128, DA, 512], F32))
        eT = ctx.enter_context(nc.psum_tensor("eT", [128, 512], F32))
        eY = ctx.enter_context(nc.psum_tensor("eY", [128, 512], F32))
        bQ = [dT[:, 1, :], dT[:, 2, :]]
        bM = dY[:, 1, :]
        bZ = dY[:, 2, :]

        ld_idx, ld_w, ld_cnt = sem("ld_idx"), sem("ld_w"), sem("ld_cnt")
        pool_const, dve_const = sem("pool_const"), sem("dve_const")
        prep = sem("prep")
        w_ready = sem("w_ready")
        idx_split, idx_turned, idx_ready = sem("idx_split"), sem("idx_turned"), sem("idx_ready")
        cnt_prods, cnt_summed, cnt_saved = sem("cnt_prods"), sem("cnt_summed"), sem("cnt_saved")
        cnt_flipped = sem("cnt_flipped")
        coef_now, coef_turned, coef_ready = sem("coef_now"), sem("coef_turned"), sem("coef_ready")
        tab_hot, tab_added, tab_sum, tab_ready = sem("tab_hot"), sem("tab_added"), sem("tab_sum"), sem("tab_ready")
        hot_ready, hot_turned, hot_saved, looked, looked_used = (
            sem("hot_ready"), sem("hot_turned"), sem("hot_saved"), sem("looked"), sem("looked_used"))
        slots_ready = sem("slots_ready")

        d_x = [sem("d_x0"), sem("d_x1")]
        d_stats, d_var, d_sd, d_rs, d_norm = (sem("d_stats"), sem("d_var"), sem("d_sd"), sem("d_rs"), sem("d_norm"))
        d_hT, d_h, d_y, d_ys = sem("d_hT"), sem("d_h"), sem("d_y"), sem("d_ys")
        d_sq, d_sd1, d_rs1, d_yn = sem("d_sq"), sem("d_sd1"), sem("d_rs1"), sem("d_yn")
        d_ynT, d_t, d_z = sem("d_ynT"), sem("d_t"), sem("d_z")
        d_y2, d_ys2, d_sq2, d_sd2, d_rs2, d_yn2 = (
            sem("d_y2"), sem("d_ys2"), sem("d_sq2"), sem("d_sd2"), sem("d_rs2"), sem("d_yn2"))
        d_yn2T, d_t2, d_z2, d_back, d_out = sem("d_yn2T"), sem("d_t2"), sem("d_z2"), sem("d_back"), sem("d_out")
        d_st = [sem("d_st0"), sem("d_st1")]

        now_ready = sem("now_ready")
        g_s = [sem("g_s0"), sem("g_s1")]
        g_d = [sem("g_d0"), sem("g_d1")]
        ld_e = [sem("ld_e0"), sem("ld_e1")]
        s_stats, s_var, s_sd, s_rs = sem("s_stats"), sem("s_var"), sem("s_sd"), sem("s_rs")
        s_norm = [sem("s_norm0"), sem("s_norm1")]
        t_x1 = [sem("t_x10"), sem("t_x11")]
        m_gT = [sem("m_gT0"), sem("m_gT1")]
        s_hT, s_h, s_m0, s_y, s_ys = sem("s_hT"), sem("s_h"), sem("s_m0"), sem("s_y"), sem("s_ys")
        s_sq, s_sd1, s_rs1, s_yn = sem("s_sq"), sem("s_sd1"), sem("s_rs1"), sem("s_yn")
        cont_ready, deg_ready, msg_ready, agg_ready, mean_ready, mean_T = (
            sem("cont_ready"), sem("deg_ready"), sem("msg_ready"), sem("agg_ready"), sem("mean_ready"), sem("mean_T"))
        carried = sem("carried")
        t_stats, t_var, t_sd, t_rs, t_norm, t_hT, t_h = (
            sem("t_stats"), sem("t_var"), sem("t_sd"), sem("t_rs"), sem("t_norm"), sem("t_hT"), sem("t_h"))
        st_ns, st_nt, st_x1, st_h, st_zs = sem("st_ns"), sem("st_nt"), sem("st_x1"), sem("st_h"), sem("st_zs")

        m_t, m_g = sem("m_t"), sem("m_g")
        m_bc, m_sc, m_mm = sem("m_bc"), sem("m_sc"), sem("m_mm")
        m_agg, m_y, m_ys, m_sq, m_sd, m_rs, m_yn = (
            sem("m_agg"), sem("m_y"), sem("m_ys"), sem("m_sq"), sem("m_sd"), sem("m_rs"), sem("m_yn"))
        m_ynT, m_tt, m_z, m_back, m_out = sem("m_ynT"), sem("m_tt"), sem("m_z"), sem("m_back"), sem("m_out")
        out_now = sem("out_now")
        st_zn, st_z, st_out = sem("st_zn"), sem("st_z"), sem("st_out")

        block = ctx.enter_context(nc.Block())

        def in_pairs(eng, body):
            with eng.Fori(0, NG // 2) as k:
                body(k * 2, k, 0)
                body(k * 2 + 1, k, 1)
            body(NG - 1, NG // 2, 0)

        def counted(eng, reg):
            eng.reg_add(reg, reg, 1)
            return eng.snap(reg)

        def grp(ap, i, n):
            return ap[:, bass.ds(i * n, n)]

        def rows_of(t, r0, i):
            return t[bass.ds(i * GE + r0, GE), :].rearrange("(t p) f -> p t f", p=P)

        A_ROWS = DA * GE

        def dense_rows(t, i, nt, base):
            return t[bass.ds(i * (nt * P) + base, nt * P), :].rearrange("(p t) f -> p t f", p=P)

        PASS_A = (DA * TG, 0, 0)
        PASS_B = (TG, NG * A_ROWS, NG)

        def slot_base(q):
            return (NG + 1) // 2 if q == 0 else NG // 2

        @block.sync
        def _(sp):
            sp.dma_start(raw[:, SRC_, :], src.rearrange("(t p) -> t p", p=P)).then_inc(ld_idx, 16)
            sp.dma_start(raw[:, DST_, :], dst_ext[1:1 + E].rearrange("(t p) -> t p", p=P)).then_inc(ld_idx, 16)
            sp.dma_start(raw[:, OUT_, :], dst_ext[2:2 + E].rearrange("(t p) -> t p", p=P)).then_inc(ld_idx, 16)
            for l, (root, v) in enumerate(((root1, v1), (root2, v2))):
                sp.dma_start(wt[:, l, 0, :], root).then_inc(ld_w, 16)
                sp.dma_start(wt[:, l, 1:9, :], v.rearrange("b i o -> i b o")).then_inc(ld_w, 16)
            for l, (b, g, be, comp) in enumerate(((bias1, g1, be1, comp1), (bias2, g2, be2, comp2))):
                sp.dma_start(brow[:, l, :], b.partition_broadcast(96)).then_inc(ld_w, 16)
                sp.dma_start(ln[:, 2 * l:2 * l + 1], g.unsqueeze(1)).then_inc(ld_w, 16)
                sp.dma_start(ln[:, 2 * l + 1:2 * l + 2], be.unsqueeze(1)).then_inc(ld_w, 16)
                sp.wait_ge(dve_const, 1)
                sp.dma_start(compt[0:R1, l * B1:(l + 1) * B1], comp).then_inc(ld_w, 16)
            sp.dma_start(w0t[:, :].rearrange("i (r o) -> i r o", r=4),
                         w0[0:4, :, 0:HEAD].rearrange("r i o -> i r o")).then_inc(ld_w, 16)
            for r in range(4):
                sp.dma_start(b0t[r * HEAD:(r + 1) * HEAD, :], b0[r, 0:HEAD].unsqueeze(1)).then_inc(ld_w, 16)

            with sp.Fori(0, NCH) as c:
                sp.wait_ge(cnt_prods, c)
                for h in range(2):
                    sp.dma_start(dstc[32 * h:32 * h + 32, :],
                                 dst_both[h, bass.ds(c * CE, CE + 1)].partition_broadcast(32)).then_inc(ld_cnt, 16)
                    sp.dma_start(etc[32 * h:32 * h + 32, :],
                                 et_both[h, bass.ds(c * CE, CE)].partition_broadcast(32)).then_inc(ld_cnt, 16)

            def load_dense(i, q, nt, base):
                sp.dma_start(xd[:, q, 0:nt, :], dense_rows(x, i, nt, base)).then_inc(d_x[q], 16)

            def load_edges(i, q):
                sp.dma_start(dstb[:, q, :], dst_ext[bass.ds(i * GE, GE + 1)].partition_broadcast(128)).then_inc(ld_e[q], 16)
                sp.dma_start(et5b[:, q, :], et5[bass.ds(i * GE, GE)].partition_broadcast(128)).then_inc(ld_e[q], 16)

            load_dense(0, 0, DA * TG, 0)
            load_edges(0, 0)

            def pass_a(i, k, q):
                if type(i) is not int:
                    if q == 0:
                        sp.wait_ge(d_st[1], 16 * k)
                    else:
                        sp.wait_ge(d_st[0], 16 * (k + 1))
                    load_dense(i + 1, 1 - q, DA * TG, 0)
                    sp.wait_ge(deg_ready, i)
                    sp.wait_ge(mean_ready, i)
                    load_edges(i + 1, 1 - q)
                sp.wait_ge(s_norm[q], k + 1)
                sp.dma_start(rows_of(tab1, E, i), ne[:, :, :]).then_inc(st_ns, 16)
                sp.wait_ge(t_x1[q], k + 1)
                sp.dma_start(rows_of(x1_dram, 0, i), x1e[:, :, :]).then_inc(st_x1, 16)
                sp.wait_ge(s_yn, i + 1)
                sp.dma_start(rows_of(tab2, E, i), ye[:, :, :]).then_inc(st_zs, 16)
                sp.wait_ge(t_norm, i + 1)
                sp.dma_start(rows_of(tab1, 0, i), ne2[:, :, :]).then_inc(st_nt, 16)
                sp.wait_ge(dve_const, 1)
                sp.wait_ge(t_h, i + 1)
                sp.dma_start(grp(own1_dram, i, GE), fo[:, :]).then_inc(st_h, 16)
                sp.wait_ge(d_out, i + 1)
                sp.dma_start(dense_rows(out, i, DA * TG, 0), xd[:, q, :, :]).then_inc(d_st[q], 16)

            in_pairs(sp, pass_a)

            def load_own(dr, i, q):
                sp.dma_start(own[:, q, :], grp(dr, i, GE)).then_inc(ld_e[q], 16)

            sp.wait_ge(st_h, 16 * NG)
            sp.wait_ge(d_st[0], 16 * slot_base(0))
            load_dense(0, 0, TG, PASS_B[1])
            load_own(own1_dram, 0, 0)

            def pass_b(i, k, q):
                if type(i) is not int:
                    if q == 0:
                        sp.wait_ge(d_st[1], 16 * (k + slot_base(1)))
                    else:
                        sp.wait_ge(d_st[0], 16 * (k + 1 + slot_base(0)))
                    load_dense(i + 1, 1 - q, TG, PASS_B[1])
                    sp.wait_ge(dve_const, 1)
                    sp.wait_ge(m_y, i)
                    load_own(own1_dram, i + 1, 1 - q)
                sp.wait_ge(m_yn, i + 1)
                sp.dma_start(rows_of(tab2, 0, i), ye[:, :, :]).then_inc(st_zn, 16)
                sp.wait_ge(dve_const, 1)
                sp.wait_ge(m_z, i + 1)
                sp.dma_start(grp(own2_dram, i, GE), fo[:, :]).then_inc(st_z, 16)
                sp.wait_ge(d_out, i + 1 + NG)
                sp.dma_start(dense_rows(out, i, TG, PASS_B[1]), xd[:, q, 0:TG, :]).then_inc(d_st[q], 16)

            in_pairs(sp, pass_b)

            def load_x1(i, q):
                sp.dma_start(xd[:, q, 0:TG, :], rows_of(x1_dram, 0, i)).then_inc(d_x[q], 16)

            sp.wait_ge(st_z, 16 * NG)
            sp.wait_ge(st_x1, 16 * NG)
            for q in range(2):
                sp.wait_ge(d_st[q], 32 * slot_base(q))
            load_own(own2_dram, 0, 0)
            load_x1(0, 0)

            def pass_c(i, k, q):
                if type(i) is not int:
                    sp.wait_ge(dve_const, 1)
                    sp.wait_ge(m_y, i + NG)
                    load_own(own2_dram, i + 1, 1 - q)
                    sp.wait_ge(m_out, i)
                    load_x1(i + 1, 1 - q)

            in_pairs(sp, pass_c)

        @block.gpsimd
        def _(pool):
            pool_reg = pool.alloc_register("pool_reg")
            pool.reg_mov(pool_reg, 0)
            pool.wait_ge(dve_const, 1)
            nc.gpsimd.affine_select(out=ident[:, :], in_=ident[:, :], compare_op=ALU.not_equal, fill=1.0,
                                    base=0, pattern=[[-1, 128]], channel_multiplier=1)
            nc.gpsimd.affine_select(out=identb[:, :], in_=identb[:, :], compare_op=ALU.not_equal, fill=1.0,
                                    base=0, pattern=[[-1, 128]], channel_multiplier=1)
            nc.gpsimd.affine_select(out=anti[:, :], in_=anti[:, :], compare_op=ALU.not_equal, fill=1.0,
                                    base=-(P - 1), pattern=[[1, 128]], channel_multiplier=1).then_inc(pool_const, 1)
            for m in range(3):
                if m:
                    pool.wait_ge(pool_const, m + 1)
                s = nc.gpsimd.affine_select(out=sel[:, :, :], in_=sel[:, :, :], compare_op=ALU.not_equal, fill=1.0,
                                            base=-R1 * m, pattern=[[-1, R1], [0, 128]], channel_multiplier=1)
                s.then_inc(pool_const, 1)
            exact = dict(allow_small_or_imprecise_dtypes=True)
            nc.gpsimd.iota(iota_lo[:, :], [[1, LOB]], base=0, channel_multiplier=0, **exact)
            nc.gpsimd.iota(rowno[:, :], [[0, 1]], base=0, channel_multiplier=1, **exact)
            nc.gpsimd.iota(tileno[:, :], [[LOB // 2, NT]], base=LOB // 2, channel_multiplier=0, **exact)
            nc.gpsimd.iota(slotno[:, :], [[P, NT]], base=E, channel_multiplier=1, **exact)
            nc.gpsimd.iota(relno[:, :], [[0, 1]], base=0, channel_multiplier=1, **exact)
            nc.gpsimd.memset(epst[:, :], EPS).then_inc(pool_const, 1)

            pool.wait_ge(idx_ready, 1)

            def now(i, k, q, ap, c0, n):
                cur = ap[:, i, :] if type(i) is int else ap[:, bass.ds(i, 1), :].squeeze(1)
                copies = counted(pool, pool_reg)
                nc.gpsimd.tensor_copy(nowidx[:, q, c0:c0 + n], cur).then_inc(now_ready, 1)
                return copies

            def gather_a(i, k, q):
                pool.wait_ge(g_d[q], 64 * k)
                pool.wait_ge(idx_ready, 1)
                copies = now(i, k, q, gidx, 0, 2 * TG)
                pool.wait_ge(idx_split, 1)
                pool.wait_ge(s_norm[q], k)
                pool.wait_ge(t_x1[q], k)
                pool.wait_ge(now_ready, copies)
                for j in range(2 * TG):
                    pool.indirect_dma_start(
                        out=gat[:, q, j, :], out_offset=None, in_=x,
                        in_offset=bass.IndirectOffsetOnAxis(ap=nowidx[:, q, j:j + 1], axis=0),
                    ).then_inc((g_s if j < TG else g_d)[q], 16)

            in_pairs(pool, gather_a)

            def gather_m(tab, i, k, q, base):
                pool.wait_ge(m_gT[q], k + (slot_base(q) if base else 0))
                pool.wait_ge(slots_ready, 1)
                copies = now(i, k, q, sidx, 0, TG)
                pool.wait_ge(idx_split, 1)
                pool.wait_ge(now_ready, copies)
                for j in range(TG):
                    pool.indirect_dma_start(
                        out=gat[:, q, j, :], out_offset=None, in_=tab,
                        in_offset=bass.IndirectOffsetOnAxis(ap=nowidx[:, q, j:j + 1], axis=0),
                    ).then_inc(g_s[q], 16)

            pool.wait_ge(st_ns, 16 * NG)
            pool.wait_ge(st_nt, 16 * NG)
            in_pairs(pool, lambda i, k, q: gather_m(tab1, i, k, q, 0))
            pool.wait_ge(st_zs, 16 * NG)
            pool.wait_ge(st_zn, 16 * NG)
            for q in range(2):
                pool.wait_ge(d_st[q], 32 * slot_base(q))

            def scatter(i):
                pool.wait_ge(st_out, 16 * TG * i)
                pool.wait_ge(slots_ready, 1)
                cur = tidx[:, i, :] if type(i) is int else tidx[:, bass.ds(i, 1), :].squeeze(1)
                nc.gpsimd.tensor_copy(nowout[:, :], cur).then_inc(out_now, 1)
                pool.wait_ge(slots_ready, 1)
                pool.wait_ge(out_now, i + 1)
                pool.wait_ge(m_out, i + 1)
                for j in range(TG):
                    pool.indirect_dma_start(
                        out=out, out_offset=bass.IndirectOffsetOnAxis(ap=nowout[:, j:j + 1], axis=0),
                        in_=x1e[:, j, :], in_offset=None, bounds_check=N - 1, oob_is_err=False,
                    ).then_inc(st_out, 16)

            gather_m(tab2, 0, 0, 0, NG)
            with pool.Fori(0, NG // 2) as k:
                gather_m(tab2, k * 2 + 1, k, 1, NG)
                scatter(k * 2)
                gather_m(tab2, k * 2 + 2, k + 1, 0, NG)
                scatter(k * 2 + 1)
            scatter(NG - 1)
            pool.wait_ge(st_out, 16 * TG * NG)

        @block.scalar
        def _(act):
            def root_of(dst, src_, ready, n, done, scale=1.0):
                act.wait_ge(ready, n)
                nc.scalar.activation(dst, src_, ACT.Sqrt, bias=epst[0:P, :], scale=scale).then_inc(done, 1)

            def bring(dst, src_, ready, n, done, func=ACT.Copy):
                act.wait_ge(ready, n)
                nc.scalar.activation(dst, src_, func).then_inc(done, 1)

            def affine(dst, src_, l, ready, n, done):
                act.wait_ge(ready, n)
                nc.scalar.activation(dst, src_, ACT.Identity, bias=ln[:, 2 * l + 1:2 * l + 2],
                                     scale=ln[:, 2 * l:2 * l + 1]).then_inc(done, 1)

            def hot(i, k, q):
                act.wait_ge(hot_turned, i + 1)
                nc.scalar.activation(hot_hit[:, :, 0:P],
                                     eT[0:HIC, :].bitcast(BF16).rearrange("p (c e) -> p c e", e=128)[:, :, 0:P],
                                     ACT.Copy).then_inc(hot_saved, 1)

            with act.Fori(0, NG) as i:
                hot(i, 0, 0)
            act.wait_ge(pool_const, 5)
            act.wait_ge(ld_w, 16 * 17)

            def dense(part, n, pas):
                nt, _, base = pas
                g = nt // TG
                n = n + base
                Y = dY[0:P, 0:g, :].rearrange("p g (t f) -> p (g t) f", f=D)
                if part == 0:
                    root_of(sd_d[:, 0:nt], mv_d[:, 1, 0:nt], d_var, n, d_sd, 1.0 / D)
                elif part == 1:
                    bring(fd[:, 0:g, :], dT[:, 0:g, 0:GE], d_hT, n, d_h, ACT.Relu)
                elif part == 2:
                    bring(nd[:, 0:nt, :], Y, d_y, n, d_ys)
                elif part == 3:
                    root_of(sd_d[:, 0:nt], ss_d[:, 0:nt], d_sq, n, d_sd1, 1.0 / D)
                elif part == 4:
                    affine(fd[:, 0:g, :], dT[:, 0:g, 0:GE], 0, d_ynT, n, d_t)
                elif part == 5:
                    bring(nd[:, 0:nt, :], Y, d_y2, n, d_ys2)
                elif part == 6:
                    root_of(sd_d[:, 0:nt], ss_d[:, 0:nt], d_sq2, n, d_sd2, 1.0 / D)
                elif part == 7:
                    affine(fd[:, 0:g, :], dT[:, 0:g, 0:GE], 1, d_yn2T, n, d_t2)

            eYr = eY[0:P, :].rearrange("p (t f) -> p t f", f=D)
            eTr = eT[0:P, :].rearrange("p (t f) -> p t f", f=D)

            def pass_a(i, k, q):
                n = i + 1
                root_of(sd_e[:, :], mv_e[:, 1, :], s_var, n, s_sd, 1.0 / D)
                dense(0, n, PASS_A)
                bring(fe[:, :], eT[:, 0:GE], s_hT, n, s_h, ACT.Relu)
                dense(1, n, PASS_A)
                act.wait_ge(st_zs, 16 * i)
                bring(ye[:, :, :], eTr, s_y, n, s_ys)
                dense(2, n, PASS_A)
                root_of(sd_e[:, :], ss_e[:, :], s_sq, n, s_sd1, 1.0 / D)
                dense(3, n, PASS_A)
                root_of(sd_e[:, :], mv_e[:, 1, :], t_var, n, t_sd, 1.0 / D)
                dense(4, n, PASS_A)
                act.wait_ge(st_h, 16 * i)
                bring(fo[:, :], eY[:, 0:GE], t_hT, n, t_h, ACT.Relu)
                dense(5, n, PASS_A)
                dense(6, n, PASS_A)
                dense(7, n, PASS_A)

            in_pairs(act, pass_a)
            act.wait_ge(st_zs, 16 * NG)

            def edges(part, n, i, k, q, l):
                if part == 0:
                    if l == 0:
                        bring(fe[:, :], eT[:, 0:GE], m_gT[q], k + 1, m_g, ACT.Relu)
                    else:
                        affine(msg[:, :], eT[:, 0:GE], 0, m_gT[q], k + 1 + slot_base(q), m_t)
                elif part == 1:
                    if l == 0:
                        act.wait_ge(st_zn, 16 * i)
                    bring(ye[:, :, :], eYr, m_y, n, m_ys)
                elif part == 2:
                    root_of(sd_e[:, :], ss_e[:, :], m_sq, n, m_sd, 1.0 / D)
                elif part == 3:
                    affine(mean[:, :], bZ[:, 0:GE], l, m_ynT, n, m_tt)

            def pass_b(i, k, q):
                n = i + 1
                dense(0, n, PASS_B)
                edges(0, n, i, k, q, 0)
                dense(1, n, PASS_B)
                dense(2, n, PASS_B)
                dense(3, n, PASS_B)
                dense(4, n, PASS_B)
                edges(1, n, i, k, q, 0)
                dense(5, n, PASS_B)
                edges(2, n, i, k, q, 0)
                dense(6, n, PASS_B)
                edges(3, n, i, k, q, 0)
                dense(7, n, PASS_B)

            in_pairs(act, pass_b)
            act.wait_ge(st_zn, 16 * NG)

            def pass_c(i, k, q):
                for part in range(4):
                    edges(part, i + 1 + NG, i, k, q, 1)

            in_pairs(act, pass_c)

        @block.tensor
        def _(pe):
            pe_reg = pe.alloc_register("pe_reg")
            pe.reg_mov(pe_reg, 0)
            pe.wait_ge(pool_const, 5)
            pe.wait_ge(idx_split, 1)
            for m in range(7):
                bank = dT[0:P, m // 4, (m % 4) * 128:(m % 4) * 128 + NT]
                t = nc.tensor.transpose(bank, turn[:, m, :], ident[0:NT, 0:NT])
            t.then_inc(idx_turned, 1)

            pe.wait_ge(dve_const, 2)
            tbank = [[dY[0:HIC, 0, 0:LOB], dY[0:HIC, 1, 0:LOB]], [dY[0:HIC, 2, 0:LOB], eY[0:HIC, 0:LOB]]]
            for v in range(2):
                for c in range(2):
                    nc.tensor.matmul(tbank[v][c], zerob[0:P, 0:HIC], zerob[0:P, :], start=True, stop=False)
            with pe.Fori(0, NG) as i:
                pe.wait_ge(tab_hot, i + 1)
                for j in range(TG):
                    for v in range(2):
                        for c in range(2):
                            t = nc.tensor.matmul(tbank[v][c], hot_hi[:, j, c * HIC:(c + 1) * HIC],
                                                 hot_lo[:, v, j, :], start=False, stop=False)
                t.then_inc(tab_added, 1)
            for v in range(2):
                for c in range(2):
                    t = nc.tensor.matmul(tbank[v][c], zerob[0:P, 0:HIC], zerob[0:P, :], start=False, stop=True)
            t.then_inc(tab_sum, 1)

            pe.wait_ge(tab_ready, 1)
            with pe.Fori(0, NG) as i:
                pe.wait_ge(hot_ready, i + 1)
                turned = eT[0:HIC, :].bitcast(BF16).rearrange("p (c e) -> p c e", e=128)
                for j in range(TG):
                    for c in range(2):
                        t = nc.tensor.transpose(turned[:, 2 * j + c, 0:P], hot_hi[:, j, c * HIC:(c + 1) * HIC],
                                                identb[0:P, 0:P])
                t.then_inc(hot_turned, 1)
                pe.wait_ge(hot_saved, i + 1)
                pe.wait_ge(looked_used, i)
                for j in range(TG):
                    bank = dT[0:P, j // 2, (j % 2) * LOB:(j % 2 + 1) * LOB]
                    for c in range(2):
                        for v in range(2):
                            t = nc.tensor.matmul(bank, hot_hit[:, 2 * j + c, 0:P], node_tab[:, v, c, :],
                                                 start=(c == 0 and v == 0), stop=(c == 1 and v == 1))
                t.then_inc(looked, 1)

            pe.wait_ge(ld_w, 16 * 17)
            with pe.Fori(0, NCH) as c:
                pe.wait_ge(cnt_prods, c + 1)
                pe.wait_ge(cnt_saved, c)
                prod = nd[0:64, :, :].rearrange("p t f -> p (t f)")
                for j in range(CT):
                    e = slice(j * P, (j + 1) * P)
                    nc.tensor.matmul(eT[0:P, j:j + 1], prod[0:32, e], ones[0:32, 0:1], start=True, stop=True)
                for j in range(CT):
                    e = slice(j * P, (j + 1) * P)
                    nc.tensor.matmul(eY[0:P, j:j + 1], prod[32:64, e], ones[32:64, 0:1], start=True, stop=True)
                for j in range(CT):
                    e = slice(j * P, (j + 1) * P)
                    t = nc.tensor.matmul(dT[0:P, 0, j * R1:(j + 1) * R1], hotc[0:32, e], compt[:, :],
                                         start=True, stop=True)
                t.then_inc(cnt_summed, 1)
            pe.wait_ge(cnt_saved, NCH)
            nc.tensor.matmul(eT[0:P, 0:NT], anti[0:P, 0:P], cnt_b[:, :], start=True, stop=True).then_inc(cnt_flipped, 1)
            with pe.Fori(0, NG) as i:
                copied = counted(pe, pe_reg)
                pe.wait_ge(dve_const, 1)
                pe.wait_ge(coef_now, copied)
                turned = eY[0:48, :].bitcast(BF16)
                for j in range(TG):
                    t = nc.tensor.transpose(turned[:, j * 128:j * 128 + P], coef3g[:, j, :], identb[0:P, 0:P])
                t.then_inc(coef_turned, 1)
            pe.wait_ge(coef_ready, NG)
            pe.wait_ge(w_ready, 1)

            def turn_rows(bank, rows, nt):
                for j in range(nt):
                    t = nc.tensor.transpose(bank[:, j // TG, (j % TG) * P:(j % TG + 1) * P], rows[:, j, :],
                                            ident[0:P, 0:P])
                return t

            def turn_back(bank, cols, nt):
                for j in range(nt):
                    t = nc.tensor.transpose(bank[0:P, j // TG, (j % TG) * D:(j % TG + 1) * D],
                                            cols[:, j // TG, (j % TG) * P:(j % TG + 1) * P], ident[:, :])
                return t

            def rows_out(bank, cols, l, nt, more=None):
                for g in range(nt // TG):
                    nc.tensor.matmul(bank[0:P, g, :], onesb[0:96, 0:P], bias[:, l, :, :].rearrange("p t f -> p (t f)"),
                                     start=True, stop=False)
                    for j in range(TG):
                        e = slice(j * P, (j + 1) * P)
                        o = bank[0:P, g, j * D:(j + 1) * D]
                        last = j == TG - 1
                        t = nc.tensor.matmul(o, cols[:, g, e], wt[:, l, 0, :], start=False, stop=last and more is None)
                        if more is not None:
                            t = nc.tensor.matmul(o, more[:, e], ident[:, :], start=False, stop=last)
                return t

            e1 = lambda ap: ap.unsqueeze(1)
            eTb, eYb, bZb = e1(eT[:, :]), e1(eY[:, :]), e1(bZ)

            def dense(part, n, pas):
                nt, _, base = pas
                n = n + base
                if part == 0:
                    pe.wait_ge(d_norm, n)
                    turn_rows(dT, nd, nt).then_inc(d_hT, 1)
                elif part == 1:
                    pe.wait_ge(d_h, n)
                    rows_out(dY, fd, 0, nt).then_inc(d_y, 1)
                elif part == 2:
                    pe.wait_ge(d_yn, n)
                    turn_rows(dT, nd, nt).then_inc(d_ynT, 1)
                elif part == 3:
                    pe.wait_ge(d_z, n)
                    rows_out(dY, zd, 1, nt).then_inc(d_y2, 1)
                elif part == 4:
                    pe.wait_ge(d_yn2, n)
                    turn_rows(dT, nd, nt).then_inc(d_yn2T, 1)
                elif part == 5:
                    pe.wait_ge(d_z2, n)
                    turn_back(dY, zd, nt).then_inc(d_back, 1)

            def pass_a(i, k, q):
                n = i + 1
                pe.wait_ge(s_norm[q], k + 1)
                turn_rows(eTb, ne, TG).then_inc(s_hT, 1)
                dense(0, n, PASS_A)
                pe.wait_ge(s_h, n)
                nc.tensor.matmul(eY[:, 0:GE], w0t[:, :], fe[:, :], start=True, stop=True).then_inc(s_m0, 1)
                rows_out(eTb, e1(fe[:, :]), 0, TG).then_inc(s_y, 1)
                dense(1, n, PASS_A)
                pe.wait_ge(mean_ready, n)
                turn_back(eYb, e1(mean[:, :]), TG).then_inc(mean_T, 1)
                dense(2, n, PASS_A)
                pe.wait_ge(t_norm, n)
                turn_rows(eYb, ne2, TG).then_inc(t_hT, 1)
                dense(3, n, PASS_A)
                dense(4, n, PASS_A)
                dense(5, n, PASS_A)

            pe.wait_ge(ld_w, 16 * 17)
            in_pairs(pe, pass_a)

            def edges(part, n, i, k, q, l):
                if part == 0:
                    pe.wait_ge(g_s[q], 64 * (k + 1 + (1 + l) * slot_base(q)))
                    turn_rows(eTb, gat[:, q, :, :], TG).then_inc(m_gT[q], 1)
                elif part == 1:
                    def spread(b):
                        nc.tensor.matmul(bQ[b % 2][:, 0:GE], sel[:, l * B1 + b, :], grp(coeft, i, GE),
                                         start=True, stop=True).then_inc(m_bc, 1)
                    spread(0)
                    spread(1)
                    for b in range(B1):
                        pe.wait_ge(m_sc, (n - 1) * B1 + b + 1)
                        nc.tensor.matmul(bM[:, 0:GE], wt[:, l, 1 + b, :], scaled[:, b % 2, :],
                                         start=(b == 0), stop=(b == B1 - 1)).then_inc(m_mm, 1)
                        if b + 2 < B1:
                            spread(b + 2)
                elif part == 2:
                    pe.wait_ge(m_agg, n)
                    pe.wait_ge(ld_e[q], 32 * slot_base(q) + 16 * (k + 1 + l * slot_base(q)))
                    rows_out(eYb, e1(own[:, q, :]), l, TG, agg).then_inc(m_y, 1)
                elif part == 3:
                    pe.wait_ge(m_yn, n)
                    turn_rows(bZb, ye, TG).then_inc(m_ynT, 1)
                elif part == 4:
                    pe.wait_ge(m_z, n)
                    turn_back(bZb, e1(fo[:, :]), TG).then_inc(m_back, 1)

            def pass_b(i, k, q):
                n = i + 1
                edges(0, n, i, k, q, 0)
                dense(0, n, PASS_B)
                dense(1, n, PASS_B)
                dense(2, n, PASS_B)
                edges(1, n, i, k, q, 0)
                edges(2, n, i, k, q, 0)
                dense(3, n, PASS_B)
                edges(3, n, i, k, q, 0)
                dense(4, n, PASS_B)
                dense(5, n, PASS_B)

            in_pairs(pe, pass_b)

            def pass_c(i, k, q):
                for part in range(5):
                    edges(part, i + 1 + NG, i, k, q, 1)

            in_pairs(pe, pass_c)

        @block.vector
        def _(dve):
            v = nc.vector
            steps = [0]

            def own_step(ins):
                steps[0] += 1
                ins.then_inc(prep, 1)
                dve.wait_ge(prep, steps[0])

            for t in (ident, identb, anti):
                v.memset(t[:, :], 0.0)
            v.memset(sel[:, :, :], 0.0)
            v.memset(compt[:, :], 0.0).then_inc(dve_const, 1)
            v.memset(zerob[:, :], 0.0)
            v.memset(ones[:, :], 1.0)
            v.memset(onesb[:, :], 1.0)
            v.memset(bias[:, :, :, :], 0.0)
            v.memset(carryc[:, :], 0.0)
            for r in range(4):
                v.memset(blockno[r * HEAD:(r + 1) * HEAD, :], float(r))
            v.memset(carry[:, :], 0.0).then_inc(dve_const, 1)

            dve.wait_ge(ld_idx, 48)
            v.tensor_copy(rawf[:, :, :], raw[:, :, :])
            for m in range(2):
                v.tensor_single_scalar(part[:, 2 * m, :], raw[:, m, :], 8, ALU.logical_shift_right)
                own_step(v.tensor_single_scalar(part[:, 2 * m + 1, :], raw[:, m, :], LOB - 1, ALU.bitwise_and))
            v.tensor_copy(turn[:, 0:2, :], rawf[:, 0:2, :])
            own_step(v.tensor_tensor(lastf[:, :], rawf[:, DST_, :], rawf[:, OUT_, :], ALU.is_equal))
            v.scalar_tensor_tensor(turn[:, 2, :], lastf[:, :], float(1 << 20), rawf[:, DST_, :], ALU.mult, ALU.add)
            v.tensor_copy(turn[:, 3:7, :], part[:, :, :])
            own_step(v.tensor_copy(rawf[:, 2, :], part[:, 2, :]))
            v.scalar_tensor_tensor(turn[:, 5, :], lastf[:, :], 1024.0, rawf[:, 2, :],
                                   ALU.mult, ALU.add).then_inc(idx_split, 1)
            dve.wait_ge(idx_turned, 1)
            tb = lambda m: dT[0:P, m // 4, (m % 4) * 128:(m % 4) * 128 + NT].rearrange("p (g t) -> p g t", t=TG)
            v.tensor_copy(gidx[:, :, 0:TG], tb(0))
            v.tensor_copy(gidx[:, :, TG:2 * TG], tb(1)).then_inc(idx_ready, 1)
            v.tensor_copy(tidx[:, :, :], tb(2))
            for m in range(4):
                v.tensor_copy(meta[:, :, m * TG:(m + 1) * TG], tb(3 + m))
            dve.wait_ge(pool_const, 5)
            v.tensor_scalar(relno[32:64, :], relno[32:64, :], -32.0, None, ALU.add)
            own_step(v.tensor_copy(meta[:, :, 4 * TG:5 * TG], tileno[:, :].rearrange("p (g t) -> p g t", t=TG)))

            tab0 = steps[0]
            with dve.Fori(0, NG) as i:
                dve.wait_ge(tab_added, i)
                v.tensor_copy(metat[:, 0:5 * TG], meta[:, bass.ds(i, 1), 0:5 * TG].squeeze(1)).then_inc(prep, 1)
                dve.wait_ge(prep, i + tab0 + 1)
                for j in range(TG):
                    c = lambda m: metat[:, m * TG + j:m * TG + j + 1]
                    v.tensor_scalar(hot_hi[:, j, :], iota_lo[:, 0:2 * HIC], c(2), None, ALU.is_equal)
                    v.tensor_scalar(hot_lo[:, 0, j, :], iota_lo[:, :], c(3), c(4), ALU.is_equal, ALU.mult)
                    t = v.tensor_scalar(hot_lo[:, 1, j, :], iota_lo[:, :], c(3), rowno[:, :], ALU.is_equal, ALU.mult)
                t.then_inc(tab_hot, 1)
            steps[0] += NG
            dve.wait_ge(tab_sum, 1)
            v.tensor_copy(node_tab[:, 0, :, :], dY[0:HIC, 0:2, 0:LOB])
            v.tensor_copy(node_tab[:, 1, 0, :], dY[0:HIC, 2, 0:LOB])
            v.tensor_copy(node_tab[:, 1, 1, :], eY[0:HIC, 0:LOB]).then_inc(tab_ready, 1)

            look0 = steps[0]
            with dve.Fori(0, NG) as i:
                v.tensor_copy(metat[:, 0:2 * TG], meta[:, bass.ds(i, 1), 0:2 * TG].squeeze(1)).then_inc(prep, 1)
                dve.wait_ge(prep, i + look0 + 1)
                for j in range(TG):
                    v.tensor_scalar(hot_lo[:, 0, j, :], iota_lo[:, :], metat[:, TG + j:TG + j + 1], None, ALU.is_equal)
                    t = v.tensor_scalar(hot_hi[:, j, :], iota_lo[:, 0:2 * HIC], metat[:, j:j + 1], None, ALU.is_equal)
                t.then_inc(hot_ready, 1)
                dve.wait_ge(looked, i + 1)
                for j in range(TG):
                    bank = dT[0:P, j // 2, (j % 2) * LOB:(j % 2 + 1) * LOB]
                    t = v.tensor_tensor_reduce(junk_d[:, 2 * j:2 * j + 2, :].rearrange("p a b -> p (a b)"), bank, hot_lo[:, 0, j, :], 1.0, 0.0, ALU.mult, ALU.add,
                                               res[:, j:j + 1])
                t.then_inc(looked_used, 1)
                dve.wait_ge(looked_used, i + 1)
                t = v.tensor_copy(found[:, bass.ds(i * TG, TG)], res[:, :])
                t.then_inc(tab_ready, 1)
            steps[0] += NG
            dve.wait_ge(tab_ready, 1 + NG)
            own_step(v.tensor_copy(foundi[:, :], found[:, :]))
            own_step(v.tensor_single_scalar(foundi[:, :], foundi[:, :], 7, ALU.logical_shift_right))
            own_step(v.tensor_copy(hit[:, :], foundi[:, :]))
            own_step(v.scalar_tensor_tensor(slotf[:, :], hit[:, :], float(P - 128), found[:, :], ALU.mult, ALU.add))
            own_step(v.tensor_scalar(slotf[:, :], slotf[:, :], -float(P), None, ALU.add))
            own_step(v.tensor_tensor(slotf[:, :], slotf[:, :], slotno[:, :], ALU.subtract))
            own_step(v.tensor_scalar(hit[:, :], hit[:, :], 0.5, None, ALU.is_gt))
            own_step(v.tensor_tensor(slotf[:, :], slotf[:, :], hit[:, :], ALU.mult))
            own_step(v.tensor_tensor(slotf[:, :], slotf[:, :], slotno[:, :], ALU.add))
            v.tensor_copy(sidx[:, :, :], slotf[:, :].rearrange("p (g t) -> p g t", t=TG)).then_inc(slots_ready, 1)

            contc = fd[0:64, :, :].rearrange("p g e -> p (g e)")[:, 0:CE]
            runc = zd[0:64, :, :].rearrange("p g e -> p (g e)")[:, 0:CE]
            prodc = nd[0:64, :, :].rearrange("p t f -> p (t f)")[:, 0:CE]
            cnt0 = steps[0]
            PER = 3
            with dve.Fori(0, NCH) as c:
                dve.wait_ge(ld_cnt, 64 * (c + 1))
                v.tensor_tensor(contc, dstc[:, 1:CE + 1], dstc[:, 0:CE], ALU.is_equal)
                v.tensor_scalar(hotc[:, :], etc[:, :], relno[:, :], None, ALU.is_equal).then_inc(prep, 1)
                dve.wait_ge(prep, c * PER + cnt0 + 1)
                v.tensor_tensor_scan(runc, contc, hotc[:, :], carryc[:, :], ALU.mult, ALU.add).then_inc(prep, 1)
                dve.wait_ge(prep, c * PER + cnt0 + 2)
                v.tensor_copy(carryc[:, :], runc[:, CE - 1:CE]).then_inc(prep, 1)
                v.tensor_tensor(prodc, runc, hotc[:, :], ALU.mult).then_inc(cnt_prods, 1)
                dve.wait_ge(prep, c * PER + cnt0 + 3)
                dve.wait_ge(cnt_summed, c + 1)
                v.tensor_copy(cnt_f[:, bass.ds(c * CT, CT)], eT[0:P, 0:CT])
                for j in range(CT):
                    v.tensor_copy(cnt_b[:, bass.ds(NT - 1 - j - c * CT, 1)], eY[0:P, j:j + 1])
                v.tensor_copy(coef[:, bass.ds(c * CT, CT), :],
                              dT[0:P, 0, 0:CT * R1].rearrange("p (t r) -> p t r", r=R1)).then_inc(cnt_saved, 1)
            steps[0] += NCH * PER
            dve.wait_ge(cnt_saved, NCH)
            dve.wait_ge(cnt_flipped, 1)
            own_step(v.scalar_tensor_tensor(cnt_f[:, :], cnt_f[:, :], -1.0, eT[0:P, 0:NT], ALU.add, ALU.add))
            own_step(v.reciprocal(cnt_b[:, :], cnt_f[:, :]))
            own_step(v.tensor_tensor(coef[:, :, :], coef[:, :, :],
                                     cnt_b[:, :].unsqueeze(2).to_broadcast([P, NT, R1]), ALU.mult))
            for m in range(3):
                own_step(v.tensor_copy(coef3[:, :, m * R1:(m + 1) * R1], coef[:, :, :]))
                if m < 2:
                    own_step(v.tensor_tensor(coef[:, :, :], coef[:, :, :], coef3[:, :, m * R1:(m + 1) * R1],
                                             ALU.subtract))
            with dve.Fori(0, NG) as i:
                v.tensor_copy(coef3g[:, :, :], coef3[:, bass.ds(i * TG, TG), :]).then_inc(coef_now, 1)
                dve.wait_ge(coef_turned, i + 1)
                v.tensor_copy(grp(coeft, i, GE).rearrange("p (t e) -> p t e", e=P),
                              eY[0:48, :].bitcast(BF16).rearrange("p (t e) -> p t e", e=128)[:, 0:TG, 0:P],
                              ).then_inc(coef_ready, 1)

            dve.wait_ge(ld_w, 16 * 17)
            wv = wt[:, :, :, :].rearrange("p l b f -> p (l b) f")
            own_step(v.tensor_reduce(wsum[:, :], wv, AX.X, ALU.add))
            own_step(v.tensor_scalar(wsum[:, :], wsum[:, :], 1.0 / D, None, ALU.mult))
            own_step(v.tensor_tensor(wv, wv, wsum[:, :].unsqueeze(2).to_broadcast([128, 18, 128]), ALU.subtract))
            own_step(v.tensor_reduce(bsum[:, :], brow[:, :, :], AX.X, ALU.add))
            own_step(v.tensor_scalar(bsum[:, :], bsum[:, :], 1.0 / D, None, ALU.mult))
            own_step(v.tensor_tensor(brow[:, :, :], brow[:, :, :], bsum[:, :].unsqueeze(2).to_broadcast([96, 2, 128]),
                                     ALU.subtract))
            for m in range(3):
                own_step(v.tensor_copy(bpart[:, :, :], brow[:, :, :]))
                for l in range(2):
                    v.tensor_copy(bias[32 * m:32 * m + 1, l, :, :],
                                  bpart[32 * m:32 * m + 1, l, :].unsqueeze(1).to_broadcast([1, TG, 128]))
                own_step(v.tensor_tensor(brow[:, :, :], brow[:, :, :], bpart[:, :, :], ALU.subtract))
            v.tensor_copy(bsum[:, :], bsum[:, :]).then_inc(w_ready, 1)

            def moments(rows, nt, st, mv, stats, n, var):
                for j in range(nt):
                    t = v.bn_stats(st[:, j, :], rows[:, j, :])
                t.then_inc(stats, 1)
                dve.wait_ge(stats, n * 3 - 2)
                c = lambda m: st[:, 0:nt, m]
                v.tensor_tensor(mv[:, 2, 0:nt], c(1), c(4), ALU.subtract)
                v.tensor_tensor(mv[:, 0, 0:nt], c(1), c(4), ALU.add)
                v.tensor_tensor(mv[:, 1, 0:nt], c(2), c(5), ALU.add).then_inc(stats, 1)
                dve.wait_ge(stats, n * 3 - 1)
                v.tensor_scalar(mv[:, 0, 0:nt], mv[:, 0, 0:nt], 0.5, None, ALU.mult)
                v.scalar_tensor_tensor(mv[:, 2, 0:nt], mv[:, 2, 0:nt], D / 4.0, mv[:, 2, 0:nt],
                                       ALU.mult, ALU.mult).then_inc(stats, 1)
                dve.wait_ge(stats, n * 3)
                v.tensor_tensor(mv[:, 1, 0:nt], mv[:, 1, 0:nt], mv[:, 2, 0:nt], ALU.add).then_inc(var, 1)

            def squares(rows, nt, ss, junk, done):
                for j in range(nt):
                    t = v.tensor_tensor_reduce(junk[:, j, :], rows[:, j, :], rows[:, j, :], 1.0, 0.0,
                                               ALU.mult, ALU.add, ss[:, j:j + 1])
                t.then_inc(done, 1)

            def inverse(rs, sd, nt, ready, n, done):
                dve.wait_ge(ready, n)
                v.reciprocal(rs[:, 0:nt], sd[:, 0:nt]).then_inc(done, 1)
                dve.wait_ge(done, n)

            def scale_rows(dst, rows, rs, nt, done, mv=None):
                for j in range(nt):
                    if mv is None:
                        t = v.tensor_scalar(dst[:, j, :], rows[:, j, :], rs[:, j:j + 1], None, ALU.mult)
                    else:
                        t = v.tensor_scalar(dst[:, j, :], rows[:, j, :], mv[:, 0, j:j + 1], rs[:, j:j + 1],
                                            ALU.subtract, ALU.mult)
                t.then_inc(done, 1)

            def leaky(dst, t_, ready, n, done):
                dve.wait_ge(ready, n)
                v.scalar_tensor_tensor(dst, t_, SLOPE, t_, ALU.mult, ALU.max).then_inc(done, 1)

            def dense(part, n, k, q, pas):
                nt, _, base = pas
                g = nt // TG
                n = n + base
                xq = xd[:, q, :, :]
                if part == 0:
                    dve.wait_ge(d_x[q], 16 * (k + 1 + (slot_base(q) if base else 0)))
                    moments(xq, nt, st_d, mv_d, d_stats, n, d_var)
                elif part == 1:
                    inverse(rs_d, sd_d, nt, d_sd, n, d_rs)
                    scale_rows(nd, xq, rs_d, nt, d_norm, mv_d)
                elif part == 2:
                    dve.wait_ge(d_ys, n)
                    squares(nd, nt, ss_d, junk_d, d_sq)
                elif part == 3:
                    inverse(rs_d, sd_d, nt, d_sd1, n, d_rs1)
                    scale_rows(nd, nd, rs_d, nt, d_yn)
                elif part == 4:
                    leaky(zd[:, 0:g, :], fd[:, 0:g, :], d_t, n, d_z)
                elif part == 5:
                    dve.wait_ge(d_ys2, n)
                    squares(nd, nt, ss_d, junk_d, d_sq2)
                elif part == 6:
                    inverse(rs_d, sd_d, nt, d_sd2, n, d_rs2)
                    scale_rows(nd, nd, rs_d, nt, d_yn2)
                elif part == 7:
                    leaky(zd[:, 0:g, :], fd[:, 0:g, :], d_t2, n, d_z2)
                elif part == 8:
                    dve.wait_ge(d_back, n)
                    v.tensor_tensor(xq[:, 0:nt, :], xq[:, 0:nt, :],
                                    dY[0:P, 0:g, :].rearrange("p g (t f) -> p (g t) f", f=D), ALU.add).then_inc(d_out, 1)

            def pass_a(i, k, q):
                n = i + 1
                dve.wait_ge(g_s[q], 64 * (k + 1))
                moments(gat[:, q, :, :], TG, st_e, mv_e, s_stats, n, s_var)
                dense(0, n, k, q, PASS_A)
                inverse(rs_e, sd_e, TG, s_sd, n, s_rs)
                dve.wait_ge(st_ns, 16 * i)
                scale_rows(ne, gat[:, q, :, :], rs_e, TG, s_norm[q], mv_e)
                dense(1, n, k, q, PASS_A)
                dve.wait_ge(ld_e[q], 32 * (k + 1))
                v.tensor_scalar(mask[:, :], et5b[:, q, :], blockno[:, :], None, ALU.is_equal)
                v.tensor_tensor(grp(cont, i, GE), dstb[:, q, 1:GE + 1], dstb[:, q, 0:GE], ALU.is_equal
                                ).then_inc(cont_ready, 1)
                dve.wait_ge(cont_ready, n)
                v.tensor_tensor_scan(deg[:, :], grp(cont, i, GE), mask[:, :], carry[:, 0:1], ALU.mult, ALU.add
                                     ).then_inc(deg_ready, 1)
                dve.wait_ge(s_m0, n)
                v.scalar_tensor_tensor(msg[:, :], eY[:, 0:GE], b0t[:, 0:1], mask[:, :], ALU.add, ALU.mult
                                       ).then_inc(msg_ready, 1)
                dve.wait_ge(msg_ready, n)
                v.tensor_tensor_scan(agg[:, :], grp(cont, i, GE), msg[:, :], carry[:, 1:2], ALU.mult, ALU.add
                                     ).then_inc(agg_ready, 1)
                dve.wait_ge(deg_ready, n)
                dve.wait_ge(agg_ready, n)
                v.tensor_copy(carry[:, 0:1], deg[:, GE - 1:GE])
                v.tensor_copy(carry[:, 1:2], agg[:, GE - 1:GE]).then_inc(carried, 1)
                dve.wait_ge(carried, i * 3 + 1)
                v.tensor_scalar(deg[:, :], deg[:, :], 1.0, None, ALU.max).then_inc(carried, 1)
                dve.wait_ge(carried, i * 3 + 2)
                v.reciprocal(mean[:, :], deg[:, :]).then_inc(carried, 1)
                dve.wait_ge(carried, i * 3 + 3)
                v.tensor_tensor(mean[:, :], mean[:, :], agg[:, :], ALU.mult).then_inc(mean_ready, 1)
                dense(2, n, k, q, PASS_A)
                dve.wait_ge(mean_T, n)
                dve.wait_ge(g_d[q], 64 * (k + 1))
                dve.wait_ge(st_x1, 16 * i)
                v.tensor_tensor(x1e[:, :, :], gat[:, q, TG:2 * TG, :], eY[0:P, :].rearrange("p (t f) -> p t f", f=D),
                                ALU.add).then_inc(t_x1[q], 1)
                dve.wait_ge(s_ys, n)
                squares(ye, TG, ss_e, junk_e, s_sq)
                dense(3, n, k, q, PASS_A)
                inverse(rs_e, sd_e, TG, s_sd1, n, s_rs1)
                scale_rows(ye, ye, rs_e, TG, s_yn)
                dve.wait_ge(t_x1[q], k + 1)
                moments(x1e, TG, st_e, mv_e, t_stats, n, t_var)
                dense(4, n, k, q, PASS_A)
                inverse(rs_e, sd_e, TG, t_sd, n, t_rs)
                dve.wait_ge(st_nt, 16 * i)
                scale_rows(ne2, x1e, rs_e, TG, t_norm, mv_e)
                for part in range(5, 9):
                    dense(part, n, k, q, PASS_A)

            in_pairs(dve, pass_a)
            v.memset(carry[:, :], 0.0).then_inc(carried, 1)
            dve.wait_ge(carried, 3 * NG + 1)

            def edges(part, n, i, k, q, l):
                if part == 0:
                    if l == 0:
                        dve.wait_ge(m_g, n)
                    else:
                        leaky(fe[:, :], msg[:, :], m_t, i + 1, m_g)
                        dve.wait_ge(m_g, n)
                    for b in range(B1):
                        dve.wait_ge(m_bc, (n - 1) * B1 + b + 1)
                        if b >= 2:
                            dve.wait_ge(m_mm, (n - 1) * B1 + b - 1)
                        v.tensor_tensor(scaled[:, b % 2, :], fe[:, :], bQ[b % 2][:, 0:GE], ALU.mult).then_inc(m_sc, 1)
                elif part == 1:
                    dve.wait_ge(m_mm, n * B1)
                    v.tensor_tensor_scan(agg[:, :], grp(cont, i, GE), bM[:, 0:GE], carry[:, l:l + 1],
                                         ALU.mult, ALU.add).then_inc(m_agg, 1)
                    dve.wait_ge(m_agg, n)
                    v.tensor_copy(carry[:, l:l + 1], agg[:, GE - 1:GE]).then_inc(carried, 1)
                    dve.wait_ge(carried, n + 3 * NG + 1)
                elif part == 2:
                    dve.wait_ge(m_ys, n)
                    squares(ye, TG, ss_e, junk_e, m_sq)
                elif part == 3:
                    inverse(rs_e, sd_e, TG, m_sd, n, m_rs)
                    scale_rows(ye, ye, rs_e, TG, m_yn)
                elif part == 4:
                    dve.wait_ge(m_tt, n)
                    if l == 0:
                        dve.wait_ge(st_z, 16 * i)
                    leaky(fo[:, :], mean[:, :], m_tt, n, m_z)
                elif part == 5:
                    dve.wait_ge(m_back, i + 1)
                    dve.wait_ge(d_x[q], 16 * (k + 1 + 2 * slot_base(q)))
                    dve.wait_ge(st_out, 16 * TG * i)
                    v.tensor_tensor(x1e[:, :, :], xd[:, q, 0:TG, :], bZ[0:P, :].rearrange("p (t f) -> p t f", f=D),
                                    ALU.add).then_inc(m_out, 1)

            def pass_b(i, k, q):
                n = i + 1
                dense(0, n, k, q, PASS_B)
                dense(1, n, k, q, PASS_B)
                dense(2, n, k, q, PASS_B)
                dense(3, n, k, q, PASS_B)
                edges(0, n, i, k, q, 0)
                edges(1, n, i, k, q, 0)
                dense(4, n, k, q, PASS_B)
                edges(2, n, i, k, q, 0)
                dense(5, n, k, q, PASS_B)
                edges(3, n, i, k, q, 0)
                dense(6, n, k, q, PASS_B)
                edges(4, n, i, k, q, 0)
                dense(7, n, k, q, PASS_B)
                dense(8, n, k, q, PASS_B)

            in_pairs(dve, pass_b)
            dve.wait_ge(st_z, 16 * NG)
            dve.wait_ge(st_x1, 16 * NG)

            def pass_c(i, k, q):
                for part in range(6):
                    edges(part, i + 1 + NG, i, k, q, 1)

            in_pairs(dve, pass_c)


_DRAM_INS = ["x", "src", "dst_ext", "dst_both", "et_both", "et5", "w0", "b0", "v1", "comp1", "root1", "bias1", "g1",
             "be1", "v2", "comp2", "root2", "bias2", "g2", "be2"]


def kernel(x, src, dst, edge_type_16, edge_type_5, L0_gnn_Ws, L0_gnn_bs, L1_gnn_weight1, L1_gnn_comp1,
           L1_gnn_root1, L1_gnn_bias1, L1_gnn_ln1_g, L1_gnn_ln1_b, L1_gnn_weight2, L1_gnn_comp2,
           L1_gnn_root2, L1_gnn_bias2, L1_gnn_ln2_g, L1_gnn_ln2_b):
    import numpy as np
    import concourse.bacc as bacc
    from concourse.bass_utils import run_bass_kernel_spmd

    dst, et16 = np.asarray(dst), np.asarray(edge_type_16)
    edge = np.full(1, -1, dst.dtype)
    arrays = {
        "x": x, "src": src,
        "dst_ext": np.concatenate([edge, dst, edge]),
        "dst_both": np.stack([np.concatenate([edge, dst]), np.concatenate([edge, dst[::-1]])]),
        "et_both": np.stack([et16, et16[::-1]]),
        "et5": edge_type_5, "w0": L0_gnn_Ws, "b0": L0_gnn_bs,
        "v1": L1_gnn_weight1, "comp1": L1_gnn_comp1, "root1": L1_gnn_root1, "bias1": L1_gnn_bias1,
        "g1": L1_gnn_ln1_g, "be1": L1_gnn_ln1_b,
        "v2": L1_gnn_weight2, "comp2": L1_gnn_comp2, "root2": L1_gnn_root2, "bias2": L1_gnn_bias2,
        "g2": L1_gnn_ln2_g, "be2": L1_gnn_ln2_b,
    }
    nc = bacc.Bacc("TRN2", target_bir_lowering=False, num_devices=1)
    feed, args = {}, []
    for name in _DRAM_INS:
        a = np.ascontiguousarray(arrays[name])
        feed[f"in_{name}"] = a
        args.append(nc.dram_tensor(f"in_{name}", a.shape, mybir.dt.from_np(a.dtype), kind="ExternalInput").ap())
    out = nc.dram_tensor("out", (N, D), F32, kind="ExternalOutput").ap()
    gnn_kernel(nc, *args, out)
    r = run_bass_kernel_spmd(nc, [feed], core_ids=[0])
    return r.results[0]["out"]
```

```python
from contextlib import ExitStack

import concourse.bass as bass
from concourse import mybir

ALU = mybir.AluOpType
ACT = mybir.ActivationFunctionType
AX = mybir.AxisListType
F32 = mybir.dt.float32
BF16 = mybir.dt.bfloat16
I32 = mybir.dt.int32

N = 50000
E = 12500
D = 128
R1 = 16
B1 = 8
HEAD = 32
P = 125
TG = 4
NT = E // P
NG = NT // TG
GE = TG * P
NI = N // GE
LOB = 256
HIC = 98
BLK = 4
EPS = 1e-5
SLOPE = 0.1
NQ = 4
SRC_, DST_, OUT_ = 0, 1, 2


def gnn_kernel(nc, x, src, dst_ext, dst_both, et_both, et5, w0, b0, v1, comp1, root1, bias1, g1, be1,
               v2, comp2, root2, bias2, g2, be2, out):
    ctx = ExitStack()
    with ctx:
        def sb(name, shape, dt=F32):
            return ctx.enter_context(nc.sbuf_tensor(name, shape, dt))

        def sem(name):
            return ctx.enter_context(nc.semaphore(name))

        def dram(name, shape, dt=F32):
            return nc.dram_tensor(name, shape, dt).ap()

        tab1 = dram("tab1", [2 * E, D])
        tab2 = dram("tab2", [2 * E, D])
        x1_dram = dram("x1_dram", [E, D])
        own1_dram = dram("own1_dram", [D, E])
        own2_dram = dram("own2_dram", [D, E])

        ident = sb("ident", [128, 128])
        identb = sb("identb", [128, 128], BF16)
        anti = sb("anti", [128, 128])
        sel = sb("sel", [48, R1, 128], BF16)
        ones = sb("ones", [128, 128])
        onesb = sb("onesb", [128, 128], BF16)
        zerob = sb("zerob", [128, LOB], BF16)
        iota_lo = sb("iota_lo", [P, LOB])
        relno = sb("relno", [64, 1])
        rowno = sb("rowno", [P, 1])
        tileno = sb("tileno", [P, NT])
        slotno = sb("slotno", [P, NT])
        blockno = sb("blockno", [128, 1])
        epst = sb("epst", [128, 1])

        wt = sb("wt", [128, 2, 9, 128])
        wsum = sb("wsum", [128, 18])
        w0t = sb("w0t", [128, 4 * HEAD])
        b0t = sb("b0t", [128, 1])
        ln = sb("ln", [128, 4])
        brow = sb("brow", [96, 2, 128])
        bsum = sb("bsum", [96, 2])
        bpart = sb("bpart", [96, 2, 128], BF16)
        bias = sb("bias", [96, 2, TG, 128], BF16)
        compt = sb("compt", [32, 2 * B1])

        raw = sb("raw", [NT, 3, P], I32)
        rawf = sb("rawf", [NT, 3, P])
        part = sb("part", [NT, 4, P], I32)
        turn = sb("turn", [NT, 7, P])
        lastf = sb("lastf", [NT, P])
        gidx = sb("gidx", [P, NG, 2 * TG], I32)
        sidx = sb("sidx", [P, NG, TG], I32)
        tidx = sb("tidx", [P, NG, TG], I32)
        meta = sb("meta", [P, NG, 6 * TG])
        metat = sb("metat", [P, 6 * TG])
        found = sb("found", [P, NT])
        foundi = sb("foundi", [P, NT], I32)
        hit = sb("hit", [P, NT])
        slotf = sb("slotf", [P, NT])
        res = sb("res", [P, TG])
        hot_hi = sb("hot_hi", [P, TG, 2 * HIC], BF16)
        hot_lo = sb("hot_lo", [P, 2, TG, LOB], BF16)
        hot_hit = sb("hot_hit", [HIC, TG * 2, 128], BF16)
        node_tab = sb("node_tab", [HIC, 2, 2, LOB], BF16)
        junk = sb("junk", [P, TG, LOB], BF16)

        dstb = sb("dstb", [128, 2, GE + 1], I32)
        et5b = sb("et5b", [128, 2, GE], I32)
        dstc, etc = dstb[0:64, :, :], et5b[0:64, :, :]
        scaled = sb("scaled", [128, NQ, GE])
        contc, hotc, runc, prodc = (scaled[0:64, m, :] for m in range(4))
        carryc = sb("carryc", [64, 1])
        first16 = sb("first16", [32, 1])
        cnt_f = sb("cnt_f", [P, NT])
        cnt_b = sb("cnt_b", [P, NT])
        rdeg = sb("rdeg", [P, NT, BLK])
        coef = sb("coef", [P, NT, R1])
        coef3 = sb("coef3", [P, NT, 48], BF16)
        coef3g = sb("coef3g", [P, TG, 48], BF16)
        coeft = sb("coeft", [48, E], BF16)
        cont = sb("cont", [128, E], BF16)

        xin = sb("xin", [P, 2, TG, D])
        outr = sb("outr", [P, 2, TG, D])
        nd = sb("nd", [P, TG, D])
        fd = sb("fd", [128, GE])
        zd = sb("zd", [128, 2, GE])
        nd2 = sb("nd2", [P, TG, D])
        fd2 = sb("fd2", [128, GE])
        zd2 = sb("zd2", [128, GE])
        sq_d = sb("sq_d", [P, TG, D], BF16)
        sq_d2 = sb("sq_d2", [P, TG, D], BF16)
        st_d = sb("st_d", [P, TG, 6])
        mv_d = sb("mv_d", [P, 6, TG])
        mv_d2 = sb("mv_d2", [P, 6, TG])

        gat = sb("gat", [P, 2, 2 * TG, D])
        nowidx = sb("nowidx", [P, 2, 2 * TG], I32)
        nowout = sb("nowout", [P, TG], I32)
        ne = sb("ne", [P, TG, D])
        fe = sb("fe", [128, 2, GE])
        te = sb("te", [128, GE])
        ye = sb("ye", [P, TG, D])
        mask = sb("mask", [128, GE])
        msg = sb("msg", [128, GE])
        agg = sb("agg", [128, 2, GE])
        mean = sb("mean", [P, TG, D])
        carry = sb("carry", [128, 3])
        x1e = sb("x1e", [P, TG, D])
        x1b = sb("x1b", [P, 2, TG, D])
        ne2 = sb("ne2", [P, TG, D])
        own = sb("own", [128, 2, GE])
        te2 = sb("te2", [128, GE])
        fo = sb("fo", [128, GE])
        sq_e = sb("sq_e", [P, TG, D], BF16)
        st_e = sb("st_e", [P, TG, 6])
        st_t = sb("st_t", [P, TG, 6])
        mv_s = sb("mv_s", [P, 6, TG])
        mv_y = sb("mv_y", [P, 6, TG])
        mv_t = sb("mv_t", [P, 6, TG])

        bank = [ctx.enter_context(nc.psum_tensor(f"bank{i}", [128, 512], F32)) for i in range(8)]
        D1, D2, E1, E2 = bank[0:4]
        rows4 = lambda b: b[0:P, :].rearrange("p (t f) -> p t f", f=D)

        ld_idx, ld_w = sem("ld_idx"), sem("ld_w")
        ld_cnt = [sem("ld_cnt0"), sem("ld_cnt1")]
        pool_const, dve_const = sem("pool_const"), sem("dve_const")
        prep = sem("prep")
        w_ready = sem("w_ready")
        idx_split, idx_turned, idx_ready = sem("idx_split"), sem("idx_turned"), sem("idx_ready")
        cnt_hot, cnt_run, cnt_prods, cnt_summed, cnt_saved, cnt_carry = (
            sem("cnt_hot"), sem("cnt_run"), sem("cnt_prods"), sem("cnt_summed"), sem("cnt_saved"), sem("cnt_carry"))
        cnt_flipped = sem("cnt_flipped")
        coef_now, coef_turned, coef_ready = sem("coef_now"), sem("coef_turned"), sem("coef_ready")
        meta_now, tab_hot, tab_added, tab_sum, tab_ready = (
            sem("meta_now"), sem("tab_hot"), sem("tab_added"), sem("tab_sum"), sem("tab_ready"))
        hot_ready, hot_turned, hot_saved, looked, looked_used, found_now = (
            sem("hot_ready"), sem("hot_turned"), sem("hot_saved"), sem("looked"), sem("looked_used"), sem("found_now"))
        slots_ready = sem("slots_ready")

        d_x = [sem("d_x0"), sem("d_x1")]
        d_copied = sem("d_copied")
        d_stats, d_var, d_sd, d_rs, d_norm = (sem("d_stats"), sem("d_var"), sem("d_sd"), sem("d_rs"), sem("d_norm"))
        d_hT, d_h, d_y = sem("d_hT"), sem("d_h"), sem("d_y")
        d_sq, d_sd1, d_rs1, d_yn = sem("d_sq"), sem("d_sd1"), sem("d_rs1"), sem("d_yn")
        d_ynT, d_t, d_z = sem("d_ynT"), sem("d_t"), sem("d_z")
        d_y2, d_sq2, d_sd2, d_rs2, d_yn2 = (sem("d_y2"), sem("d_sq2"), sem("d_sd2"), sem("d_rs2"), sem("d_yn2"))
        d_yn2T, d_t2, d_z2, d_back, d_out = sem("d_yn2T"), sem("d_t2"), sem("d_z2"), sem("d_back"), sem("d_out")
        d_st = [sem("d_st0"), sem("d_st1")]

        now_ready = sem("now_ready")
        g_s = [sem("g_s0"), sem("g_s1")]
        g_d = [sem("g_d0"), sem("g_d1")]
        ld_e = [sem("ld_e0"), sem("ld_e1")]
        ld_x1 = [sem("ld_x10"), sem("ld_x11")]
        s_stats, s_var, s_sd, s_rs = sem("s_stats"), sem("s_var"), sem("s_sd"), sem("s_rs")
        s_norm = [sem("s_norm0"), sem("s_norm1")]
        t_x1 = [sem("t_x10"), sem("t_x11")]
        s_hT, s_h, s_m0, s_y = sem("s_hT"), sem("s_h"), sem("s_m0"), sem("s_y")
        s_sq, s_sd1, s_rs1, s_yn = sem("s_sq"), sem("s_sd1"), sem("s_rs1"), sem("s_yn")
        cont_ready, msg_ready, agg_ready, agg_T, carried, t_mean = (
            sem("cont_ready"), sem("msg_ready"), sem("agg_ready"), sem("agg_T"), sem("carried"), sem("t_mean"))
        t_stats, t_var, t_sd, t_rs, t_norm, t_hT, t_h = (
            sem("t_stats"), sem("t_var"), sem("t_sd"), sem("t_rs"), sem("t_norm"), sem("t_hT"), sem("t_h"))
        st_ns, st_nt, st_x1, st_h, st_zs = sem("st_ns"), sem("st_nt"), sem("st_x1"), sem("st_h"), sem("st_zs")

        m_gT = [sem("m_gT0"), sem("m_gT1")]
        m_t, m_g = sem("m_t"), sem("m_g")
        m_bc, m_sc, m_mm = sem("m_bc"), sem("m_sc"), sem("m_mm")
        m_agg, m_y, m_sq, m_sd, m_rs, m_yn = (
            sem("m_agg"), sem("m_y"), sem("m_sq"), sem("m_sd"), sem("m_rs"), sem("m_yn"))
        m_ynT, m_tt, m_z, m_back, m_out = sem("m_ynT"), sem("m_tt"), sem("m_z"), sem("m_back"), sem("m_out")
        out_now = sem("out_now")
        st_zn, st_z, st_out = sem("st_zn"), sem("st_z"), sem("st_out")

        block = ctx.enter_context(nc.Block())

        def each_group(eng, body, tail=1):
            body(0, 0, 0)
            body(1, 0, 1)
            with eng.Fori(1, (NG - tail) // 2) as k:
                body(k * 2, k, 0)
                body(k * 2 + 1, k, 1)
            for i in range(NG - tail, NG):
                body(i, i // 2, i % 2)

        def is_last(i):
            return type(i) is int and i == NG - 1

        def reuse(eng, s, n):
            if type(n) is not int or n > 0:
                eng.wait_ge(s, n)

        def counted(eng, reg):
            eng.reg_add(reg, reg, 1)
            return eng.snap(reg)

        def column(ap, i):
            return ap[:, i, :] if type(i) is int else ap[:, bass.ds(i, 1), :].squeeze(1)

        def grp(ap, i, n):
            return ap[:, bass.ds(i * n, n)]

        def rows_of(t, r0, i):
            return t[bass.ds(i * GE + r0, GE), :].rearrange("(t p) f -> p t f", p=P)

        def dense_rows(t, n):
            return t[bass.ds(n * GE, GE), :].rearrange("(p t) f -> p t f", p=P)

        def steps_p(i, k, q):
            return [((i, k, q), (i + 1, k + q, 1 - q))]

        def steps_a(i, k, q):
            n = i * 2 + NG
            h = i + NG // 2
            return [((n, h, 1), (n + 1, h + 1, 0)), ((n + 1, h + 1, 0), (n + 2, h + 1, 1))]

        def steps_b(i, k, q):
            n = i + 3 * NG
            h = 3 * NG // 2
            now = (n, k + (h + q), 1 - q)
            return [(now, None if is_last(i) else (n + 1, k + (h + 1), q))]

        def ahead(i, k, q):
            return None if is_last(i) else (i + 1, k + q, 1 - q)

        def uses(q):
            return (NG + 1) // 2 if q == 0 else NG // 2

        def merged(*streams):
            at = [((j + 0.5) / len(s), n, x) for n, s in enumerate(streams) for j, x in enumerate(s)]
            return [x for _, _, x in sorted(at, key=lambda a: a[:2])]

        def stream(kind, n, sub=0):
            return [(kind, j, sub) for j in range(n)]

        ORDER_P = merged(stream("D", 9), stream("F", 8), stream("T", 4), stream("C", 5))
        ORDER_A = merged(stream("D", 9) + stream("D", 9, 1), stream("F", 8) + stream("F", 8, 1), stream("E", 16),
                         stream("L", 5), stream("K", 3))
        ORDER_B = merged(stream("D", 9), stream("F", 8), stream("M", 3 + B1 + NQ), stream("U", 8))
        ORDER_C = merged(stream("M", 3 + B1 + NQ), stream("U", 8))

        @block.sync
        def _(sp):
            sp.dma_start(raw[:, SRC_, :], src.rearrange("(t p) -> t p", p=P)).then_inc(ld_idx, 16)
            sp.dma_start(raw[:, DST_, :], dst_ext[1:1 + E].rearrange("(t p) -> t p", p=P)).then_inc(ld_idx, 16)
            sp.dma_start(raw[:, OUT_, :], dst_ext[2:2 + E].rearrange("(t p) -> t p", p=P)).then_inc(ld_idx, 16)

            def load_x(item):
                n, _, par = item
                sp.dma_start(xin[:, par, :, :], dense_rows(x, n)).then_inc(d_x[par], 16)

            def store_out(item):
                n, _, par = item
                sp.wait_ge(d_out, n + 1)
                sp.dma_start(dense_rows(out, n), outr[:, par, :, :]).then_inc(d_st[par], 16)

            load_x((0, 0, 0))
            load_x((1, 0, 1))
            for l, (root, v) in enumerate(((root1, v1), (root2, v2))):
                sp.dma_start(wt[:, l, 0, :], root).then_inc(ld_w, 16)
                sp.dma_start(wt[:, l, 1:9, :], v.rearrange("b i o -> i b o")).then_inc(ld_w, 16)
            for l, (b, g, be, comp) in enumerate(((bias1, g1, be1, comp1), (bias2, g2, be2, comp2))):
                sp.dma_start(brow[:, l, :], b.partition_broadcast(96)).then_inc(ld_w, 16)
                sp.dma_start(ln[:, 2 * l:2 * l + 1], g.unsqueeze(1)).then_inc(ld_w, 16)
                sp.dma_start(ln[:, 2 * l + 1:2 * l + 2], be.unsqueeze(1)).then_inc(ld_w, 16)
                sp.wait_ge(dve_const, 1)
                sp.dma_start(compt[0:R1, l * B1:(l + 1) * B1], comp).then_inc(ld_w, 16)
            sp.dma_start(w0t[:, :].rearrange("i (r o) -> i r o", r=4),
                         w0[0:4, :, 0:HEAD].rearrange("r i o -> i r o")).then_inc(ld_w, 16)
            for r in range(4):
                sp.dma_start(b0t[r * HEAD:(r + 1) * HEAD, :], b0[r, 0:HEAD].unsqueeze(1)).then_inc(ld_w, 16)

            def next_x(item):
                n, h, par = item
                sp.wait_ge(d_norm, n + 1)
                sp.wait_ge(d_copied, n + 1)
                load_x((n + 2, h + 1, par))

            def load_count(i, q):
                for h in range(2):
                    sp.dma_start(dstc[32 * h:32 * h + 32, q, :],
                                 dst_both[h, bass.ds(i * GE, GE + 1)].partition_broadcast(32)).then_inc(ld_cnt[q], 16)
                sp.dma_start(etc[0:R1, q, :], et_both[0, bass.ds(i * GE, GE)].partition_broadcast(R1)).then_inc(ld_cnt[q], 16)
                sp.dma_start(etc[R1:32, q, :], et5[bass.ds(i * GE, GE)].partition_broadcast(32 - R1)).then_inc(ld_cnt[q], 16)
                sp.dma_start(etc[32:64, q, :], et_both[1, bass.ds(i * GE, GE)].partition_broadcast(32)).then_inc(ld_cnt[q], 16)

            load_count(0, 0)

            def pass_p(i, k, q):
                if not is_last(i):
                    sp.wait_ge(dve_const, 1)
                    reuse(sp, cnt_hot, i)
                    load_count(i + 1, 1 - q)
                for now, _ in steps_p(i, k, q):
                    next_x(now)
                    store_out(now)

            each_group(sp, pass_p)

            def load_edges(i, q):
                sp.dma_start(dstb[:, q, :], dst_ext[bass.ds(i * GE, GE + 1)].partition_broadcast(128)).then_inc(ld_e[q], 16)
                sp.dma_start(et5b[:, q, :], et5[bass.ds(i * GE, GE)].partition_broadcast(128)).then_inc(ld_e[q], 16)

            sp.wait_ge(cnt_hot, NG)
            load_edges(0, 0)

            def pass_a(i, k, q):
                if not is_last(i):
                    reuse(sp, cont_ready, i)
                    load_edges(i + 1, 1 - q)
                (now, _), (then, _) = steps_a(i, k, q)
                next_x(now)
                sp.wait_ge(s_norm[q], k + 1)
                sp.dma_start(rows_of(tab1, E, i), ne[:, :, :]).then_inc(st_ns, 16)
                store_out(now)
                next_x(then)
                sp.wait_ge(s_yn, i + 1)
                sp.dma_start(rows_of(tab2, E, i), ye[:, :, :]).then_inc(st_zs, 16)
                sp.wait_ge(t_x1[q], k + 1)
                sp.dma_start(rows_of(x1_dram, 0, i), x1e[:, :, :]).then_inc(st_x1, 16)
                sp.wait_ge(t_norm, i + 1)
                sp.dma_start(rows_of(tab1, 0, i), ne2[:, :, :]).then_inc(st_nt, 16)
                sp.wait_ge(dve_const, 1)
                sp.wait_ge(t_h, i + 1)
                sp.dma_start(grp(own1_dram, i, GE), fo[:, :]).then_inc(st_h, 16)
                store_out(then)

            each_group(sp, pass_a)

            def load_own(dr, i, q):
                sp.dma_start(own[:, q, :], grp(dr, i, GE)).then_inc(ld_e[q], 16)

            sp.wait_ge(st_h, 16 * NG)
            load_own(own1_dram, 0, 0)

            def pass_b(i, k, q):
                if not is_last(i):
                    reuse(sp, m_y, i)
                    load_own(own1_dram, i + 1, 1 - q)
                ((now, _),) = steps_b(i, k, q)
                if not (type(i) is int and i >= NG - 2):
                    next_x(now)
                sp.wait_ge(m_yn, i + 1)
                sp.dma_start(rows_of(tab2, 0, i), ye[:, :, :]).then_inc(st_zn, 16)
                sp.wait_ge(dve_const, 1)
                sp.wait_ge(m_z, i + 1)
                sp.dma_start(grp(own2_dram, i, GE), fo[:, :]).then_inc(st_z, 16)
                store_out(now)

            each_group(sp, pass_b, 3)

            def load_x1(i, q):
                sp.dma_start(x1b[:, q, :, :], rows_of(x1_dram, 0, i)).then_inc(ld_x1[q], 16)

            sp.wait_ge(st_z, 16 * NG)
            sp.wait_ge(st_x1, 16 * NG)
            load_own(own2_dram, 0, 0)
            load_x1(0, 0)

            def pass_c(i, k, q):
                if not is_last(i):
                    sp.wait_ge(dve_const, 1)
                    sp.wait_ge(m_y, i + NG)
                    load_own(own2_dram, i + 1, 1 - q)
                    reuse(sp, m_out, i)
                    load_x1(i + 1, 1 - q)

            each_group(sp, pass_c)

        @block.gpsimd
        def _(pool):
            pool_reg = pool.alloc_register("pool_reg")
            pool.reg_mov(pool_reg, 0)
            pool.wait_ge(dve_const, 1)
            nc.gpsimd.affine_select(out=ident[:, :], in_=ident[:, :], compare_op=ALU.not_equal, fill=1.0,
                                    base=0, pattern=[[-1, 128]], channel_multiplier=1)
            nc.gpsimd.affine_select(out=identb[:, :], in_=identb[:, :], compare_op=ALU.not_equal, fill=1.0,
                                    base=0, pattern=[[-1, 128]], channel_multiplier=1)
            exact = dict(allow_small_or_imprecise_dtypes=True)
            nc.gpsimd.iota(iota_lo[:, :], [[1, LOB]], base=0, channel_multiplier=0, **exact)
            nc.gpsimd.iota(rowno[:, :], [[0, 1]], base=0, channel_multiplier=1, **exact)
            nc.gpsimd.iota(tileno[:, :], [[LOB // 2, NT]], base=LOB // 2, channel_multiplier=0, **exact)
            nc.gpsimd.iota(slotno[:, :], [[P, NT]], base=E, channel_multiplier=1, **exact)
            nc.gpsimd.iota(relno[:, :], [[0, 1]], base=0, channel_multiplier=1, **exact)
            nc.gpsimd.memset(epst[:, :], EPS)
            nc.gpsimd.affine_select(out=anti[:, :], in_=anti[:, :], compare_op=ALU.not_equal, fill=1.0,
                                    base=-(P - 1), pattern=[[1, 128]], channel_multiplier=1).then_inc(pool_const, 1)
            for m in range(3):
                if m:
                    pool.wait_ge(pool_const, m + 1)
                nc.gpsimd.affine_select(out=sel[:, :, :], in_=sel[:, :, :], compare_op=ALU.not_equal, fill=1.0,
                                        base=-R1 * m, pattern=[[-1, R1], [0, 128]], channel_multiplier=1
                                        ).then_inc(pool_const, 1)

            def now(i, q, ap, c0, n):
                copies = counted(pool, pool_reg)
                nc.gpsimd.tensor_copy(nowidx[:, q, c0:c0 + n], column(ap, i)).then_inc(now_ready, 1)
                return copies

            def gather_a(i, k, q):
                reuse(pool, g_d[q], 64 * k)
                pool.wait_ge(idx_ready, 1)
                copies = now(i, q, gidx, 0, 2 * TG)
                pool.wait_ge(idx_split, 1)
                reuse(pool, s_norm[q], k)
                reuse(pool, t_x1[q], k)
                pool.wait_ge(now_ready, copies)
                for j in range(2 * TG):
                    pool.indirect_dma_start(
                        out=gat[:, q, j, :], out_offset=None, in_=x,
                        in_offset=bass.IndirectOffsetOnAxis(ap=nowidx[:, q, j:j + 1], axis=0),
                    ).then_inc((g_s if j < TG else g_d)[q], 16)

            each_group(pool, gather_a)

            def gather_m(tab, i, k, q, l):
                reuse(pool, m_gT[q], k + (uses(q) if l else 0))
                pool.wait_ge(slots_ready, 1)
                copies = now(i, q, sidx, 0, TG)
                pool.wait_ge(idx_split, 1)
                pool.wait_ge(now_ready, copies)
                for j in range(TG):
                    pool.indirect_dma_start(
                        out=gat[:, q, j, :], out_offset=None, in_=tab,
                        in_offset=bass.IndirectOffsetOnAxis(ap=nowidx[:, q, j:j + 1], axis=0),
                    ).then_inc(g_s[q], 16)

            pool.wait_ge(st_ns, 16 * NG)
            pool.wait_ge(st_nt, 16 * NG)
            pool.wait_ge(t_x1[0], uses(0))
            pool.wait_ge(t_x1[1], uses(1))
            each_group(pool, lambda i, k, q: gather_m(tab1, i, k, q, 0))
            pool.wait_ge(st_zs, 16 * NG)
            pool.wait_ge(st_zn, 16 * NG)

            def scatter(i):
                reuse(pool, st_out, 16 * TG * i)
                pool.wait_ge(slots_ready, 1)
                nc.gpsimd.tensor_copy(nowout[:, :], column(tidx, i)).then_inc(out_now, 1)
                pool.wait_ge(slots_ready, 1)
                pool.wait_ge(out_now, i + 1)
                pool.wait_ge(m_out, i + 1)
                for j in range(TG):
                    pool.indirect_dma_start(
                        out=out, out_offset=bass.IndirectOffsetOnAxis(ap=nowout[:, j:j + 1], axis=0),
                        in_=x1e[:, j, :], in_offset=None, bounds_check=N - 1, oob_is_err=False,
                    ).then_inc(st_out, 16)

            gather_m(tab2, 0, 0, 0, 1)
            for par in range(2):
                pool.wait_ge(d_st[par], 16 * (NI // 2))

            def pass_c(i, k, q):
                if not is_last(i):
                    gather_m(tab2, *ahead(i, k, q), 1)
                scatter(i)

            each_group(pool, pass_c)
            pool.wait_ge(st_out, 16 * TG * NG)

        @block.scalar
        def _(act):
            VAR, SUM, ROOT = 1, 3, 4

            def root_of(mv, row, ready, n, done):
                act.wait_ge(ready, n)
                nc.scalar.activation(mv[:, ROOT, :], mv[:, row, :], ACT.Sqrt, bias=epst[0:P, :],
                                     scale=1.0 / D).then_inc(done, 1)

            def squares(b, sq, mv, ready, n, summed, done):
                act.wait_ge(ready, n)
                for j in range(TG):
                    t = nc.scalar.activation(sq[:, j, :], b[0:P, j * D:(j + 1) * D], ACT.Square,
                                             accum_out=mv[:, SUM, j:j + 1])
                t.then_inc(summed, 1)
                root_of(mv, SUM, summed, n, done)

            def bring(dst, src_, ready, n, done, func):
                act.wait_ge(ready, n)
                nc.scalar.activation(dst, src_, func).then_inc(done, 1)

            def affine(dst, src_, l, ready, n, done):
                act.wait_ge(ready, n)
                nc.scalar.activation(dst, src_, ACT.Identity, bias=ln[:, 2 * l + 1:2 * l + 2],
                                     scale=ln[:, 2 * l:2 * l + 1]).then_inc(done, 1)

            def first(j, item):
                n, h, par = item
                n = n + 1
                if j == 1:
                    root_of(mv_d, VAR, d_var, n, d_sd)
                elif j == 2:
                    reuse(act, d_st[par], h * 16)
                    act.wait_ge(d_x[par], (h + 1) * 16)
                    nc.scalar.activation(outr[:, par, :, :], xin[:, par, :, :], ACT.Copy).then_inc(d_copied, 1)
                elif j == 4:
                    bring(fd[:, :], D1[:, 0:GE], d_hT, n, d_h, ACT.Relu)
                elif j == 6:
                    squares(D1, sq_d, mv_d, d_y, n, d_sq, d_sd1)
                elif j == 8:
                    affine(fd[:, :], D1[:, 0:GE], 0, d_ynT, n, d_t)

            def second(j, item):
                n, _, _ = item
                n = n + 1
                if j == 1:
                    squares(D2, sq_d2, mv_d2, d_y2, n, d_sq2, d_sd2)
                elif j == 4:
                    affine(fd2[:, :], D2[:, 0:GE], 1, d_yn2T, n, d_t2)

            act.wait_ge(pool_const, 4)
            act.wait_ge(ld_w, 16 * 17)
            for j in range(9):
                first(j, (0, 0, 0))

            def dense(x_, steps):
                kind, j, sub = x_
                now, then = steps[sub]
                if kind == "F":
                    second(j, now)
                elif then is not None:
                    first(j, then)

            def pass_p(i, k, q):
                for x_ in ORDER_P:
                    if x_[0] in "DF":
                        dense(x_, steps_p(i, k, q))

            each_group(act, pass_p)

            def pass_a(i, k, q):
                n = i + 1
                for x_ in ORDER_A:
                    kind, j, _ = x_
                    if kind in "DF":
                        dense(x_, steps_a(i, k, q))
                    elif (kind, j) == ("E", 1):
                        root_of(mv_s, VAR, s_var, n, s_sd)
                    elif (kind, j) == ("E", 4):
                        bring(fe[:, 0, :], E1[:, 0:GE], s_hT, n, s_h, ACT.Relu)
                    elif (kind, j) == ("E", 8):
                        squares(E1, sq_e, mv_y, s_y, n, s_sq, s_sd1)
                    elif (kind, j) == ("E", 12):
                        root_of(mv_t, VAR, t_var, n, t_sd)
                    elif (kind, j) == ("E", 15):
                        reuse(act, st_h, 16 * i)
                        bring(fo[:, :], E2[:, 0:GE], t_hT, n, t_h, ACT.Relu)
                    elif (kind, j) == ("L", 2):
                        bring(hot_hit[:, :, 0:P],
                              bank[4][0:HIC, :].bitcast(BF16).rearrange("p (c e) -> p c e", e=128)[:, :, 0:P],
                              hot_turned, n, hot_saved, ACT.Copy)
                    elif (kind, j) == ("K", 2):
                        bring(grp(coeft, i, GE).rearrange("p (t e) -> p t e", e=P),
                              bank[7][0:48, :].bitcast(BF16).rearrange("p (t e) -> p t e", e=128)[:, 0:TG, 0:P],
                              coef_turned, n, coef_ready, ACT.Copy)

            each_group(act, pass_a)
            act.wait_ge(st_h, 16 * NG)

            def messages(x_, group, l):
                if group is None:
                    return
                i, k, q = group
                if x_[1] == 1:
                    n = k + 1 + l * uses(q)
                    if l == 0:
                        reuse(act, m_mm, B1 * (i - 1))
                        bring(fe[:, q, :], E1[:, 0:GE], m_gT[q], n, m_g, ACT.Relu)
                    else:
                        affine(te[:, :], E1[:, 0:GE], 0, m_gT[q], n, m_t)

            def edge_rows(x_, i, l):
                j, n = x_[1], i + 1 + l * NG
                if j == 1:
                    squares(E2, sq_e, mv_y, m_y, n, m_sq, m_sd)
                elif j == 4:
                    affine(te2[:, :], E2[:, 0:GE], l, m_ynT, n, m_tt)

            def two_halves(order, l):
                messages(("M", 1, 0), (0, 0, 0), l)

                def one(i, k, q):
                    for x_ in order:
                        if x_[0] in "DF":
                            dense(x_, steps_b(i, k, q))
                        elif x_[0] == "M":
                            messages(x_, ahead(i, k, q), l)
                        elif x_[0] == "U":
                            edge_rows(x_, i, l)
                each_group(act, one)

            two_halves(ORDER_B, 0)
            two_halves(ORDER_C, 1)

        @block.tensor
        def _(pe):
            pe_reg = pe.alloc_register("pe_reg")
            pe.reg_mov(pe_reg, 0)
            pe.wait_ge(pool_const, 4)
            pe.wait_ge(idx_split, 1)
            for m in range(7):
                t = nc.tensor.transpose(bank[2 + m // 4][0:P, (m % 4) * 128:(m % 4) * 128 + NT], turn[:, m, :],
                                        ident[0:NT, 0:NT])
            t.then_inc(idx_turned, 1)

            def turn_rows(b, rows):
                for j in range(TG):
                    t = nc.tensor.transpose(b[:, j * P:(j + 1) * P], rows[:, j, :], ident[0:P, 0:P])
                return t

            def turn_back(b, cols):
                for j in range(TG):
                    t = nc.tensor.transpose(b[0:P, j * D:(j + 1) * D], cols[:, j * P:(j + 1) * P], ident[:, :])
                return t

            def rows_out(b, cols, l, more=None):
                nc.tensor.matmul(b[0:P, :], onesb[0:96, 0:P], bias[:, l, :, :].rearrange("p t f -> p (t f)"),
                                 start=True, stop=False)
                for j in range(TG):
                    e = slice(j * P, (j + 1) * P)
                    o = b[0:P, j * D:(j + 1) * D]
                    last = j == TG - 1
                    t = nc.tensor.matmul(o, cols[:, e], wt[:, l, 0, :], start=False, stop=last and more is None)
                    if more is not None:
                        t = nc.tensor.matmul(o, more[:, e], ident[:, :], start=False, stop=last)
                return t

            def first(j, item):
                n, _, par = item
                n = n + 1
                if j == 3:
                    pe.wait_ge(d_norm, n)
                    reuse(pe, d_t, n - 1)
                    turn_rows(D1, nd).then_inc(d_hT, 1)
                elif j == 5:
                    pe.wait_ge(d_h, n)
                    rows_out(D1, fd, 0).then_inc(d_y, 1)
                elif j == 7:
                    pe.wait_ge(d_yn, n)
                    turn_rows(D1, nd).then_inc(d_ynT, 1)

            def second(j, item):
                n, _, par = item
                n = n + 1
                if j == 0:
                    pe.wait_ge(d_z, n)
                    reuse(pe, d_out, n - 1)
                    rows_out(D2, zd[:, par, :], 1).then_inc(d_y2, 1)
                elif j == 3:
                    pe.wait_ge(d_yn2, n)
                    turn_rows(D2, nd2).then_inc(d_yn2T, 1)
                elif j == 6:
                    pe.wait_ge(d_z2, n)
                    turn_back(D2, zd2).then_inc(d_back, 1)

            def dense(x_, steps):
                kind, j, sub = x_
                now, then = steps[sub]
                if kind == "F":
                    second(j, now)
                elif then is not None:
                    first(j, then)

            pe.wait_ge(w_ready, 1)
            for j in range(9):
                first(j, (0, 0, 0))

            def table_zero(**flags):
                for b in range(4):
                    t = nc.tensor.matmul(bank[4 + b][0:HIC, 0:LOB], zerob[0:P, 0:HIC], zerob[0:P, :], **flags)
                return t

            table_zero(start=True, stop=False)

            def pass_p(i, k, q):
                for x_ in ORDER_P:
                    kind, j, _ = x_
                    if kind in "DF":
                        dense(x_, steps_p(i, k, q))
                    elif (kind, j) == ("T", 2):
                        pe.wait_ge(tab_hot, i + 1)
                        for t_ in range(TG):
                            for v in range(2):
                                for c in range(2):
                                    t = nc.tensor.matmul(bank[4 + 2 * v + c][0:HIC, 0:LOB],
                                                         hot_hi[:, t_, c * HIC:(c + 1) * HIC],
                                                         hot_lo[:, v, t_, :], start=False, stop=False)
                        t.then_inc(tab_added, 1)
                    elif (kind, j) == ("C", 3):
                        pe.wait_ge(cnt_prods, i + 1)
                        reuse(pe, cnt_saved, i)
                        for t_ in range(TG):
                            e = slice(t_ * P, (t_ + 1) * P)
                            c = lambda b, w: E1[0:P, b + t_ * w:b + (t_ + 1) * w]
                            nc.tensor.matmul(c(0, 1), prodc[0:32, e], first16[:, :], start=True, stop=True)
                            nc.tensor.matmul(c(16, BLK), runc[0:32, e], ident[0:32, R1:R1 + BLK], start=True, stop=True)
                            nc.tensor.matmul(c(64, R1), hotc[0:32, e], compt[:, :], start=True, stop=True)
                        for t_ in range(TG):
                            e = slice(t_ * P, (t_ + 1) * P)
                            t = nc.tensor.matmul(E2[0:P, TG - 1 - t_:TG - t_], prodc[32:64, e], ones[32:64, 0:1],
                                                 start=True, stop=True)
                        t.then_inc(cnt_summed, 1)

            each_group(pe, pass_p)
            table_zero(start=False, stop=True).then_inc(tab_sum, 1)
            pe.wait_ge(cnt_saved, NG)
            nc.tensor.matmul(E1[0:P, 0:NT], anti[0:P, 0:P], cnt_b[:, :], start=True, stop=True).then_inc(cnt_flipped, 1)
            pe.wait_ge(tab_ready, 1)

            def pass_a(i, k, q):
                n = i + 1
                for x_ in ORDER_A:
                    kind, j, _ = x_
                    if kind in "DF":
                        dense(x_, steps_a(i, k, q))
                    elif (kind, j) == ("E", 3):
                        pe.wait_ge(s_norm[q], k + 1)
                        reuse(pe, s_yn, i)
                        turn_rows(E1, ne).then_inc(s_hT, 1)
                    elif (kind, j) == ("E", 5):
                        pe.wait_ge(s_h, n)
                        reuse(pe, t_h, i)
                        nc.tensor.matmul(E2[:, 0:GE], w0t[:, :], fe[:, 0, :], start=True, stop=True).then_inc(s_m0, 1)
                        rows_out(E1, fe[:, 0, :], 0).then_inc(s_y, 1)
                    elif (kind, j) == ("E", 7):
                        pe.wait_ge(agg_ready, n)
                        turn_back(E2, agg[:, 0, :]).then_inc(agg_T, 1)
                    elif (kind, j) == ("E", 14):
                        pe.wait_ge(t_norm, n)
                        turn_rows(E2, ne2).then_inc(t_hT, 1)
                    elif (kind, j) == ("L", 1):
                        pe.wait_ge(hot_ready, n)
                        turned = bank[4][0:HIC, :].bitcast(BF16).rearrange("p (c e) -> p c e", e=128)
                        for t_ in range(TG):
                            for c in range(2):
                                t = nc.tensor.transpose(turned[:, 2 * t_ + c, 0:P],
                                                        hot_hi[:, t_, c * HIC:(c + 1) * HIC], identb[0:P, 0:P])
                        t.then_inc(hot_turned, 1)
                    elif (kind, j) == ("L", 3):
                        pe.wait_ge(hot_saved, n)
                        reuse(pe, looked_used, i)
                        for t_ in range(TG):
                            b = bank[5 + t_ // 2][0:P, (t_ % 2) * LOB:(t_ % 2 + 1) * LOB]
                            for c in range(2):
                                for v in range(2):
                                    t = nc.tensor.matmul(b, hot_hit[:, 2 * t_ + c, 0:P], node_tab[:, v, c, :],
                                                         start=(c == 0 and v == 0), stop=(c == 1 and v == 1))
                        t.then_inc(looked, 1)
                    elif (kind, j) == ("K", 1):
                        copied = counted(pe, pe_reg)
                        pe.wait_ge(dve_const, 1)
                        pe.wait_ge(coef_now, copied)
                        turned = bank[7][0:48, :].bitcast(BF16)
                        for t_ in range(TG):
                            t = nc.tensor.transpose(turned[:, t_ * 128:t_ * 128 + P], coef3g[:, t_, :], identb[0:P, 0:P])
                        t.then_inc(coef_turned, 1)

            each_group(pe, pass_a)

            def messages(x_, group, l):
                if group is None:
                    return
                i, k, q = group
                j, m = x_[1], i + l * NG
                if j == 0:
                    pe.wait_ge(g_s[q], (k + 1 + (1 + l) * uses(q)) * 64)
                    reuse(pe, m_agg, m)
                    turn_rows(E1, gat[:, q, :, :]).then_inc(m_gT[q], 1)
                elif 2 <= j < 2 + B1 + NQ:
                    b = j - 2 - NQ
                    if b >= 0:
                        pe.wait_ge(m_sc, m * B1 + b + 1)
                        nc.tensor.matmul(E1[:, 0:GE], wt[:, l, 1 + b, :], scaled[:, b % NQ, :],
                                         start=(b == 0), stop=(b == B1 - 1)).then_inc(m_mm, 1)
                    if b + NQ < B1:
                        nc.tensor.matmul(bank[4 + (b + NQ) % NQ][:, 0:GE], sel[:, l * B1 + b + NQ, :],
                                         grp(coeft, i, GE), start=True, stop=True).then_inc(m_bc, 1)

            def edge_rows(x_, i, k, q, l):
                j, n = x_[1], i + 1 + l * NG
                if j == 0:
                    pe.wait_ge(m_agg, n)
                    pe.wait_ge(ld_e[q], (k + 1 + (2 + l) * uses(q)) * 16)
                    reuse(pe, m_out if l else m_tt, i)
                    rows_out(E2, own[:, q, :], l, agg[:, q, :]).then_inc(m_y, 1)
                elif j == 3:
                    pe.wait_ge(m_yn, n)
                    turn_rows(E2, ye).then_inc(m_ynT, 1)
                elif j == 6 and l:
                    pe.wait_ge(m_z, n)
                    turn_back(E2, fo).then_inc(m_back, 1)

            def two_halves(order, l):
                for x_ in stream("M", 3 + B1 + NQ):
                    messages(x_, (0, 0, 0), l)

                def one(i, k, q):
                    for x_ in order:
                        if x_[0] in "DF":
                            dense(x_, steps_b(i, k, q))
                        elif x_[0] == "M":
                            messages(x_, ahead(i, k, q), l)
                        elif x_[0] == "U":
                            edge_rows(x_, i, k, q, l)
                each_group(pe, one)

            pe.wait_ge(coef_ready, NG)
            pe.wait_ge(looked_used, NG)
            two_halves(ORDER_B, 0)
            pe.wait_ge(m_tt, NG)
            two_halves(ORDER_C, 1)

        @block.vector
        def _(dve):
            v = nc.vector
            steps = [0]

            def own_step(ins):
                steps[0] += 1
                ins.then_inc(prep, 1)
                dve.wait_ge(prep, steps[0])

            for t in (ident, identb, anti):
                v.memset(t[:, :], 0.0)
            v.memset(sel[:, :, :], 0.0)
            v.memset(compt[:, :], 0.0).then_inc(dve_const, 1)
            v.memset(zerob[:, :], 0.0)
            v.memset(ones[:, :], 1.0)
            v.memset(onesb[:, :], 1.0)
            v.memset(bias[:, :, :, :], 0.0)
            v.memset(carryc[:, :], 0.0)
            v.memset(first16[:, :], 0.0)
            for r in range(4):
                v.memset(blockno[r * HEAD:(r + 1) * HEAD, :], float(r))
            v.memset(carry[:, :], 0.0).then_inc(dve_const, 1)
            dve.wait_ge(dve_const, 2)
            v.memset(first16[0:R1, :], 1.0).then_inc(dve_const, 1)

            dve.wait_ge(ld_idx, 48)
            v.tensor_copy(rawf[:, :, :], raw[:, :, :])
            for m in range(2):
                v.tensor_single_scalar(part[:, 2 * m, :], raw[:, m, :], 8, ALU.logical_shift_right)
                own_step(v.tensor_single_scalar(part[:, 2 * m + 1, :], raw[:, m, :], LOB - 1, ALU.bitwise_and))
            v.tensor_copy(turn[:, 0:2, :], rawf[:, 0:2, :])
            own_step(v.tensor_tensor(lastf[:, :], rawf[:, DST_, :], rawf[:, OUT_, :], ALU.is_equal))
            v.scalar_tensor_tensor(turn[:, 2, :], lastf[:, :], float(1 << 20), rawf[:, DST_, :], ALU.mult, ALU.add)
            v.tensor_copy(turn[:, 3:7, :], part[:, :, :])
            own_step(v.tensor_copy(rawf[:, 2, :], part[:, 2, :]))
            v.scalar_tensor_tensor(turn[:, 5, :], lastf[:, :], 1024.0, rawf[:, 2, :],
                                   ALU.mult, ALU.add).then_inc(idx_split, 1)
            dve.wait_ge(idx_turned, 1)
            tb = lambda m: bank[2 + m // 4][0:P, (m % 4) * 128:(m % 4) * 128 + NT].rearrange("p (g t) -> p g t", t=TG)
            v.tensor_copy(gidx[:, :, 0:TG], tb(0))
            v.tensor_copy(gidx[:, :, TG:2 * TG], tb(1)).then_inc(idx_ready, 1)
            v.tensor_copy(tidx[:, :, :], tb(2))
            for m in range(4):
                v.tensor_copy(meta[:, :, m * TG:(m + 1) * TG], tb(3 + m))
            dve.wait_ge(pool_const, 4)
            v.tensor_scalar(relno[32:64, :], relno[32:64, :], -32.0, None, ALU.add)
            own_step(v.tensor_copy(meta[:, :, 4 * TG:5 * TG], tileno[:, :].rearrange("p (g t) -> p g t", t=TG)))
            v.tensor_scalar(hit[0:32, 0:1], relno[0:32, :], float(R1), None, ALU.is_ge)
            own_step(v.tensor_copy(hit[0:32, 1:2], relno[0:32, :]))
            own_step(v.scalar_tensor_tensor(relno[0:32, :], hit[0:32, 0:1], -float(R1), hit[0:32, 1:2],
                                            ALU.mult, ALU.add))

            dve.wait_ge(ld_w, 16 * 17)
            wv = wt[:, :, :, :].rearrange("p l b f -> p (l b) f")
            own_step(v.tensor_reduce(wsum[:, :], wv, AX.X, ALU.add))
            own_step(v.tensor_scalar(wsum[:, :], wsum[:, :], 1.0 / D, None, ALU.mult))
            own_step(v.tensor_tensor(wv, wv, wsum[:, :].unsqueeze(2).to_broadcast([128, 18, 128]), ALU.subtract))
            own_step(v.tensor_reduce(bsum[:, :], brow[:, :, :], AX.X, ALU.add))
            own_step(v.tensor_scalar(bsum[:, :], bsum[:, :], 1.0 / D, None, ALU.mult))
            own_step(v.tensor_tensor(brow[:, :, :], brow[:, :, :], bsum[:, :].unsqueeze(2).to_broadcast([96, 2, 128]),
                                     ALU.subtract))
            for m in range(3):
                own_step(v.tensor_copy(bpart[:, :, :], brow[:, :, :]))
                for l in range(2):
                    v.tensor_copy(bias[32 * m:32 * m + 1, l, :, :],
                                  bpart[32 * m:32 * m + 1, l, :].unsqueeze(1).to_broadcast([1, TG, 128]))
                own_step(v.tensor_tensor(brow[:, :, :], brow[:, :, :], bpart[:, :, :], ALU.subtract))
            v.tensor_copy(bsum[:, :], bsum[:, :]).then_inc(w_ready, 1)

            MEAN, VAR, SPARE, SUM, ROOT, INV = range(6)

            def moments(rows, st, mv, stats, n, var):
                for j in range(TG):
                    t = v.bn_stats(st[:, j, :], rows[:, j, :])
                t.then_inc(stats, 1)
                dve.wait_ge(stats, n * 3 - 2)
                c = lambda m: st[:, :, m]
                v.tensor_tensor(mv[:, SPARE, :], c(1), c(4), ALU.subtract)
                v.tensor_tensor(mv[:, MEAN, :], c(1), c(4), ALU.add)
                v.tensor_tensor(mv[:, VAR, :], c(2), c(5), ALU.add).then_inc(stats, 1)
                dve.wait_ge(stats, n * 3 - 1)
                v.tensor_scalar(mv[:, MEAN, :], mv[:, MEAN, :], 0.5, None, ALU.mult)
                v.scalar_tensor_tensor(mv[:, SPARE, :], mv[:, SPARE, :], D / 4.0, mv[:, SPARE, :],
                                       ALU.mult, ALU.mult).then_inc(stats, 1)
                dve.wait_ge(stats, n * 3)
                v.tensor_tensor(mv[:, VAR, :], mv[:, VAR, :], mv[:, SPARE, :], ALU.add).then_inc(var, 1)

            def inverse(mv, ready, n, done):
                dve.wait_ge(ready, n)
                v.reciprocal(mv[:, INV, :], mv[:, ROOT, :]).then_inc(done, 1)
                dve.wait_ge(done, n)

            def normalize(dst, rows, mv, done):
                for j in range(TG):
                    t = v.tensor_scalar(dst[:, j, :], rows[:, j, :], mv[:, MEAN, j:j + 1], mv[:, INV, j:j + 1],
                                        ALU.subtract, ALU.mult)
                t.then_inc(done, 1)

            def scale_rows(dst, b, mv, done):
                v.tensor_tensor(dst[:, :, :], rows4(b), mv[:, INV, :].unsqueeze(2).to_broadcast([P, TG, D]),
                                ALU.mult).then_inc(done, 1)

            def leaky(dst, t_, ready, n, done):
                dve.wait_ge(ready, n)
                v.scalar_tensor_tensor(dst, t_, SLOPE, t_, ALU.mult, ALU.max).then_inc(done, 1)

            def first(j, item):
                n, h, par = item
                n = n + 1
                if j == 0:
                    dve.wait_ge(d_x[par], (h + 1) * 16)
                    moments(xin[:, par, :, :], st_d, mv_d, d_stats, n, d_var)
                elif j == 2:
                    inverse(mv_d, d_sd, n, d_rs)
                    normalize(nd, xin[:, par, :, :], mv_d, d_norm)
                elif j == 7:
                    inverse(mv_d, d_sd1, n, d_rs1)
                    scale_rows(nd, D1, mv_d, d_yn)
                elif j == 8:
                    reuse(dve, d_y2, n - 2)
                    leaky(zd[:, par, :], fd[:, :], d_t, n, d_z)

            def second(j, item):
                n, _, par = item
                n = n + 1
                if j == 2:
                    inverse(mv_d2, d_sd2, n, d_rs2)
                    scale_rows(nd2, D2, mv_d2, d_yn2)
                elif j == 5:
                    leaky(zd2[:, :], fd2[:, :], d_t2, n, d_z2)
                elif j == 7:
                    dve.wait_ge(d_back, n)
                    dve.wait_ge(d_copied, n)
                    v.tensor_tensor(outr[:, par, :, :], outr[:, par, :, :], rows4(D2), ALU.add).then_inc(d_out, 1)

            def dense(x_, steps_):
                kind, j, sub = x_
                now, then = steps_[sub]
                if kind == "F":
                    second(j, now)
                elif then is not None:
                    first(j, then)

            for j in range(9):
                first(j, (0, 0, 0))

            def one_hots(i, kinds):
                v.tensor_copy(metat[:, 0:kinds * TG], column(meta, i)[:, 0:kinds * TG]).then_inc(meta_now, 1)

            def pass_p(i, k, q):
                n = i + 1
                for x_ in ORDER_P:
                    kind, j, _ = x_
                    if kind in "DF":
                        dense(x_, steps_p(i, k, q))
                    elif (kind, j) == ("T", 0):
                        reuse(dve, tab_added, i)
                        one_hots(i, 5)
                        dve.wait_ge(meta_now, n)
                    elif (kind, j) == ("T", 1):
                        for t_ in range(TG):
                            c = lambda m: metat[:, m * TG + t_:m * TG + t_ + 1]
                            v.tensor_scalar(hot_hi[:, t_, :], iota_lo[:, 0:2 * HIC], c(2), None, ALU.is_equal)
                            v.tensor_scalar(hot_lo[:, 0, t_, :], iota_lo[:, :], c(3), c(4), ALU.is_equal, ALU.mult)
                            t = v.tensor_scalar(hot_lo[:, 1, t_, :], iota_lo[:, :], c(3), rowno[:, :],
                                                ALU.is_equal, ALU.mult)
                        t.then_inc(tab_hot, 1)
                    elif (kind, j) == ("C", 0):
                        dve.wait_ge(ld_cnt[q], (k + 1) * 80)
                        reuse(dve, cnt_summed, i)
                        v.tensor_tensor(contc[:, :], dstc[:, q, 1:GE + 1], dstc[:, q, 0:GE], ALU.is_equal)
                        v.tensor_scalar(hotc[:, :], etc[:, q, :], relno[:, :], None, ALU.is_equal).then_inc(cnt_hot, 1)
                    elif (kind, j) == ("C", 1):
                        dve.wait_ge(cnt_hot, n)
                        reuse(dve, cnt_carry, i)
                        v.tensor_tensor_scan(runc[:, :], contc[:, :], hotc[:, :], carryc[:, :],
                                             ALU.mult, ALU.add).then_inc(cnt_run, 1)
                    elif (kind, j) == ("C", 2):
                        dve.wait_ge(cnt_run, n)
                        v.tensor_copy(carryc[:, :], runc[:, GE - 1:GE]).then_inc(cnt_carry, 1)
                        v.tensor_tensor(prodc[:, :], runc[:, :], hotc[:, :], ALU.mult).then_inc(cnt_prods, 1)
                    elif (kind, j) == ("C", 4):
                        dve.wait_ge(cnt_summed, n)
                        g = lambda b, w: E1[0:P, b:b + TG * w]
                        v.tensor_copy(cnt_f[:, bass.ds(i * TG, TG)], g(0, 1))
                        v.tensor_copy(rdeg[:, bass.ds(i * TG, TG), :], g(16, BLK).rearrange("p (t r) -> p t r", r=BLK))
                        v.tensor_copy(cnt_b[:, bass.ds(NT - TG - i * TG, TG)], E2[0:P, 0:TG])
                        v.tensor_copy(coef[:, bass.ds(i * TG, TG), :],
                                      g(64, R1).rearrange("p (t r) -> p t r", r=R1)).then_inc(cnt_saved, 1)

            each_group(dve, pass_p)
            dve.wait_ge(tab_sum, 1)
            for v_ in range(2):
                for c in range(2):
                    t = v.tensor_copy(node_tab[:, v_, c, :], bank[4 + 2 * v_ + c][0:HIC, 0:LOB])
            t.then_inc(tab_ready, 1)
            dve.wait_ge(cnt_saved, NG)
            own_step(v.tensor_scalar(rdeg[:, :, :], rdeg[:, :, :], 1.0, None, ALU.max))
            own_step(v.reciprocal(rdeg[:, :, :], rdeg[:, :, :]))
            dve.wait_ge(cnt_flipped, 1)
            own_step(v.scalar_tensor_tensor(cnt_f[:, :], cnt_f[:, :], -1.0, E1[0:P, 0:NT], ALU.add, ALU.add))
            own_step(v.reciprocal(cnt_b[:, :], cnt_f[:, :]))
            own_step(v.tensor_tensor(coef[:, :, :], coef[:, :, :],
                                     cnt_b[:, :].unsqueeze(2).to_broadcast([P, NT, R1]), ALU.mult))
            for m in range(3):
                own_step(v.tensor_copy(coef3[:, :, m * R1:(m + 1) * R1], coef[:, :, :]))
                if m < 2:
                    own_step(v.tensor_tensor(coef[:, :, :], coef[:, :, :], coef3[:, :, m * R1:(m + 1) * R1],
                                             ALU.subtract))

            def pass_a(i, k, q):
                n = i + 1
                for x_ in ORDER_A:
                    kind, j, _ = x_
                    if kind in "DF":
                        dense(x_, steps_a(i, k, q))
                    elif (kind, j) == ("E", 0):
                        dve.wait_ge(g_s[q], (k + 1) * 64)
                        moments(gat[:, q, :, :], st_e, mv_s, s_stats, n, s_var)
                    elif (kind, j) == ("E", 1):
                        dve.wait_ge(ld_e[q], (k + 1) * 32)
                        v.tensor_scalar(mask[:, :], et5b[:, q, :], blockno[:, :], None, ALU.is_equal)
                        v.tensor_tensor(grp(cont, i, GE), dstb[:, q, 1:GE + 1], dstb[:, q, 0:GE], ALU.is_equal
                                        ).then_inc(cont_ready, 1)
                    elif (kind, j) == ("E", 2):
                        inverse(mv_s, s_sd, n, s_rs)
                        reuse(dve, st_ns, 16 * i)
                        normalize(ne, gat[:, q, :, :], mv_s, s_norm[q])
                    elif (kind, j) == ("E", 6):
                        dve.wait_ge(cont_ready, n)
                        dve.wait_ge(s_m0, n)
                        v.scalar_tensor_tensor(msg[:, :], E2[:, 0:GE], b0t[:, 0:1], mask[:, :], ALU.add, ALU.mult
                                               ).then_inc(msg_ready, 1)
                        dve.wait_ge(msg_ready, n)
                        reuse(dve, carried, i)
                        v.tensor_tensor_scan(agg[:, 0, :], grp(cont, i, GE), msg[:, :], carry[:, 2:3],
                                             ALU.mult, ALU.add).then_inc(agg_ready, 1)
                    elif (kind, j) == ("E", 7):
                        dve.wait_ge(agg_ready, n)
                        v.tensor_copy(carry[:, 2:3], agg[:, 0, GE - 1:GE]).then_inc(carried, 1)
                    elif (kind, j) == ("E", 8):
                        dve.wait_ge(agg_T, n)
                        inv = rdeg[:, bass.ds(i * TG, TG), :].rearrange("p t r -> p (t r)")
                        v.tensor_tensor(mean[:, :, :].rearrange("p t (r c) -> p (t r) c", c=HEAD),
                                        E2[0:P, :].rearrange("p (r c) -> p r c", c=HEAD),
                                        inv.unsqueeze(2).to_broadcast([P, TG * BLK, HEAD]), ALU.mult
                                        ).then_inc(t_mean, 1)
                    elif (kind, j) == ("E", 9):
                        dve.wait_ge(g_d[q], (k + 1) * 64)
                        dve.wait_ge(t_mean, n)
                        reuse(dve, st_x1, 16 * i)
                        v.tensor_tensor(x1e[:, :, :], gat[:, q, TG:2 * TG, :], mean[:, :, :], ALU.add
                                        ).then_inc(t_x1[q], 1)
                    elif (kind, j) == ("E", 10):
                        inverse(mv_y, s_sd1, n, s_rs1)
                        reuse(dve, st_zs, 16 * i)
                        scale_rows(ye, E1, mv_y, s_yn)
                    elif (kind, j) == ("E", 11):
                        dve.wait_ge(t_x1[q], k + 1)
                        moments(x1e, st_t, mv_t, t_stats, n, t_var)
                    elif (kind, j) == ("E", 13):
                        inverse(mv_t, t_sd, n, t_rs)
                        reuse(dve, st_nt, 16 * i)
                        normalize(ne2, x1e, mv_t, t_norm)
                    elif (kind, j) == ("L", 0):
                        one_hots(i, 2)
                        dve.wait_ge(meta_now, n + NG)
                        for t_ in range(TG):
                            v.tensor_scalar(hot_lo[:, 0, t_, :], iota_lo[:, :], metat[:, TG + t_:TG + t_ + 1],
                                            None, ALU.is_equal)
                            t = v.tensor_scalar(hot_hi[:, t_, :], iota_lo[:, 0:2 * HIC], metat[:, t_:t_ + 1],
                                                None, ALU.is_equal)
                        t.then_inc(hot_ready, 1)
                    elif (kind, j) == ("L", 4):
                        dve.wait_ge(looked, n)
                        for t_ in range(TG):
                            t = v.tensor_tensor_reduce(
                                junk[:, t_, :], bank[5 + t_ // 2][0:P, (t_ % 2) * LOB:(t_ % 2 + 1) * LOB],
                                hot_lo[:, 0, t_, :], 1.0, 0.0, ALU.mult, ALU.add, res[:, t_:t_ + 1])
                        t.then_inc(looked_used, 1)
                        dve.wait_ge(looked_used, n)
                        v.tensor_copy(found[:, bass.ds(i * TG, TG)], res[:, :]).then_inc(found_now, 1)
                    elif (kind, j) == ("K", 0):
                        reuse(dve, coef_turned, i)
                        v.tensor_copy(coef3g[:, :, :], coef3[:, bass.ds(i * TG, TG), :]).then_inc(coef_now, 1)

            each_group(dve, pass_a)
            dve.wait_ge(found_now, NG)
            own_step(v.tensor_copy(foundi[:, :], found[:, :]))
            own_step(v.tensor_single_scalar(foundi[:, :], foundi[:, :], 7, ALU.logical_shift_right))
            own_step(v.tensor_copy(hit[:, :], foundi[:, :]))
            own_step(v.scalar_tensor_tensor(slotf[:, :], hit[:, :], float(P - 128), found[:, :], ALU.mult, ALU.add))
            own_step(v.tensor_scalar(slotf[:, :], slotf[:, :], -float(P), None, ALU.add))
            own_step(v.tensor_tensor(slotf[:, :], slotf[:, :], slotno[:, :], ALU.subtract))
            own_step(v.tensor_scalar(hit[:, :], hit[:, :], 0.5, None, ALU.is_gt))
            own_step(v.tensor_tensor(slotf[:, :], slotf[:, :], hit[:, :], ALU.mult))
            own_step(v.tensor_tensor(slotf[:, :], slotf[:, :], slotno[:, :], ALU.add))
            v.tensor_copy(sidx[:, :, :], slotf[:, :].rearrange("p (g t) -> p g t", t=TG)).then_inc(slots_ready, 1)

            def messages(x_, group, l):
                if group is None:
                    return
                i, k, q = group
                j, m = x_[1], i + l * NG
                if j == 2 and l:
                    reuse(dve, m_mm, B1 * (m - 1))
                    leaky(fe[:, q, :], te[:, :], m_t, i + 1, m_g)
                elif 3 <= j < 3 + B1:
                    b = j - 3
                    if b == 0:
                        dve.wait_ge(m_g, m + 1)
                    dve.wait_ge(m_bc, m * B1 + b + 1)
                    reuse(dve, m_mm, m * B1 + b + 1 - NQ)
                    v.tensor_tensor(scaled[:, b % NQ, :], fe[:, q, :], bank[4 + b % NQ][:, 0:GE], ALU.mult
                                    ).then_inc(m_sc, 1)
                elif j == 2 + B1 + NQ:
                    dve.wait_ge(m_mm, (m + 1) * B1)
                    reuse(dve, m_y, m - 1)
                    reuse(dve, carried, m + NG)
                    v.tensor_tensor_scan(agg[:, q, :], grp(cont, i, GE), E1[:, 0:GE], carry[:, l:l + 1],
                                         ALU.mult, ALU.add).then_inc(m_agg, 1)
                    dve.wait_ge(m_agg, m + 1)
                    v.tensor_copy(carry[:, l:l + 1], agg[:, q, GE - 1:GE]).then_inc(carried, 1)

            def edge_rows(x_, i, k, q, l):
                j, n = x_[1], i + 1 + l * NG
                if j == 2:
                    inverse(mv_y, m_sd, n, m_rs)
                    if l == 0:
                        reuse(dve, st_zn, 16 * i)
                    scale_rows(ye, E2, mv_y, m_yn)
                elif j == 5:
                    if l == 0:
                        reuse(dve, st_z, 16 * i)
                    leaky(fo[:, :], te2[:, :], m_tt, n, m_z)
                elif j == 7 and l:
                    dve.wait_ge(m_back, i + 1)
                    dve.wait_ge(ld_x1[q], (k + 1) * 16)
                    reuse(dve, st_out, 16 * TG * i)
                    v.tensor_tensor(x1e[:, :, :], x1b[:, q, :, :], rows4(E2), ALU.add).then_inc(m_out, 1)

            def two_halves(order, l):
                for x_ in stream("M", 3 + B1 + NQ):
                    messages(x_, (0, 0, 0), l)

                def one(i, k, q):
                    for x_ in order:
                        if x_[0] in "DF":
                            dense(x_, steps_b(i, k, q))
                        elif x_[0] == "M":
                            messages(x_, ahead(i, k, q), l)
                        elif x_[0] == "U":
                            edge_rows(x_, i, k, q, l)
                each_group(dve, one)

            dve.wait_ge(st_zs, 16 * NG)
            dve.wait_ge(st_h, 16 * NG)
            two_halves(ORDER_B, 0)
            dve.wait_ge(st_x1, 16 * NG)
            dve.wait_ge(st_zn, 16 * NG)
            dve.wait_ge(st_z, 16 * NG)
            two_halves(ORDER_C, 1)


_DRAM_INS = ["x", "src", "dst_ext", "dst_both", "et_both", "et5", "w0", "b0", "v1", "comp1", "root1", "bias1", "g1",
             "be1", "v2", "comp2", "root2", "bias2", "g2", "be2"]


def kernel(x, src, dst, edge_type_16, edge_type_5, L0_gnn_Ws, L0_gnn_bs, L1_gnn_weight1, L1_gnn_comp1,
           L1_gnn_root1, L1_gnn_bias1, L1_gnn_ln1_g, L1_gnn_ln1_b, L1_gnn_weight2, L1_gnn_comp2,
           L1_gnn_root2, L1_gnn_bias2, L1_gnn_ln2_g, L1_gnn_ln2_b):
    import numpy as np
    import concourse.bacc as bacc
    from concourse.bass_utils import run_bass_kernel_spmd

    dst, et16 = np.asarray(dst), np.asarray(edge_type_16)
    edge = np.full(1, -1, dst.dtype)
    arrays = {
        "x": x, "src": src,
        "dst_ext": np.concatenate([edge, dst, edge]),
        "dst_both": np.stack([np.concatenate([edge, dst]), np.concatenate([edge, dst[::-1]])]),
        "et_both": np.stack([et16, et16[::-1]]),
        "et5": edge_type_5, "w0": L0_gnn_Ws, "b0": L0_gnn_bs,
        "v1": L1_gnn_weight1, "comp1": L1_gnn_comp1, "root1": L1_gnn_root1, "bias1": L1_gnn_bias1,
        "g1": L1_gnn_ln1_g, "be1": L1_gnn_ln1_b,
        "v2": L1_gnn_weight2, "comp2": L1_gnn_comp2, "root2": L1_gnn_root2, "bias2": L1_gnn_bias2,
        "g2": L1_gnn_ln2_g, "be2": L1_gnn_ln2_b,
    }
    nc = bacc.Bacc("TRN2", target_bir_lowering=False, num_devices=1)
    feed, args = {}, []
    for name in _DRAM_INS:
        a = np.ascontiguousarray(arrays[name])
        feed[f"in_{name}"] = a
        args.append(nc.dram_tensor(f"in_{name}", a.shape, mybir.dt.from_np(a.dtype), kind="ExternalInput").ap())
    out = nc.dram_tensor("out", (N, D), F32, kind="ExternalOutput").ap()
    gnn_kernel(nc, *args, out)
    r = run_bass_kernel_spmd(nc, [feed], core_ids=[0])
    return r.results[0]["out"]
```

```python
from contextlib import ExitStack

import concourse.bass as bass
from concourse import mybir

ALU = mybir.AluOpType
ACT = mybir.ActivationFunctionType
AX = mybir.AxisListType
F32 = mybir.dt.float32
BF16 = mybir.dt.bfloat16
I32 = mybir.dt.int32

N = 50000
E = 12500
D = 128
R1 = 16
B1 = 8
HEAD = 32
P = 125
TG = 4
NT = E // P
NG = NT // TG
GE = TG * P
NI = N // GE
LOB = 256
HIC = 98
BLK = 4
EPS = 1e-5
SLOPE = 0.1
NS = 4
NQ = 3
SRC_, DST_, OUT_ = 0, 1, 2


def gnn_kernel(nc, x, src, dst_ext, dst_both, et_both, et5, w0, b0, v1, comp1, root1, bias1, g1, be1,
               v2, comp2, root2, bias2, g2, be2, out):
    ctx = ExitStack()
    with ctx:
        def sb(name, shape, dt=F32):
            return ctx.enter_context(nc.sbuf_tensor(name, shape, dt))

        def sem(name):
            return ctx.enter_context(nc.semaphore(name))

        def dram(name, shape, dt=F32):
            return nc.dram_tensor(name, shape, dt).ap()

        tab1 = dram("tab1", [2 * E, D])
        tab2 = dram("tab2", [2 * E, D])
        x1_dram = dram("x1_dram", [E, D])
        own1_dram = dram("own1_dram", [D, E])
        own2_dram = dram("own2_dram", [D, E])

        ident = sb("ident", [128, 128])
        identb = sb("identb", [128, 128], BF16)
        anti = sb("anti", [128, 128])
        anti_t = sb("anti_t", [NT, NT])
        sel = sb("sel", [48, R1, 128], BF16)
        ones = sb("ones", [128, 128])
        onesb = sb("onesb", [128, 128], BF16)
        zerob = sb("zerob", [48, HIC], BF16)
        iota_lo = sb("iota_lo", [P, LOB])
        relno = sb("relno", [128, 1])
        runs = sb("runs", [128, 1])
        rowno = sb("rowno", [P, 1])
        tileno = sb("tileno", [P, NT])
        slotno = sb("slotno", [P, NT])
        blockno = sb("blockno", [128, 1])
        epst = sb("epst", [128, 1])

        wt = sb("wt", [128, 2, 9, 128])
        wsum = sb("wsum", [128, 18])
        w0t = sb("w0t", [128, 4 * HEAD])
        b0t = sb("b0t", [128, 1])
        ln = sb("ln", [128, 4])
        brow = sb("brow", [128, 2, 128])
        bcol = sb("bcol", [128, 2])
        bsum = sb("bsum", [128, 2])
        bpart = sb("bpart", [96, 2, 128], BF16)
        bias = sb("bias", [96, 2, TG, 128], BF16)
        take = sb("take", [128, 2 + BLK + 2 * B1])

        raw = sb("raw", [NT, 3, P], I32)
        rawf = sb("rawf", [NT, 3, P])
        part = sb("part", [NT, 4, P], I32)
        turn = sb("turn", [NT, 7, P])
        lastf = sb("lastf", [NT, P])
        gidx = sb("gidx", [P, NG, 2 * TG], I32)
        sidx = sb("sidx", [P, NG, TG], I32)
        tidx = sb("tidx", [P, NG, TG], I32)
        meta = sb("meta", [P, NG, 6 * TG])
        metat = sb("metat", [P, 5 * TG])
        metag = sb("metag", [P, 5 * TG])
        found = sb("found", [P, NT])
        foundi = sb("foundi", [P, NT], I32)
        hit = sb("hit", [P, NT])
        slotf = sb("slotf", [P, NT])
        res = sb("res", [P, TG])
        hot_hi = sb("hot_hi", [P, TG, 2 * HIC], BF16)
        hot_lo = sb("hot_lo", [P, 2, TG, LOB], BF16)
        hot_hit = sb("hot_hit", [HIC, TG * 2, 128], BF16)
        node_tab = sb("node_tab", [HIC, 2, 2, LOB], BF16)
        junk = sb("junk", [P, TG, LOB], BF16)

        dstb = sb("dstb", [128, 2, GE + 1], I32)
        et5b = sb("et5b", [128, 2, GE], I32)
        scaled = sb("scaled", [128, NS, GE])
        contc, hotc, runc, prodc = (scaled[:, m, :] for m in range(4))
        carryc = sb("carryc", [128, 1])
        flip = sb("flip", [NT, P])
        cnt_f = sb("cnt_f", [P, NT])
        cnt_b = sb("cnt_b", [P, NT])
        rdeg = sb("rdeg", [P, NT, BLK])
        coef = sb("coef", [P, NT, R1])
        coef3 = sb("coef3", [P, NT, 48], BF16)
        coef3g = sb("coef3g", [P, TG, 48], BF16)
        coeft = sb("coeft", [48, E], BF16)
        cont = sb("cont", [128, E], BF16)

        xin = sb("xin", [P, 2, TG, D])
        outr = sb("outr", [P, 2, TG, D])
        nd, nd1, nd2 = sb("nd", [P, TG, D]), sb("nd1", [P, TG, D]), sb("nd2", [P, TG, D])
        fd, fd1, fd2 = sb("fd", [128, GE]), sb("fd1", [128, GE]), sb("fd2", [128, GE])
        zd, zd2 = sb("zd", [128, GE]), sb("zd2", [128, GE])
        sq_d = sb("sq_d", [P, TG, D], BF16)
        sq_d2 = sb("sq_d2", [P, TG, D], BF16)
        st_d = sb("st_d", [P, TG, 6])
        mv_d, mv_d1, mv_d2 = sb("mv_d", [P, TG, 6]), sb("mv_d1", [P, TG, 6]), sb("mv_d2", [P, TG, 6])

        gat = sb("gat", [P, 2, 2 * TG, D])
        nowidx = sb("nowidx", [P, 2, 2 * TG], I32)
        nowout = sb("nowout", [P, TG], I32)
        ne = sb("ne", [P, TG, D])
        fe = sb("fe", [128, 2, GE])
        te = sb("te", [128, GE])
        ye = sb("ye", [P, TG, D])
        mask = sb("mask", [128, GE])
        msg = sb("msg", [128, GE])
        total = msg
        agg = sb("agg", [128, 2, GE])
        mean = sb("mean", [P, TG, D])
        carry = sb("carry", [128, 3])
        x1e = sb("x1e", [P, TG, D])
        x1b = sb("x1b", [P, 2, TG, D])
        ne2 = sb("ne2", [P, TG, D])
        own = sb("own", [128, 2, GE])
        te2 = sb("te2", [128, GE])
        fo = sb("fo", [128, GE])
        sq_e = sb("sq_e", [P, TG, D], BF16)
        st_e = sb("st_e", [P, TG, 6])
        st_t = sb("st_t", [P, TG, 6])
        mv_s = sb("mv_s", [P, TG, 6])
        mv_y = sb("mv_y", [P, TG, 6])
        mv_t = sb("mv_t", [P, TG, 6])

        bank = [ctx.enter_context(nc.psum_tensor(f"bank{i}", [128, 512], F32)) for i in range(8)]
        D1, D2, D3, E1, E2, E3 = bank[0:6]
        hot_bank = bank[6]
        look_bank = [bank[6], bank[7]]
        table_bank = lambda v, c: bank[6 + v][0:HIC, c * LOB:(c + 1) * LOB]
        coef_bank = bank[5:8]
        rows4 = lambda b: b[0:P, :].rearrange("p (t f) -> p t f", f=D)

        ld_idx, ld_w = sem("ld_idx"), sem("ld_w")
        ld_cnt = [sem("ld_cnt0"), sem("ld_cnt1")]
        pool_const, dve_const = sem("pool_const"), sem("dve_const")
        prep = sem("prep")
        w_ready = sem("w_ready")
        idx_split, idx_turned, idx_ready = sem("idx_split"), sem("idx_turned"), sem("idx_ready")
        cnt_hot, cnt_run, cnt_prods, cnt_summed, cnt_saved, cnt_carry = (
            sem("cnt_hot"), sem("cnt_run"), sem("cnt_prods"), sem("cnt_summed"), sem("cnt_saved"), sem("cnt_carry"))
        cnt_flipped, flip_saved = sem("cnt_flipped"), sem("flip_saved")
        coef_now, coef_turned, coef_ready = sem("coef_now"), sem("coef_turned"), sem("coef_ready")
        meta_now, metag_now, tab_high, tab_hot, tab_added, tab_sum, tab_ready = (
            sem("meta_now"), sem("metag_now"), sem("tab_high"), sem("tab_hot"), sem("tab_added"), sem("tab_sum"), sem("tab_ready"))
        hot_ready, hot_turned, hot_saved, looked, looked_used, found_now = (
            sem("hot_ready"), sem("hot_turned"), sem("hot_saved"), sem("looked"), sem("looked_used"), sem("found_now"))
        slots_ready, meta_ready = sem("slots_ready"), sem("meta_ready")

        d_x = [sem("d_x0"), sem("d_x1")]
        d_copied = sem("d_copied")
        stats, d_var, d_sd, d_rs, d_norm = (sem("stats"), sem("d_var"), sem("d_sd"), sem("d_rs"), sem("d_norm"))
        d_hT, d_h, d_y = sem("d_hT"), sem("d_h"), sem("d_y")
        d_sq, d_sd1, d_rs1, d_yn = sem("d_sq"), sem("d_sd1"), sem("d_rs1"), sem("d_yn")
        d_ynT, d_t, d_z = sem("d_ynT"), sem("d_t"), sem("d_z")
        d_y2, d_sq2, d_sd2, d_rs2, d_yn2 = (sem("d_y2"), sem("d_sq2"), sem("d_sd2"), sem("d_rs2"), sem("d_yn2"))
        d_yn2T, d_t2, d_z2, d_back, d_out = sem("d_yn2T"), sem("d_t2"), sem("d_z2"), sem("d_back"), sem("d_out")
        d_st = [sem("d_st0"), sem("d_st1")]

        now_ready = sem("now_ready")
        g_s = [sem("g_s0"), sem("g_s1")]
        g_d = [sem("g_d0"), sem("g_d1")]
        ld_e = [sem("ld_e0"), sem("ld_e1")]
        ld_x1 = [sem("ld_x10"), sem("ld_x11")]
        s_var, s_sd, s_rs = sem("s_var"), sem("s_sd"), sem("s_rs")
        s_norm = [sem("s_norm0"), sem("s_norm1")]
        t_x1 = [sem("t_x10"), sem("t_x11")]
        s_hT, s_h, s_m0, s_y = sem("s_hT"), sem("s_h"), sem("s_m0"), sem("s_y")
        s_sq, s_sd1, s_rs1, s_yn = sem("s_sq"), sem("s_sd1"), sem("s_rs1"), sem("s_yn")
        cont_ready, msg_ready, agg_ready, agg_T, carried, t_mean = (
            sem("cont_ready"), sem("msg_ready"), sem("agg_ready"), sem("agg_T"), sem("carried"), sem("t_mean"))
        t_var, t_sd, t_rs, t_norm, t_hT, t_h = (
            sem("t_var"), sem("t_sd"), sem("t_rs"), sem("t_norm"), sem("t_hT"), sem("t_h"))
        st_ns, st_nt, st_x1, st_h, st_zs = sem("st_ns"), sem("st_nt"), sem("st_x1"), sem("st_h"), sem("st_zs")

        m_gT = [sem("m_gT0"), sem("m_gT1")]
        m_t, m_g = sem("m_t"), sem("m_g")
        m_bc, m_sc, m_mm = sem("m_bc"), sem("m_sc"), sem("m_mm")
        m_own, m_sum = sem("m_own"), sem("m_sum")
        m_agg, m_y, m_sq, m_sd, m_rs, m_yn = (
            sem("m_agg"), sem("m_y"), sem("m_sq"), sem("m_sd"), sem("m_rs"), sem("m_yn"))
        m_ynT, m_tt, m_z, m_back, m_out = sem("m_ynT"), sem("m_tt"), sem("m_z"), sem("m_back"), sem("m_out")
        out_now = sem("out_now")
        st_zn, st_z, st_out = sem("st_zn"), sem("st_z"), sem("st_out")

        block = ctx.enter_context(nc.Block())

        def each_group(eng, body, tail=1):
            body(0, 0, 0)
            body(1, 0, 1)
            with eng.Fori(1, (NG - tail) // 2) as k:
                body(k * 2, k, 0)
                body(k * 2 + 1, k, 1)
            for i in range(NG - tail, NG):
                body(i, i // 2, i % 2)

        def is_last(i):
            return type(i) is int and i == NG - 1

        def reuse(eng, s, n):
            if type(n) is not int or n > 0:
                eng.wait_ge(s, n)

        def counted(eng, reg):
            eng.reg_add(reg, reg, 1)
            return eng.snap(reg)

        def column(ap, i):
            return ap[:, i, :] if type(i) is int else ap[:, bass.ds(i, 1), :].squeeze(1)

        def grp(ap, i, n):
            return ap[:, bass.ds(i * n, n)]

        def rows_of(t, r0, i):
            return t[bass.ds(i * GE + r0, GE), :].rearrange("(t p) f -> p t f", p=P)

        def dense_rows(t, n):
            return t[bass.ds(n * GE, GE), :].rearrange("(p t) f -> p t f", p=P)

        def steps_p(i, k, q):
            return [((i, k, q), (i + 1, k + q, 1 - q), (i + 2, k + 1, q))]

        def steps_a(i, k, q):
            n = i * 2 + NG
            h = i + NG // 2
            a, b, c, d = (n, h, 1), (n + 1, h + 1, 0), (n + 2, h + 1, 1), (n + 3, h + 2, 0)
            return [(a, b, c), (b, c, d)]

        def steps_b(i, k, q):
            n = i + 3 * NG
            h = 3 * NG // 2
            left = NG - 1 - i if type(i) is int else 2
            return [((n, k + (h + q), 1 - q), (n + 1, k + (h + 1), q) if left >= 1 else None,
                     (n + 2, k + (h + q + 1), 1 - q) if left >= 2 else None)]

        def ahead(i, k, q):
            return None if is_last(i) else (i + 1, k + q, 1 - q)

        def ahead2(i, k, q):
            return None if type(i) is int and i > NG - 3 else (i + 2, k + 1, q)

        def message_group(kind, i, k, q, l):
            return ahead2(i, k, q) if l and kind == "N" else ahead(i, k, q)

        turn_bank = [E1, D1]

        def uses(q):
            return (NG + 1) // 2 if q == 0 else NG // 2

        def merged(*streams):
            at = [((j + 0.5) / len(s), n, x) for n, s in enumerate(streams) for j, x in enumerate(s)]
            return [x for _, _, x in sorted(at, key=lambda a: a[:2])]

        def stream(kind, n, sub=0):
            return [(kind, j, sub) for j in range(n)]

        def steps_in(text):
            return [(x[0], int(x[1:].rstrip("'")), int(x[-1] == "'")) for x in text.split()]

        ORDER_P = steps_in("C0 X0 Z0 X1 C1 Z1 C2 Y0 Z2 C3 T0 X2 Y1 T1 Y2 T2 Z3 X3 Z4 T3 Z5 Y3 Y4 X4 X5 C4 Z6 Y5 "
                           "X6 W0 T4")
        ORDER_A = steps_in("G0 E0 Z0 X0 Y0 L0 X1 L1 L2 E1 Z1 Z2 Y1 W0 X2 Y2 Z3 G1 Y3 Z4 X3 E2 Y4 L3 E3 Z5 X4 G2 "
                           "I0 X5 Z6 Y5 X6 L4 I1 G3 E4 Z0' Z1' L5 Z2' Y0' E5 X0' L6 G4 Z3' E6 X1' Y1' G5 X2' "
                           "Z4' X3' Y2' G6 Y3' Z5' X4' L7 E7 G7 Y4' W0' E8 X5' Y5' Z6' X6'")
        ORDER_B = steps_in("X0 Z0 N0 N1 X1 Z1 U0 U1 M0 Y0 M1 Z2 U2 M2 M3 U3 Y1 M4 U4 M5 M6 I0 M7 Y2 X2 M8 Z3 X3 "
                           "U5 Y3 Z4 Y4 X4 M9 W0 U6 M10 X5 Z5 U7 Y5 M11 Z6 X6")
        ORDER_C = steps_in("M0 M1 U0 U1 M2 M3 U2 U3 M4 U4 M5 M6 U5 M7 U6 U7 M8 U8 N0 N1 M9 U9 N2 M10 M11")
        THIRD = dict(Z=0, Y=1, W=1, X=2)
        START = stream("X", 7, 0) + merged(stream("W", 1), stream("Y", 6), stream("X", 7, 1))
        BARE = 6
        first_items = lambda x_: (1, 0, 1) if x_[2] else (0, 0, 0)

        @block.sync
        def _(sp):
            sp.dma_start(raw[:, SRC_, :], src.rearrange("(t p) -> t p", p=P)).then_inc(ld_idx, 16)
            sp.dma_start(raw[:, DST_, :], dst_ext[1:1 + E].rearrange("(t p) -> t p", p=P)).then_inc(ld_idx, 16)
            sp.dma_start(raw[:, OUT_, :], dst_ext[2:2 + E].rearrange("(t p) -> t p", p=P)).then_inc(ld_idx, 16)

            def load_x(item):
                n, _, par = item
                sp.dma_start(xin[:, par, :, :], dense_rows(x, n)).then_inc(d_x[par], 16)

            def store_out(item):
                n, _, par = item
                sp.wait_ge(d_out, n + 1)
                sp.dma_start(dense_rows(out, n), outr[:, par, :, :]).then_inc(d_st[par], 16)

            load_x((0, 0, 0))
            load_x((1, 0, 1))
            for l, (root, v) in enumerate(((root1, v1), (root2, v2))):
                sp.dma_start(wt[:, l, 0, :], root).then_inc(ld_w, 16)
                sp.dma_start(wt[:, l, 1:9, :], v.rearrange("b i o -> i b o")).then_inc(ld_w, 16)
            for l, (b, g, be, comp) in enumerate(((bias1, g1, be1, comp1), (bias2, g2, be2, comp2))):
                sp.dma_start(brow[:, l, :], b.partition_broadcast(128)).then_inc(ld_w, 16)
                sp.dma_start(bcol[:, l:l + 1], b.unsqueeze(1)).then_inc(ld_w, 16)
                sp.dma_start(ln[:, 2 * l:2 * l + 1], g.unsqueeze(1)).then_inc(ld_w, 16)
                sp.dma_start(ln[:, 2 * l + 1:2 * l + 2], be.unsqueeze(1)).then_inc(ld_w, 16)
                sp.wait_ge(dve_const, 1)
                sp.dma_start(take[96:96 + R1, 2 + BLK + l * B1:2 + BLK + (l + 1) * B1], comp).then_inc(ld_w, 16)
            sp.dma_start(w0t[:, :].rearrange("i (r o) -> i r o", r=4),
                         w0[0:4, :, 0:HEAD].rearrange("r i o -> i r o")).then_inc(ld_w, 16)
            for r in range(4):
                sp.dma_start(b0t[r * HEAD:(r + 1) * HEAD, :], b0[r, 0:HEAD].unsqueeze(1)).then_inc(ld_w, 16)

            def next_x(item):
                n, h, par = item
                sp.wait_ge(d_norm, n + 1)
                sp.wait_ge(d_copied, n + 1)
                load_x((n + 2, h + 1, par))

            next_x((0, 0, 0))

            def load_count(i, q):
                for h, p0 in ((0, 0), (1, 32), (0, 64)):
                    sp.dma_start(dstb[p0:p0 + 32, q, :],
                                 dst_both[h, bass.ds(i * GE, GE + 1)].partition_broadcast(32)).then_inc(ld_cnt[q], 16)
                for h, p0 in ((0, 0), (1, 32), (0, 96)):
                    sp.dma_start(et5b[p0:p0 + 32, q, :],
                                 et_both[h, bass.ds(i * GE, GE)].partition_broadcast(32)).then_inc(ld_cnt[q], 16)
                sp.dma_start(et5b[64:96, q, :], et5[bass.ds(i * GE, GE)].partition_broadcast(32)).then_inc(ld_cnt[q], 16)

            load_count(0, 0)

            def pass_p(i, k, q):
                if not is_last(i):
                    sp.wait_ge(dve_const, 1)
                    reuse(sp, cnt_hot, i)
                    load_count(i + 1, 1 - q)
                ((last, mid, _),) = steps_p(i, k, q)
                next_x(mid)
                store_out(last)

            each_group(sp, pass_p)

            def load_edges(i, q):
                sp.dma_start(dstb[:, q, :], dst_ext[bass.ds(i * GE, GE + 1)].partition_broadcast(128)).then_inc(ld_e[q], 16)
                sp.dma_start(et5b[:, q, :], et5[bass.ds(i * GE, GE)].partition_broadcast(128)).then_inc(ld_e[q], 16)

            sp.wait_ge(cnt_hot, NG)
            load_edges(0, 0)
            load_edges(1, 1)

            def store_sources(i, k, q):
                sp.wait_ge(s_norm[q], k + 1)
                sp.dma_start(rows_of(tab1, E, i), ne[:, :, :]).then_inc(st_ns, 16)

            store_sources(0, 0, 0)

            def pass_a(i, k, q):
                (last, mid, _), (last1, mid1, _) = steps_a(i, k, q)
                if type(i) is not int or i < NG - 2:
                    sp.wait_ge(dve_const, 1)
                    sp.wait_ge(cont_ready, i + 1)
                    load_edges(i + 2, q)
                sp.wait_ge(s_yn, i + 1)
                sp.dma_start(rows_of(tab2, E, i), ye[:, :, :]).then_inc(st_zs, 16)
                sp.wait_ge(t_x1[q], k + 1)
                sp.dma_start(rows_of(x1_dram, 0, i), x1e[:, :, :]).then_inc(st_x1, 16)
                if not is_last(i):
                    store_sources(*ahead(i, k, q))
                next_x(mid)
                store_out(last)
                sp.wait_ge(t_norm, i + 1)
                sp.dma_start(rows_of(tab1, 0, i), ne2[:, :, :]).then_inc(st_nt, 16)
                next_x(mid1)
                sp.wait_ge(dve_const, 1)
                sp.wait_ge(t_h, i + 1)
                sp.dma_start(grp(own1_dram, i, GE), fo[:, :]).then_inc(st_h, 16)
                store_out(last1)

            each_group(sp, pass_a, 3)

            def load_own(dr, i, q):
                sp.dma_start(own[:, q, :], grp(dr, i, GE)).then_inc(ld_e[q], 16)

            sp.wait_ge(st_h, 16 * NG)
            load_own(own1_dram, 0, 0)

            def pass_b(i, k, q):
                if not is_last(i):
                    reuse(sp, m_y, i)
                    load_own(own1_dram, i + 1, 1 - q)
                ((last, mid, _),) = steps_b(i, k, q)
                if type(i) is not int or i < NG - 3:
                    next_x(mid)
                sp.wait_ge(m_yn, i + 1)
                sp.dma_start(rows_of(tab2, 0, i), ye[:, :, :]).then_inc(st_zn, 16)
                sp.wait_ge(dve_const, 1)
                sp.wait_ge(m_z, i + 1)
                sp.dma_start(grp(own2_dram, i, GE), fo[:, :]).then_inc(st_z, 16)
                store_out(last)

            each_group(sp, pass_b, 3)

            def load_x1(i, q):
                sp.dma_start(x1b[:, q, :, :], rows_of(x1_dram, 0, i)).then_inc(ld_x1[q], 16)

            sp.wait_ge(st_z, 16 * NG)
            sp.wait_ge(st_x1, 16 * NG)
            load_own(own2_dram, 0, 0)
            load_x1(0, 0)

            def pass_c(i, k, q):
                if not is_last(i):
                    sp.wait_ge(dve_const, 1)
                    sp.wait_ge(m_y, i + NG)
                    load_own(own2_dram, i + 1, 1 - q)
                    reuse(sp, st_out, 16 * TG * i)
                    load_x1(i + 1, 1 - q)

            each_group(sp, pass_c)

        @block.gpsimd
        def _(pool):
            pool_reg = pool.alloc_register("pool_reg")
            pool.reg_mov(pool_reg, 0)
            out_reg = pool.alloc_register("out_reg")
            pool.reg_mov(out_reg, 0)
            pool.wait_ge(dve_const, 1)
            nc.gpsimd.affine_select(out=ident[:, :], in_=ident[:, :], compare_op=ALU.not_equal, fill=1.0,
                                    base=0, pattern=[[-1, 128]], channel_multiplier=1)
            nc.gpsimd.affine_select(out=identb[:, :], in_=identb[:, :], compare_op=ALU.not_equal, fill=1.0,
                                    base=0, pattern=[[-1, 128]], channel_multiplier=1)
            exact = dict(allow_small_or_imprecise_dtypes=True)
            nc.gpsimd.iota(iota_lo[:, :], [[1, LOB]], base=0, channel_multiplier=0, **exact)
            nc.gpsimd.iota(rowno[:, :], [[0, 1]], base=0, channel_multiplier=1, **exact)
            nc.gpsimd.iota(tileno[:, :], [[LOB // 2, NT]], base=LOB // 2, channel_multiplier=0, **exact)
            nc.gpsimd.iota(slotno[:, :], [[P, NT]], base=E, channel_multiplier=1, **exact)
            nc.gpsimd.iota(relno[:, :], [[0, 1]], base=0, channel_multiplier=1, **exact)
            nc.gpsimd.iota(dstb[:, :, :], [[0, 2], [1, GE + 1]], base=0, channel_multiplier=0)
            nc.gpsimd.memset(epst[:, :], EPS)
            nc.gpsimd.affine_select(out=anti_t[:, :], in_=anti_t[:, :], compare_op=ALU.not_equal, fill=1.0,
                                    base=-(NT - 1), pattern=[[1, NT]], channel_multiplier=1)
            nc.gpsimd.affine_select(out=anti[:, :], in_=anti[:, :], compare_op=ALU.not_equal, fill=1.0,
                                    base=-(P - 1), pattern=[[1, 128]], channel_multiplier=1).then_inc(pool_const, 1)
            for m in range(3):
                if m:
                    pool.wait_ge(pool_const, m + 1)
                nc.gpsimd.affine_select(out=sel[:, :, :], in_=sel[:, :, :], compare_op=ALU.not_equal, fill=1.0,
                                        base=-R1 * m, pattern=[[-1, R1], [0, 128]], channel_multiplier=1
                                        ).then_inc(pool_const, 1)

            pool.wait_ge(pool_const, 4)
            nc.gpsimd.affine_select(out=take[:, 2:2 + BLK], in_=take[:, 2:2 + BLK], compare_op=ALU.not_equal,
                                    fill=1.0, base=-64, pattern=[[-1, BLK]], channel_multiplier=1
                                    ).then_inc(pool_const, 1)

            def counter(name):
                reg = pool.alloc_register(name)
                pool.reg_mov(reg, 0)
                return reg

            def next_of(reg, by=1):
                pool.reg_add(reg, reg, by)
                return pool.snap(reg)

            stored_reg, landed_reg = [counter("stored0"), counter("stored1")], [counter("landed0"), counter("landed1")]
            added_reg = counter("added")

            def copy_x(x_, steps):
                item = steps[x_[2]][THIRD["W"]]
                if item is None:
                    return
                _, h, par = item
                again = type(h) is not int or h > 0
                stored = next_of(stored_reg[par], 16) if again else None
                landed = next_of(landed_reg[par], 16)
                pool.wait_ge(idx_split, 1)
                if again:
                    pool.wait_ge(d_st[par], stored)
                pool.wait_ge(d_x[par], landed)
                nc.gpsimd.tensor_copy(outr[:, par, :, :], xin[:, par, :, :]).then_inc(d_copied, 1)

            meta_reg = pool.alloc_register("meta_reg")
            pool.reg_mov(meta_reg, 0)

            def parts_of(i):
                copies = counted(pool, meta_reg)
                nc.gpsimd.tensor_copy(metag[:, :], column(meta, i)[:, 0:5 * TG]).then_inc(metag_now, 1)
                return copies

            def now(i, q, ap, c0, n):
                copies = counted(pool, pool_reg)
                nc.gpsimd.tensor_copy(nowidx[:, q, c0:c0 + n], column(ap, i)).then_inc(now_ready, 1)
                return copies

            def gather_x(i, k, q, j0):
                for j in range(j0, j0 + TG):
                    pool.indirect_dma_start(
                        out=gat[:, q, j, :], out_offset=None, in_=x,
                        in_offset=bass.IndirectOffsetOnAxis(ap=nowidx[:, q, j:j + 1], axis=0),
                    ).then_inc((g_s if j < TG else g_d)[q], 16)

            def gather_sources(i, k, q):
                reuse(pool, g_d[q], 64 * k)
                pool.wait_ge(idx_ready, 1)
                copies = now(i, q, gidx, 0, 2 * TG)
                pool.wait_ge(idx_split, 1)
                reuse(pool, s_norm[q], k)
                pool.wait_ge(now_ready, copies)
                gather_x(i, k, q, 0)

            def gather_dests(i, k, q):
                pool.wait_ge(idx_split, 1)
                reuse(pool, t_x1[q], k)
                gather_x(i, k, q, TG)

            gather_sources(0, 0, 0)
            gather_dests(0, 0, 0)
            copy_x(("W", 0, 0), [(None, (0, 0, 0), None)])
            gather_sources(1, 0, 1)
            gather_dests(1, 0, 1)

            def pass_p(i, k, q):
                for x_ in ORDER_P:
                    kind, j, _ = x_
                    if kind == "W":
                        copy_x(x_, steps_p(i, k, q))
                    elif kind == "T" and j < TG:
                        again = type(i) is not int or i > 0
                        if j == 0:
                            pool.wait_ge(meta_ready, 1)
                            reuse(pool, tab_high, i * TG)
                            there = parts_of(i)
                        free = next_of(added_reg) if again else None
                        pool.wait_ge(meta_ready, 1)
                        if again:
                            pool.wait_ge(tab_added, free)
                        pool.wait_ge(metag_now, there)
                        nc.gpsimd.tensor_scalar(hot_hi[:, j, :], iota_lo[:, 0:2 * HIC],
                                                metag[:, 2 * TG + j:2 * TG + j + 1], None,
                                                ALU.is_equal).then_inc(tab_high, 1)

            each_group(pool, pass_p)

            def pass_a(i, k, q):
                for x_ in ORDER_A:
                    kind, j, _ = x_
                    if kind == "W":
                        copy_x(x_, steps_a(i, k, q))
                    elif kind == "I" and ahead2(i, k, q):
                        (gather_dests if j else gather_sources)(*ahead2(i, k, q))
                    elif (kind, j) == ("L", 0):
                        pool.wait_ge(tab_ready, 1)
                        reuse(pool, looked_used, i)
                        there = parts_of(i)
                        pool.wait_ge(tab_ready, 1)
                        pool.wait_ge(metag_now, there)
                        for t_ in range(TG):
                            nc.gpsimd.tensor_scalar(hot_lo[:, 0, t_, :], iota_lo[:, :],
                                                    metag[:, TG + t_:TG + t_ + 1], None, ALU.is_equal)
                            t = nc.gpsimd.tensor_scalar(hot_hi[:, t_, :], iota_lo[:, 0:2 * HIC],
                                                        metag[:, t_:t_ + 1], None, ALU.is_equal)
                        t.then_inc(hot_ready, 1)

            each_group(pool, pass_a, 3)

            def gather_m(tab, i, k, q, l):
                reuse(pool, m_gT[q], k + (uses(q) if l else 0))
                pool.wait_ge(slots_ready, 1)
                copies = now(i, q, sidx, 0, TG)
                pool.wait_ge(idx_split, 1)
                pool.wait_ge(now_ready, copies)
                for j in range(TG):
                    pool.indirect_dma_start(
                        out=gat[:, q, j, :], out_offset=None, in_=tab,
                        in_offset=bass.IndirectOffsetOnAxis(ap=nowidx[:, q, j:j + 1], axis=0),
                    ).then_inc(g_s[q], 16)

            pool.wait_ge(st_ns, 16 * NG)
            pool.wait_ge(st_nt, 16 * NG)
            pool.wait_ge(t_x1[0], uses(0))
            pool.wait_ge(t_x1[1], uses(1))
            gather_m(tab1, 0, 0, 0, 0)
            gather_m(tab1, 1, 0, 1, 0)

            def pass_b(i, k, q):
                for x_ in ORDER_B:
                    if x_[0] == "W":
                        copy_x(x_, steps_b(i, k, q))
                    elif x_[0] == "I" and ahead2(i, k, q):
                        gather_m(tab1, *ahead2(i, k, q), 0)

            each_group(pool, pass_b, 3)
            pool.wait_ge(st_zs, 16 * NG)
            pool.wait_ge(st_zn, 16 * NG)

            def scatter(i, q):
                reuse(pool, st_out, 16 * TG * i)
                done = counted(pool, out_reg)
                pool.wait_ge(slots_ready, 1)
                nc.gpsimd.tensor_copy(nowout[:, :], column(tidx, i)).then_inc(out_now, 1)
                pool.wait_ge(slots_ready, 1)
                pool.wait_ge(out_now, done)
                pool.wait_ge(m_out, done)
                for j in range(TG):
                    pool.indirect_dma_start(
                        out=out, out_offset=bass.IndirectOffsetOnAxis(ap=nowout[:, j:j + 1], axis=0),
                        in_=x1b[:, q, j, :], in_offset=None, bounds_check=N - 1, oob_is_err=False,
                    ).then_inc(st_out, 16)

            gather_m(tab2, 0, 0, 0, 1)
            gather_m(tab2, 1, 0, 1, 1)
            for par in range(2):
                pool.wait_ge(d_st[par], 16 * (NI // 2))

            def pass_c(i, k, q):
                if type(i) is not int or i < NG - 2:
                    gather_m(tab2, i + 2, k + 1, q, 1)
                scatter(i, q)

            each_group(pool, pass_c, 3)
            pool.wait_ge(st_out, 16 * TG * NG)

        @block.scalar
        def _(act):
            VAR, SHIFT, SUM, ROOT, INV = range(1, 6)

            def root_of(mv, col, scale, ready, n, done):
                act.wait_ge(ready, n)
                nc.scalar.activation(mv[:, :, ROOT], mv[:, :, col], ACT.Sqrt, bias=epst[0:P, :],
                                     scale=scale).then_inc(done, 1)

            def squares(b, sq, mv, ready, n, summed, done):
                act.wait_ge(ready, n)
                for j in range(TG):
                    t = nc.scalar.activation(sq[:, j, :], b[0:P, j * D:(j + 1) * D], ACT.Square,
                                             accum_out=mv[:, j, SUM:SUM + 1])
                t.then_inc(summed, 1)
                root_of(mv, SUM, 1.0 / D, summed, n, done)

            def normalize(dst, rows, mv, ready, n, done):
                act.wait_ge(ready, 2 * n)
                for j in range(TG):
                    t = nc.scalar.activation(dst[:, j, :], rows[:, j, :], ACT.Identity,
                                             bias=mv[:, j, SHIFT:SHIFT + 1], scale=mv[:, j, INV:INV + 1])
                t.then_inc(done, 1)

            def bring(dst, src_, ready, n, done, func):
                act.wait_ge(ready, n)
                nc.scalar.activation(dst, src_, func).then_inc(done, 1)

            def affine(dst, src_, l, ready, n, done):
                act.wait_ge(ready, n)
                nc.scalar.activation(dst, src_, ACT.Identity, bias=ln[:, 2 * l + 1:2 * l + 2],
                                     scale=ln[:, 2 * l:2 * l + 1]).then_inc(done, 1)

            def dense(x_, steps):
                kind, j, sub = x_
                item = steps[sub][THIRD[kind]]
                if item is None:
                    return
                n, h, par = item
                n = n + 1
                if (kind, j) == ("X", 1):
                    root_of(mv_d, VAR, 1.0, d_var, n, d_sd)
                elif (kind, j) == ("X", 3):
                    normalize(nd, xin[:, par, :, :], mv_d, d_rs, n, d_norm)
                elif (kind, j) == ("X", 5):
                    bring(fd[:, :], D1[:, 0:GE], d_hT, n, d_h, ACT.Relu)
                elif (kind, j) == ("Y", 0):
                    squares(D1, sq_d, mv_d1, d_y, n, d_sq, d_sd1)
                elif (kind, j) == ("Y", 3):
                    affine(fd1[:, :], D2[:, 0:GE], 0, d_ynT, n, d_t)
                elif (kind, j) == ("Z", 0):
                    squares(D2, sq_d2, mv_d2, d_y2, n, d_sq2, d_sd2)
                elif (kind, j) == ("Z", 3):
                    affine(fd2[:, :], D3[:, 0:GE], 1, d_yn2T, n, d_t2)

            act.wait_ge(pool_const, 5)
            for n_, x_ in enumerate(START):
                if n_ == BARE:
                    act.wait_ge(ld_w, 16 * 19)
                dense(x_, [(None, first_items(x_), first_items(x_))] * 2)

            def pass_p(i, k, q):
                for x_ in ORDER_P:
                    if x_[0] in "XYZW":
                        dense(x_, steps_p(i, k, q))

            each_group(act, pass_p)

            def edges(j, group):
                if group is None:
                    return
                i, k, q = group
                n = i + 1
                if j == 1:
                    root_of(mv_s, VAR, 1.0, s_var, n, s_sd)
                elif j == 3:
                    reuse(act, st_ns, 16 * i)
                    normalize(ne, gat[:, q, :, :], mv_s, s_rs, n, s_norm[q])
                elif j == 5:
                    bring(fe[:, 0, :], E1[:, 0:GE], s_hT, n, s_h, ACT.Relu)

            def pass_a(i, k, q):
                n = i + 1
                for x_ in ORDER_A:
                    kind, j, _ = x_
                    if kind in "XYZW":
                        dense(x_, steps_a(i, k, q))
                    elif kind == "E":
                        edges(j, ahead(i, k, q))
                    elif (kind, j) == ("G", 0):
                        squares(E1, sq_e, mv_y, s_y, n, s_sq, s_sd1)
                    elif (kind, j) == ("G", 3):
                        root_of(mv_t, VAR, 1.0, t_var, n, t_sd)
                    elif (kind, j) == ("G", 5):
                        reuse(act, st_nt, 16 * i)
                        normalize(ne2, x1e, mv_t, t_rs, n, t_norm)
                    elif (kind, j) == ("G", 7):
                        reuse(act, st_h, 16 * i)
                        bring(fo[:, :], E3[:, 0:GE], t_hT, n, t_h, ACT.Relu)
                    elif (kind, j) == ("L", 2):
                        bring(hot_hit[:, :, 0:P],
                              hot_bank[0:HIC, :].bitcast(BF16).rearrange("p (c e) -> p c e", e=128)[:, :, 0:P],
                              hot_turned, n, hot_saved, ACT.Copy)
                    elif (kind, j) == ("L", 7):
                        bring(grp(coeft, i, GE).rearrange("p (t e) -> p t e", e=P),
                              hot_bank[0:48, :].bitcast(BF16).rearrange("p (t e) -> p t e", e=128)[:, 0:TG, 0:P],
                              coef_turned, n, coef_ready, ACT.Copy)

            for j in range(9):
                edges(j, (0, 0, 0))
            each_group(act, pass_a)
            act.wait_ge(st_h, 16 * NG)

            def messages(x_, group, l):
                if group is None:
                    return
                i, k, q = group
                if x_[:2] == ("N", 1):
                    n = k + 1 + l * uses(q)
                    if l == 0:
                        reuse(act, m_mm, B1 * (i - 1))
                        bring(fe[:, q, :], E1[:, 0:GE], m_gT[q], n, m_g, ACT.Relu)
                    else:
                        act.wait_ge(m_g, i + NG)
                        affine(te[:, :], turn_bank[l][:, 0:GE], 0, m_gT[q], n, m_t)

            def edge_rows(x_, i, l):
                j, n = x_[1], i + 1 + l * NG
                if j == 3:
                    squares(E2, sq_e, mv_y, m_y, n, m_sq, m_sd)
                elif j == 6:
                    affine(te2[:, :], E2[:, 0:GE], l, m_ynT, n, m_tt)

            def two_halves(order, l):
                messages(("N", 1, 0), (0, 0, 0), l)
                if l:
                    messages(("N", 1, 0), (1, 0, 1), l)

                def one(i, k, q):
                    for x_ in order:
                        if x_[0] in "XYZW":
                            dense(x_, steps_b(i, k, q))
                        elif x_[0] in "MN":
                            messages(x_, message_group(x_[0], i, k, q, l), l)
                        elif x_[0] == "U":
                            edge_rows(x_, i, l)
                each_group(act, one, 3)

            two_halves(ORDER_B, 0)
            two_halves(ORDER_C, 1)

        @block.tensor
        def _(pe):
            pe_reg = pe.alloc_register("pe_reg")
            pe.reg_mov(pe_reg, 0)
            pe.wait_ge(pool_const, 5)
            pe.wait_ge(idx_split, 1)
            for m in range(7):
                t = nc.tensor.transpose((E1, E2)[m // 4][0:P, (m % 4) * 128:(m % 4) * 128 + NT], turn[:, m, :],
                                        ident[0:NT, 0:NT])
            t.then_inc(idx_turned, 1)

            def turn_rows(b, rows):
                for j in range(TG):
                    t = nc.tensor.transpose(b[:, j * P:(j + 1) * P], rows[:, j, :], ident[0:P, 0:P])
                return t

            def turn_back(b, cols):
                for j in range(TG):
                    t = nc.tensor.transpose(b[0:P, j * D:(j + 1) * D], cols[:, j * P:(j + 1) * P], ident[:, :])
                return t

            def rows_out(b, cols, l, more=None):
                nc.tensor.matmul(b[0:P, :], onesb[0:96, 0:P], bias[:, l, :, :].rearrange("p t f -> p (t f)"),
                                 start=True, stop=False)
                for j in range(TG):
                    e = slice(j * P, (j + 1) * P)
                    o = b[0:P, j * D:(j + 1) * D]
                    last = j == TG - 1
                    t = nc.tensor.matmul(o, cols[:, e], wt[:, l, 0, :], start=False, stop=last and more is None)
                    if more is not None:
                        t = nc.tensor.matmul(o, more[:, e], ident[:, :], start=False, stop=last)
                return t

            def dense(x_, steps):
                kind, j, sub = x_
                item = steps[sub][THIRD[kind]]
                if item is None:
                    return
                n = item[0] + 1
                if (kind, j) == ("X", 4):
                    pe.wait_ge(d_norm, n)
                    reuse(pe, d_yn, n - 1)
                    turn_rows(D1, nd).then_inc(d_hT, 1)
                elif (kind, j) == ("X", 6):
                    pe.wait_ge(d_h, n)
                    rows_out(D1, fd, 0).then_inc(d_y, 1)
                elif (kind, j) == ("Y", 2):
                    pe.wait_ge(d_yn, n)
                    reuse(pe, d_yn2, n - 1)
                    turn_rows(D2, nd1).then_inc(d_ynT, 1)
                elif (kind, j) == ("Y", 5):
                    pe.wait_ge(d_z, n)
                    rows_out(D2, zd, 1).then_inc(d_y2, 1)
                elif (kind, j) == ("Z", 2):
                    pe.wait_ge(d_yn2, n)
                    reuse(pe, d_out, n - 1)
                    turn_rows(D3, nd2).then_inc(d_yn2T, 1)
                elif (kind, j) == ("Z", 5):
                    pe.wait_ge(d_z2, n)
                    turn_back(D3, zd2).then_inc(d_back, 1)

            for n_, x_ in enumerate(START):
                if n_ == BARE:
                    pe.wait_ge(w_ready, 1)
                dense(x_, [(None, first_items(x_), first_items(x_))] * 2)

            def table_zero(**flags):
                for v in range(2):
                    t = nc.tensor.matmul(bank[6 + v][0:HIC, :], zerob[0:48, 0:HIC],
                                         sel[:, 0:4, :].rearrange("p c e -> p (c e)"), **flags)
                return t

            table_zero(start=True, stop=False)

            def pass_p(i, k, q):
                for x_ in ORDER_P:
                    kind, j, _ = x_
                    if kind in "XYZW":
                        dense(x_, steps_p(i, k, q))
                    elif kind == "T" and j > 0:
                        pe.wait_ge(tab_hot, i * TG + j)
                        pe.wait_ge(tab_high, i * TG + j)
                        for v in range(2):
                            for c in range(2):
                                t = nc.tensor.matmul(table_bank(v, c), hot_hi[:, j - 1, c * HIC:(c + 1) * HIC],
                                                     hot_lo[:, v, j - 1, :], start=False, stop=False)
                        t.then_inc(tab_added, 1)
                    elif (kind, j) == ("C", 3):
                        pe.wait_ge(cnt_prods, i + 1)
                        reuse(pe, cnt_saved, i)
                        for t_ in range(TG):
                            t = nc.tensor.matmul(E1[0:P, t_ * 32:t_ * 32 + 2 + BLK + R1],
                                                 prodc[:, t_ * P:(t_ + 1) * P], take[:, :], start=True, stop=True)
                        t.then_inc(cnt_summed, 1)

            each_group(pe, pass_p)
            table_zero(start=False, stop=True).then_inc(tab_sum, 1)
            pe.wait_ge(cnt_saved, NG)
            nc.tensor.matmul(E3[0:NT, 0:P], cnt_b[:, :], anti[0:P, 0:P], start=True, stop=True).then_inc(cnt_flipped, 1)
            pe.wait_ge(flip_saved, 1)
            nc.tensor.matmul(E3[0:P, 128:128 + NT], flip[:, :], anti_t[:, :], start=True, stop=True).then_inc(cnt_flipped, 1)
            pe.wait_ge(tab_ready, 1)

            def edges(j, group):
                if group is None:
                    return
                i, k, q = group
                n = i + 1
                if j == 4:
                    pe.wait_ge(s_norm[q], k + 1)
                    reuse(pe, s_yn, i)
                    turn_rows(E1, ne).then_inc(s_hT, 1)
                elif j == 6:
                    pe.wait_ge(s_h, n)
                    reuse(pe, t_mean, i)
                    nc.tensor.matmul(E2[:, 0:GE], w0t[:, :], fe[:, 0, :], start=True, stop=True).then_inc(s_m0, 1)
                    rows_out(E1, fe[:, 0, :], 0).then_inc(s_y, 1)
                elif j == 8:
                    pe.wait_ge(agg_ready, n)
                    turn_back(E2, agg[:, 0, :]).then_inc(agg_T, 1)

            for j in range(9):
                edges(j, (0, 0, 0))

            def pass_a(i, k, q):
                n = i + 1
                for x_ in ORDER_A:
                    kind, j, _ = x_
                    if kind in "XYZW":
                        dense(x_, steps_a(i, k, q))
                    elif kind == "E":
                        edges(j, ahead(i, k, q))
                    elif (kind, j) == ("G", 6):
                        pe.wait_ge(t_norm, n)
                        reuse(pe, t_h, i)
                        turn_rows(E3, ne2).then_inc(t_hT, 1)
                    elif (kind, j) == ("L", 1):
                        pe.wait_ge(hot_ready, n)
                        reuse(pe, coef_ready, i)
                        turned = hot_bank[0:HIC, :].bitcast(BF16).rearrange("p (c e) -> p c e", e=128)
                        for t_ in range(TG):
                            for c in range(2):
                                t = nc.tensor.transpose(turned[:, 2 * t_ + c, 0:P],
                                                        hot_hi[:, t_, c * HIC:(c + 1) * HIC], identb[0:P, 0:P])
                        t.then_inc(hot_turned, 1)
                    elif (kind, j) == ("L", 3):
                        pe.wait_ge(hot_saved, n)
                        reuse(pe, looked_used, i)
                        for t_ in range(TG):
                            b = look_bank[t_ // 2][0:P, (t_ % 2) * LOB:(t_ % 2 + 1) * LOB]
                            for c in range(2):
                                for v in range(2):
                                    t = nc.tensor.matmul(b, hot_hit[:, 2 * t_ + c, 0:P], node_tab[:, v, c, :],
                                                         start=(c == 0 and v == 0), stop=(c == 1 and v == 1))
                        t.then_inc(looked, 1)
                    elif (kind, j) == ("L", 6):
                        copied = counted(pe, pe_reg)
                        pe.wait_ge(dve_const, 1)
                        pe.wait_ge(coef_now, copied)
                        turned = hot_bank[0:48, :].bitcast(BF16)
                        for t_ in range(TG):
                            t = nc.tensor.transpose(turned[:, t_ * 128:t_ * 128 + P], coef3g[:, t_, :], identb[0:P, 0:P])
                        t.then_inc(coef_turned, 1)

            each_group(pe, pass_a)

            def messages(x_, group, l):
                if group is None:
                    return
                i, k, q = group
                j, m = x_[1], i + l * NG
                if x_[0] == "N":
                    if j == 0:
                        pe.wait_ge(g_s[q], (k + 1 + (1 + l) * uses(q)) * 64)
                        if l:
                            reuse(pe, m_t, i)
                        else:
                            reuse(pe, m_agg, m)
                        turn_rows(turn_bank[l], gat[:, q, :, :]).then_inc(m_gT[q], 1)
                elif j < B1 + NQ:
                    b = j - NQ
                    if b == 0:
                        pe.wait_ge(dve_const, 1)
                        reuse(pe, m_agg, m)
                    if b >= 0:
                        pe.wait_ge(m_sc, m * B1 + b + 1)
                        nc.tensor.matmul(E1[:, 0:GE], wt[:, l, 1 + b, :], scaled[:, b % NS, :],
                                         start=(b == 0), stop=(b == B1 - 1)).then_inc(m_mm, 1)
                    if b + NQ < B1:
                        nc.tensor.matmul(coef_bank[(b + NQ) % NQ][:, 0:GE], sel[:, l * B1 + b + NQ, :],
                                         grp(coeft, i, GE), start=True, stop=True).then_inc(m_bc, 1)

            def edge_rows(x_, i, k, q, l):
                j, n = x_[1], i + 1 + l * NG
                if j == 0:
                    pe.wait_ge(ld_e[q], (k + 1 + (2 + l) * uses(q)) * 16)
                    reuse(pe, m_out if l else m_tt, i)
                    nc.tensor.matmul(E2[:, 0:GE], wt[:, l, 0, :], own[:, q, :], start=True, stop=True
                                     ).then_inc(m_own, 1)
                elif j == 2:
                    pe.wait_ge(m_sum, n)
                    turn_back(E2, total).then_inc(m_y, 1)
                elif j == 5:
                    pe.wait_ge(m_yn, n)
                    turn_rows(E2, ye).then_inc(m_ynT, 1)
                elif j == 8 and l:
                    pe.wait_ge(m_z, n)
                    turn_back(E2, fo).then_inc(m_back, 1)

            def two_halves(order, l):
                for x_ in stream("N", 3) + stream("M", B1 + NQ + 1):
                    messages(x_, (0, 0, 0), l)
                if l:
                    for x_ in stream("N", 3):
                        messages(x_, (1, 0, 1), l)

                def one(i, k, q):
                    for x_ in order:
                        if x_[0] in "XYZW":
                            dense(x_, steps_b(i, k, q))
                        elif x_[0] in "MN":
                            messages(x_, message_group(x_[0], i, k, q, l), l)
                        elif x_[0] == "U":
                            edge_rows(x_, i, k, q, l)
                each_group(pe, one, 3)

            pe.wait_ge(coef_ready, NG)
            pe.wait_ge(looked_used, NG)
            pe.wait_ge(t_h, NG)
            two_halves(ORDER_B, 0)
            pe.wait_ge(m_tt, NG)
            two_halves(ORDER_C, 1)

        @block.vector
        def _(dve):
            v = nc.vector
            steps = [0]

            def own_step(ins):
                steps[0] += 1
                ins.then_inc(prep, 1)
                dve.wait_ge(prep, steps[0])

            for t in (ident, identb, anti):
                v.memset(t[:, :], 0.0)
            v.memset(sel[:, :, :], 0.0)
            v.memset(anti_t[:, :], 0.0)
            v.memset(take[:, :], 0.0).then_inc(dve_const, 1)
            v.memset(zerob[:, :], 0.0)
            v.memset(ones[:, :], 1.0)
            v.memset(onesb[:, :], 1.0)
            v.memset(bias[:, :, :, :], 0.0)
            v.memset(carryc[:, :], 0.0)
            v.memset(runs[0:64, :], 0.0)
            v.memset(runs[64:128, :], 1.0)
            for r in range(4):
                v.memset(blockno[r * HEAD:(r + 1) * HEAD, :], float(r))
            v.memset(carry[:, :], 0.0).then_inc(dve_const, 1)
            dve.wait_ge(dve_const, 2)
            v.memset(take[0:32, 0:1], 1.0)
            v.memset(take[32:64, 1:2], 1.0).then_inc(dve_const, 1)

            dve.wait_ge(ld_idx, 48)
            v.tensor_copy(rawf[:, :, :], raw[:, :, :])
            for m in range(2):
                v.tensor_single_scalar(part[:, 2 * m, :], raw[:, m, :], 8, ALU.logical_shift_right)
                own_step(v.tensor_single_scalar(part[:, 2 * m + 1, :], raw[:, m, :], LOB - 1, ALU.bitwise_and))
            v.tensor_copy(turn[:, 0:2, :], rawf[:, 0:2, :])
            own_step(v.tensor_tensor(lastf[:, :], rawf[:, DST_, :], rawf[:, OUT_, :], ALU.is_equal))
            v.scalar_tensor_tensor(turn[:, 2, :], lastf[:, :], float(1 << 20), rawf[:, DST_, :], ALU.mult, ALU.add)
            v.tensor_copy(turn[:, 3:7, :], part[:, :, :])
            own_step(v.tensor_copy(rawf[:, 2, :], part[:, 2, :]))
            v.scalar_tensor_tensor(turn[:, 5, :], lastf[:, :], 1024.0, rawf[:, 2, :],
                                   ALU.mult, ALU.add).then_inc(idx_split, 1)
            dve.wait_ge(idx_turned, 1)
            tb = lambda m: (E1, E2)[m // 4][0:P, (m % 4) * 128:(m % 4) * 128 + NT].rearrange("p (g t) -> p g t", t=TG)
            v.tensor_copy(gidx[:, :, 0:TG], tb(0))
            v.tensor_copy(gidx[:, :, TG:2 * TG], tb(1)).then_inc(idx_ready, 1)
            v.tensor_copy(tidx[:, :, :], tb(2))
            for m in range(4):
                v.tensor_copy(meta[:, :, m * TG:(m + 1) * TG], tb(3 + m))
            for r in range(1, 4):
                v.tensor_scalar(relno[32 * r:32 * r + 32, :], relno[32 * r:32 * r + 32, :], -32.0 * r, None, ALU.add)
            v.tensor_copy(meta[:, :, 4 * TG:5 * TG], tileno[:, :].rearrange("p (g t) -> p g t", t=TG)
                          ).then_inc(meta_ready, 1)

            MEAN, VAR, SHIFT, SUM, ROOT, INV = range(6)

            stats_reg = dve.alloc_register("stats_reg")
            dve.reg_mov(stats_reg, 0)

            def moments(rows, st, mv, var):
                taken = counted(dve, stats_reg)
                for j in range(TG):
                    t = v.bn_stats(st[:, j, :], rows[:, j, :])
                t.then_inc(stats, 1)
                dve.wait_ge(dve_const, 1)
                dve.wait_ge(stats, taken)
                for j in range(TG):
                    t = v.bn_aggr(mv[:, j, MEAN:VAR + 1], st[:, j, :])
                t.then_inc(var, 1)

            def inverse(mv, ready, n, done, steps_=1):
                dve.wait_ge(ready, n)
                v.reciprocal(mv[:, :, INV], mv[:, :, ROOT]).then_inc(done, 1)
                dve.wait_ge(done, n if steps_ == 1 else n * steps_ - 1)

            def scale_and_shift(mv, ready, n, done):
                inverse(mv, ready, n, done, 2)
                v.scalar_tensor_tensor(mv[:, :, SHIFT], mv[:, :, MEAN], -1.0, mv[:, :, INV], ALU.mult, ALU.mult
                                       ).then_inc(done, 1)

            def scale_rows(dst, b, mv, done):
                v.tensor_tensor(dst[:, :, :], rows4(b), mv[:, :, INV:INV + 1].to_broadcast([P, TG, D]),
                                ALU.mult).then_inc(done, 1)

            def leaky(dst, t_, ready, n, done):
                dve.wait_ge(ready, n)
                v.scalar_tensor_tensor(dst, t_, SLOPE, t_, ALU.mult, ALU.max).then_inc(done, 1)

            def dense(x_, steps_):
                kind, j, sub = x_
                item = steps_[sub][THIRD[kind]]
                if item is None:
                    return
                n, h, par = item
                n = n + 1
                if (kind, j) == ("X", 0):
                    dve.wait_ge(d_x[par], (h + 1) * 16)
                    moments(xin[:, par, :, :], st_d, mv_d, d_var)
                elif (kind, j) == ("X", 2):
                    scale_and_shift(mv_d, d_sd, n, d_rs)
                elif (kind, j) == ("Y", 1):
                    inverse(mv_d1, d_sd1, n, d_rs1)
                    scale_rows(nd1, D1, mv_d1, d_yn)
                elif (kind, j) == ("Y", 4):
                    leaky(zd[:, :], fd1[:, :], d_t, n, d_z)
                elif (kind, j) == ("Z", 1):
                    inverse(mv_d2, d_sd2, n, d_rs2)
                    scale_rows(nd2, D2, mv_d2, d_yn2)
                elif (kind, j) == ("Z", 4):
                    leaky(zd2[:, :], fd2[:, :], d_t2, n, d_z2)
                elif (kind, j) == ("Z", 6):
                    dve.wait_ge(d_back, n)
                    dve.wait_ge(d_copied, n)
                    v.tensor_tensor(outr[:, par, :, :], outr[:, par, :, :], rows4(D3), ALU.add).then_inc(d_out, 1)

            def start(steps_):
                for x_ in steps_:
                    dense(x_, [(None, first_items(x_), first_items(x_))] * 2)

            start(START[:BARE])

            dve.wait_ge(ld_w, 16 * 19)
            wv = wt[:, :, :, :].rearrange("p l b f -> p (l b) f")
            own_step(v.tensor_reduce(wsum[:, :], wv, AX.X, ALU.add))
            own_step(v.tensor_scalar(wsum[:, :], wsum[:, :], 1.0 / D, None, ALU.mult))
            own_step(v.tensor_tensor(wv, wv, wsum[:, :].unsqueeze(2).to_broadcast([128, 18, 128]), ALU.subtract))
            own_step(v.tensor_reduce(bsum[:, :], brow[:, :, :], AX.X, ALU.add))
            own_step(v.tensor_scalar(bsum[:, :], bsum[:, :], 1.0 / D, None, ALU.mult))
            own_step(v.tensor_tensor(bcol[:, :], bcol[:, :], bsum[:, :], ALU.subtract))
            own_step(v.tensor_tensor(brow[:, :, :], brow[:, :, :], bsum[:, :].unsqueeze(2).to_broadcast([128, 2, 128]),
                                     ALU.subtract))
            for m in range(3):
                own_step(v.tensor_copy(bpart[:, :, :], brow[0:96, :, :]))
                for l in range(2):
                    v.tensor_copy(bias[32 * m:32 * m + 1, l, :, :],
                                  bpart[32 * m:32 * m + 1, l, :].unsqueeze(1).to_broadcast([1, TG, 128]))
                own_step(v.tensor_tensor(brow[0:96, :, :], brow[0:96, :, :], bpart[:, :, :], ALU.subtract))
            v.tensor_copy(bsum[:, :], bsum[:, :]).then_inc(w_ready, 1)

            start(START[BARE:])

            def one_hots(i, kinds):
                v.tensor_copy(metat[:, 0:kinds * TG], column(meta, i)[:, 0:kinds * TG]).then_inc(meta_now, 1)

            def pass_p(i, k, q):
                n = i + 1
                for x_ in ORDER_P:
                    kind, j, _ = x_
                    if kind in "XYZW":
                        dense(x_, steps_p(i, k, q))
                    elif kind == "T" and j < TG:
                        if j == 0:
                            reuse(dve, tab_hot, i * TG)
                            one_hots(i, 5)
                            dve.wait_ge(meta_now, n)
                        reuse(dve, tab_added, i * TG + (j + 1 - TG))
                        c = lambda m: metat[:, m * TG + j:m * TG + j + 1]
                        v.tensor_scalar(hot_lo[:, 0, j, :], iota_lo[:, :], c(3), c(4), ALU.is_equal, ALU.mult)
                        v.tensor_scalar(hot_lo[:, 1, j, :], iota_lo[:, :], c(3), rowno[:, :],
                                        ALU.is_equal, ALU.mult).then_inc(tab_hot, 1)
                    elif (kind, j) == ("C", 0):
                        dve.wait_ge(ld_cnt[q], (k + 1) * 112)
                        reuse(dve, cnt_summed, i)
                        v.tensor_tensor(contc[:, :], dstb[:, q, 1:GE + 1], dstb[:, q, 0:GE], ALU.is_equal)
                        v.tensor_scalar(hotc[:, :], et5b[:, q, :], relno[:, :], None, ALU.is_equal).then_inc(cnt_hot, 1)
                    elif (kind, j) == ("C", 1):
                        dve.wait_ge(cnt_hot, n)
                        reuse(dve, cnt_carry, i)
                        v.tensor_tensor_scan(runc[:, :], contc[:, :], hotc[:, :], carryc[:, :],
                                             ALU.mult, ALU.add).then_inc(cnt_run, 1)
                    elif (kind, j) == ("C", 2):
                        dve.wait_ge(cnt_run, n)
                        v.tensor_copy(carryc[:, :], runc[:, GE - 1:GE]).then_inc(cnt_carry, 1)
                        v.scalar_tensor_tensor(prodc[:, :], hotc[:, :], runs[:, :], runc[:, :], ALU.max, ALU.mult
                                               ).then_inc(cnt_prods, 1)
                    elif (kind, j) == ("C", 4):
                        dve.wait_ge(cnt_summed, n)
                        g = E1[0:P, 0:TG * 32].rearrange("p (t c) -> p t c", c=32)
                        now = bass.ds(i * TG, TG)
                        v.tensor_copy(cnt_f[:, now], g[:, :, 0])
                        v.tensor_copy(cnt_b[:, now], g[:, :, 1])
                        v.tensor_copy(rdeg[:, now, :], g[:, :, 2:2 + BLK])
                        v.tensor_copy(coef[:, now, :], g[:, :, 2 + BLK:2 + BLK + R1]).then_inc(cnt_saved, 1)

            each_group(dve, pass_p)
            def edges(j, group):
                if group is None:
                    return
                i, k, q = group
                n = i + 1
                if j == 0:
                    dve.wait_ge(g_s[q], (k + 1) * 64)
                    moments(gat[:, q, :, :], st_e, mv_s, s_var)
                elif j == 1:
                    dve.wait_ge(ld_e[q], (k + 1) * 32)
                    v.tensor_scalar(mask[:, :], et5b[:, q, :], blockno[:, :], None, ALU.is_equal)
                    v.tensor_tensor(grp(cont, i, GE), dstb[:, q, 1:GE + 1], dstb[:, q, 0:GE], ALU.is_equal
                                    ).then_inc(cont_ready, 1)
                elif j == 2:
                    scale_and_shift(mv_s, s_sd, n, s_rs)
                elif j == 7:
                    dve.wait_ge(cont_ready, n)
                    dve.wait_ge(s_m0, n)
                    v.scalar_tensor_tensor(msg[:, :], E2[:, 0:GE], b0t[:, 0:1], mask[:, :], ALU.add, ALU.mult
                                           ).then_inc(msg_ready, 1)
                    dve.wait_ge(msg_ready, n)
                    reuse(dve, carried, i)
                    v.tensor_tensor_scan(agg[:, 0, :], grp(cont, i, GE), msg[:, :], carry[:, 2:3],
                                         ALU.mult, ALU.add).then_inc(agg_ready, 1)
                elif j == 8:
                    dve.wait_ge(agg_ready, n)
                    v.tensor_copy(carry[:, 2:3], agg[:, 0, GE - 1:GE]).then_inc(carried, 1)

            for j in range(3):
                edges(j, (0, 0, 0))

            dve.wait_ge(tab_sum, 1)
            for v_ in range(2):
                for c in range(2):
                    t = v.tensor_copy(node_tab[:, v_, c, :], table_bank(v_, c))
            t.then_inc(tab_ready, 1)
            dve.wait_ge(cnt_saved, NG)
            own_step(v.tensor_scalar(rdeg[:, :, :], rdeg[:, :, :], 1.0, None, ALU.max))
            own_step(v.reciprocal(rdeg[:, :, :], rdeg[:, :, :]))
            dve.wait_ge(cnt_flipped, 1)
            v.tensor_copy(flip[:, :], E3[0:NT, 0:P]).then_inc(flip_saved, 1)
            dve.wait_ge(cnt_flipped, 2)
            own_step(v.scalar_tensor_tensor(cnt_f[:, :], cnt_f[:, :], -1.0, E3[0:P, 128:128 + NT], ALU.add, ALU.add))
            own_step(v.reciprocal(cnt_b[:, :], cnt_f[:, :]))
            own_step(v.tensor_tensor(coef[:, :, :], coef[:, :, :],
                                     cnt_b[:, :].unsqueeze(2).to_broadcast([P, NT, R1]), ALU.mult))
            for m in range(3):
                own_step(v.tensor_copy(coef3[:, :, m * R1:(m + 1) * R1], coef[:, :, :]))
                if m < 2:
                    own_step(v.tensor_tensor(coef[:, :, :], coef[:, :, :], coef3[:, :, m * R1:(m + 1) * R1],
                                             ALU.subtract))

            for j in range(3, 9):
                edges(j, (0, 0, 0))

            def pass_a(i, k, q):
                n = i + 1
                for x_ in ORDER_A:
                    kind, j, _ = x_
                    if kind in "XYZW":
                        dense(x_, steps_a(i, k, q))
                    elif kind == "E":
                        edges(j, ahead(i, k, q))
                    elif (kind, j) == ("G", 0):
                        dve.wait_ge(agg_T, n)
                        inv = rdeg[:, bass.ds(i * TG, TG), :].rearrange("p t r -> p (t r)")
                        v.tensor_tensor(mean[:, :, :].rearrange("p t (r c) -> p (t r) c", c=HEAD),
                                        E2[0:P, :].rearrange("p (r c) -> p r c", c=HEAD),
                                        inv.unsqueeze(2).to_broadcast([P, TG * BLK, HEAD]), ALU.mult
                                        ).then_inc(t_mean, 1)
                    elif (kind, j) == ("G", 1):
                        dve.wait_ge(g_d[q], (k + 1) * 64)
                        dve.wait_ge(t_mean, n)
                        reuse(dve, st_x1, 16 * i)
                        v.tensor_tensor(x1e[:, :, :], gat[:, q, TG:2 * TG, :], mean[:, :, :], ALU.add
                                        ).then_inc(t_x1[q], 1)
                        inverse(mv_y, s_sd1, n, s_rs1)
                        reuse(dve, st_zs, 16 * i)
                        scale_rows(ye, E1, mv_y, s_yn)
                    elif (kind, j) == ("G", 2):
                        dve.wait_ge(t_x1[q], k + 1)
                        moments(x1e, st_t, mv_t, t_var)
                    elif (kind, j) == ("G", 4):
                        scale_and_shift(mv_t, t_sd, n, t_rs)
                    elif (kind, j) == ("L", 4):
                        dve.wait_ge(looked, n)
                        for t_ in range(TG):
                            t = v.tensor_tensor_reduce(
                                junk[:, t_, :], look_bank[t_ // 2][0:P, (t_ % 2) * LOB:(t_ % 2 + 1) * LOB],
                                hot_lo[:, 0, t_, :], 1.0, 0.0, ALU.mult, ALU.add, res[:, t_:t_ + 1])
                        t.then_inc(looked_used, 1)
                        dve.wait_ge(looked_used, n)
                        v.tensor_copy(found[:, bass.ds(i * TG, TG)], res[:, :]).then_inc(found_now, 1)
                    elif (kind, j) == ("L", 5):
                        reuse(dve, coef_turned, i)
                        v.tensor_copy(coef3g[:, :, :], coef3[:, bass.ds(i * TG, TG), :]).then_inc(coef_now, 1)

            each_group(dve, pass_a)
            dve.wait_ge(found_now, NG)
            own_step(v.tensor_copy(foundi[:, :], found[:, :]))
            own_step(v.tensor_single_scalar(foundi[:, :], foundi[:, :], 7, ALU.logical_shift_right))
            own_step(v.tensor_copy(hit[:, :], foundi[:, :]))
            own_step(v.scalar_tensor_tensor(slotf[:, :], hit[:, :], float(P - 128), found[:, :], ALU.mult, ALU.add))
            own_step(v.tensor_scalar(slotf[:, :], slotf[:, :], -float(P), None, ALU.add))
            own_step(v.tensor_tensor(slotf[:, :], slotf[:, :], slotno[:, :], ALU.subtract))
            own_step(v.tensor_scalar(hit[:, :], hit[:, :], 0.5, None, ALU.is_gt))
            own_step(v.tensor_tensor(slotf[:, :], slotf[:, :], hit[:, :], ALU.mult))
            own_step(v.tensor_tensor(slotf[:, :], slotf[:, :], slotno[:, :], ALU.add))
            v.tensor_copy(sidx[:, :, :], slotf[:, :].rearrange("p (g t) -> p g t", t=TG)).then_inc(slots_ready, 1)

            def messages(x_, group, l):
                if group is None:
                    return
                i, k, q = group
                j, m = x_[1], i + l * NG
                if x_[0] == "N":
                    if j == 2 and l:
                        reuse(dve, m_mm, B1 * (m - 1))
                        leaky(fe[:, q, :], te[:, :], m_t, i + 1, m_g)
                elif 1 <= j < 1 + B1:
                    b = j - 1
                    if b == 0:
                        dve.wait_ge(m_g, m + 1)
                    dve.wait_ge(m_bc, m * B1 + b + 1)
                    reuse(dve, m_mm, m * B1 + b + 1 - NS)
                    v.tensor_tensor(scaled[:, b % NS, :], fe[:, q, :], coef_bank[b % NQ][:, 0:GE], ALU.mult
                                    ).then_inc(m_sc, 1)
                elif j == B1 + NQ:
                    dve.wait_ge(m_mm, (m + 1) * B1)
                    reuse(dve, carried, m + NG)
                    v.tensor_tensor_scan(agg[:, q, :], grp(cont, i, GE), E1[:, 0:GE], carry[:, l:l + 1],
                                         ALU.mult, ALU.add).then_inc(m_agg, 1)
                    dve.wait_ge(m_agg, m + 1)
                    v.tensor_copy(carry[:, l:l + 1], agg[:, q, GE - 1:GE]).then_inc(carried, 1)

            def edge_rows(x_, i, k, q, l):
                j, n = x_[1], i + 1 + l * NG
                if j == 1:
                    dve.wait_ge(m_own, n)
                    v.scalar_tensor_tensor(total[:, :], E2[:, 0:GE], bcol[:, l:l + 1], agg[:, q, :],
                                           ALU.add, ALU.add).then_inc(m_sum, 1)
                elif j == 4:
                    inverse(mv_y, m_sd, n, m_rs)
                    if l == 0:
                        reuse(dve, st_zn, 16 * i)
                    scale_rows(ye, E2, mv_y, m_yn)
                elif j == 7:
                    if l == 0:
                        reuse(dve, st_z, 16 * i)
                    leaky(fo[:, :], te2[:, :], m_tt, n, m_z)
                elif j == 9 and l:
                    dve.wait_ge(m_back, i + 1)
                    dve.wait_ge(ld_x1[q], (k + 1) * 16)
                    v.tensor_tensor(x1b[:, q, :, :], x1b[:, q, :, :], rows4(E2), ALU.add).then_inc(m_out, 1)

            def two_halves(order, l):
                for x_ in stream("N", 3) + stream("M", B1 + NQ + 1):
                    messages(x_, (0, 0, 0), l)
                if l:
                    for x_ in stream("N", 3):
                        messages(x_, (1, 0, 1), l)

                def one(i, k, q):
                    for x_ in order:
                        if x_[0] in "XYZW":
                            dense(x_, steps_b(i, k, q))
                        elif x_[0] in "MN":
                            messages(x_, message_group(x_[0], i, k, q, l), l)
                        elif x_[0] == "U":
                            edge_rows(x_, i, k, q, l)
                each_group(dve, one, 3)

            dve.wait_ge(st_zs, 16 * NG)
            dve.wait_ge(st_h, 16 * NG)
            two_halves(ORDER_B, 0)
            dve.wait_ge(st_x1, 16 * NG)
            dve.wait_ge(st_zn, 16 * NG)
            dve.wait_ge(st_z, 16 * NG)
            two_halves(ORDER_C, 1)


_DRAM_INS = ["x", "src", "dst_ext", "dst_both", "et_both", "et5", "w0", "b0", "v1", "comp1", "root1", "bias1", "g1",
             "be1", "v2", "comp2", "root2", "bias2", "g2", "be2"]


def kernel(x, src, dst, edge_type_16, edge_type_5, L0_gnn_Ws, L0_gnn_bs, L1_gnn_weight1, L1_gnn_comp1,
           L1_gnn_root1, L1_gnn_bias1, L1_gnn_ln1_g, L1_gnn_ln1_b, L1_gnn_weight2, L1_gnn_comp2,
           L1_gnn_root2, L1_gnn_bias2, L1_gnn_ln2_g, L1_gnn_ln2_b):
    import numpy as np
    import concourse.bacc as bacc
    from concourse.bass_utils import run_bass_kernel_spmd

    dst, et16 = np.asarray(dst), np.asarray(edge_type_16)
    edge = np.full(1, -1, dst.dtype)
    arrays = {
        "x": x, "src": src,
        "dst_ext": np.concatenate([edge, dst, edge]),
        "dst_both": np.stack([np.concatenate([edge, dst]), np.concatenate([edge, dst[::-1]])]),
        "et_both": np.stack([et16, et16[::-1]]),
        "et5": edge_type_5, "w0": L0_gnn_Ws, "b0": L0_gnn_bs,
        "v1": L1_gnn_weight1, "comp1": L1_gnn_comp1, "root1": L1_gnn_root1, "bias1": L1_gnn_bias1,
        "g1": L1_gnn_ln1_g, "be1": L1_gnn_ln1_b,
        "v2": L1_gnn_weight2, "comp2": L1_gnn_comp2, "root2": L1_gnn_root2, "bias2": L1_gnn_bias2,
        "g2": L1_gnn_ln2_g, "be2": L1_gnn_ln2_b,
    }
    nc = bacc.Bacc("TRN2", target_bir_lowering=False, num_devices=1)
    feed, args = {}, []
    for name in _DRAM_INS:
        a = np.ascontiguousarray(arrays[name])
        feed[f"in_{name}"] = a
        args.append(nc.dram_tensor(f"in_{name}", a.shape, mybir.dt.from_np(a.dtype), kind="ExternalInput").ap())
    out = nc.dram_tensor("out", (N, D), F32, kind="ExternalOutput").ap()
    gnn_kernel(nc, *args, out)
    r = run_bass_kernel_spmd(nc, [feed], core_ids=[0])
    return r.results[0]["out"]
```
